# Optimizing a Trainium2 kernel written in Bass

```python
import numpy as np
import jax
import jax.numpy as jnp

def _softmax(x, axis=-1):
    return jax.nn.softmax(x, axis=axis)

def _gelu(x):
    return jax.nn.gelu(x, approximate=True)

def _silu(x):
    return jax.nn.silu(x)

def _sigmoid(x):
    return jax.nn.sigmoid(x)

def _layernorm(x, axis=-1, eps=1e-05):
    m = jnp.mean(x, axis=axis, keepdims=True)
    v = jnp.var(x, axis=axis, keepdims=True)
    return (x - m) / jnp.sqrt(v + eps)

def _scatter_add(tgt, idx, src, axis=0):
    return tgt.at[idx].add(src)

def _segment_sum(src, seg, n):
    return jax.ops.segment_sum(src, seg, n)
kernel_name = 'mk_xattn_seq_d2_seqx_r8_ee323d'

def setup_inputs(seed: int=0):
    np.random.seed(seed)
    _w = jnp.asarray

    def _rec_inputs():
        import jax
        import jax.numpy as jnp
        _rk = jax.random.key(seed)
        x = -0.0002928 + 1 * jax.random.normal(jax.random.fold_in(_rk, 1), (16, 56, 128), jnp.float32)
        _lenS = 56 - jax.random.randint(jax.random.fold_in(_rk, 7), (16,), 0, max(1, 56 // 4) + 1, jnp.int32)
        _lenS2 = 1500 - jax.random.randint(jax.random.fold_in(_rk, 8), (16,), 0, max(1, 1500 // 4) + 1, jnp.int32)
        _ctx_768P = jax.random.normal(jax.random.fold_in(_rk, 11), (16, 16, 96), jnp.float32)
        _ctx_768c = jax.random.dirichlet(jax.random.fold_in(_rk, 511), 0.3 * jnp.ones((16,), jnp.float32), (16, 1500))
        _ctx_768t = jnp.einsum('bsk,bkd->bsd', _ctx_768c, _ctx_768P)
        _ctx_768t = _ctx_768t * jax.lax.rsqrt(jnp.mean(jnp.square(_ctx_768t)) + 1e-12) * 0.953939
        ctx_768 = 0.000651243 + 0.998673 * (_ctx_768t + 0.3 * jax.random.normal(jax.random.fold_in(_rk, 611), (16, 1500, 96), jnp.float32))
        return (x, ctx_768)
    x, ctx_768 = _rec_inputs()

    def _L0_xattn_setup():
        import jax, jax.numpy as jnp
        import numpy as np
        import math
        N_HEADS = 16
        D_EMBED = 128
        D_CROSS = 96
        FF_DIM = 512
        D_HEAD = D_EMBED // N_HEADS
        LN_EPS = 1e-05

        def layer_norm(h, g, b):
            mu = jnp.mean(h, axis=-1, keepdims=True)
            var = jnp.var(h, axis=-1, keepdims=True)
            return (h - mu) * jax.lax.rsqrt(var + LN_EPS) * g + b

        def mha(q, k, v):
            B, Sq, _ = q.shape
            Skv = k.shape[1]
            qh = q.reshape(B, Sq, N_HEADS, D_HEAD).transpose(0, 2, 1, 3)
            kh = k.reshape(B, Skv, N_HEADS, D_HEAD).transpose(0, 2, 1, 3)
            vh = v.reshape(B, Skv, N_HEADS, D_HEAD).transpose(0, 2, 1, 3)
            scores = jnp.einsum('bhqd,bhkd->bhqk', qh, kh) / math.sqrt(D_HEAD)
            attn = jax.nn.softmax(scores, axis=-1)
            out = jnp.einsum('bhqk,bhkd->bhqd', attn, vh)
            return out.transpose(0, 2, 1, 3).reshape(B, Sq, D_EMBED)
        key = jax.random.key(seed)
        ks = jax.random.split(key, 24)
        s = 0.02
        inp = {'x': jax.random.normal(ks[0], (4, 128, D_EMBED), jnp.float32), 'y': jax.random.normal(ks[1], (4, 77, D_CROSS), jnp.float32), 'w_qkv': jax.random.normal(ks[2], (D_EMBED, 3 * D_EMBED), jnp.float32) * s, 'b_qkv': jnp.zeros((3 * D_EMBED,), jnp.float32), 'w_so': jax.random.normal(ks[3], (D_EMBED, D_EMBED), jnp.float32) * s, 'b_so': jnp.zeros((D_EMBED,), jnp.float32), 'w_q': jax.random.normal(ks[4], (D_EMBED, D_EMBED), jnp.float32) * s, 'b_q': jnp.zeros((D_EMBED,), jnp.float32), 'w_k': jax.random.normal(ks[5], (D_CROSS, D_EMBED), jnp.float32) * s, 'b_k': jnp.zeros((D_EMBED,), jnp.float32), 'w_v': jax.random.normal(ks[6], (D_CROSS, D_EMBED), jnp.float32) * s, 'b_v': jnp.zeros((D_EMBED,), jnp.float32), 'w_co': jax.random.normal(ks[7], (D_EMBED, D_EMBED), jnp.float32) * s, 'b_co': jnp.zeros((D_EMBED,), jnp.float32), 'w1': jax.random.normal(ks[8], (D_EMBED, FF_DIM), jnp.float32) * s, 'b1': jnp.zeros((FF_DIM,), jnp.float32), 'w2': jax.random.normal(ks[9], (FF_DIM, FF_DIM), jnp.float32) * s, 'b2': jnp.zeros((FF_DIM,), jnp.float32), 'w3': jax.random.normal(ks[10], (FF_DIM, D_EMBED), jnp.float32) * s, 'b3': jnp.zeros((D_EMBED,), jnp.float32), 'ln_g': jnp.ones((D_EMBED,), jnp.float32), 'ln_b': jnp.zeros((D_EMBED,), jnp.float32)}
        return inp
    _L0_xattn_all = _L0_xattn_setup()
    _L0_xattn_in = {k: v for k, v in _L0_xattn_all.items() if k in ('w_qkv', 'b_qkv', 'w_so', 'b_so', 'w_q', 'b_q', 'w_k', 'b_k', 'w_v', 'b_v', 'w_co', 'b_co', 'w1', 'b1', 'w2', 'b2', 'w3', 'b3', 'ln_g', 'ln_b')}
    del _L0_xattn_all

    def _L1_xattn_setup():
        import jax, jax.numpy as jnp
        import numpy as np
        D_Q, D_CTX, N_HEADS, HEAD_DIM = (128, 96, 16, 64)
        INNER = N_HEADS * HEAD_DIM
        EPS = 1e-05

        def _layernorm(x, gamma, beta):
            mu = jnp.mean(x, axis=-1, keepdims=True)
            var = jnp.var(x, axis=-1, keepdims=True)
            return (x - mu) * jax.lax.rsqrt(var + EPS) * gamma + beta
        key = jax.random.key(seed)
        ks = jax.random.split(key, 8)
        B, NQ, NC = (4, 128, 128)
        s_q = 1.0 / np.sqrt(D_Q)
        s_c = 1.0 / np.sqrt(D_CTX)
        s_i = 1.0 / np.sqrt(INNER)
        return {'x': jax.random.normal(ks[0], (B, NQ, D_Q), jnp.float32), 'context': jax.random.normal(ks[1], (B, NC, D_CTX), jnp.float32), 'Wq': jax.random.normal(ks[2], (D_Q, INNER), jnp.float32) * s_q, 'Wk': jax.random.normal(ks[3], (D_CTX, INNER), jnp.float32) * s_c, 'Wv': jax.random.normal(ks[4], (D_CTX, INNER), jnp.float32) * s_c, 'Wo': jax.random.normal(ks[5], (INNER, D_Q), jnp.float32) * s_i, 'bo': jnp.zeros((D_Q,), jnp.float32), 'gamma': jnp.ones((D_Q,), jnp.float32), 'beta': jnp.zeros((D_Q,), jnp.float32)}
    _L1_xattn_all = _L1_xattn_setup()
    _L1_xattn_in = {k: v for k, v in _L1_xattn_all.items() if k in ('Wq', 'Wk', 'Wv', 'Wo', 'bo', 'gamma', 'beta')}
    del _L1_xattn_all
    return {'x': x, 'ctx_768': ctx_768, 'L0_xattn_w_qkv': _L0_xattn_in['w_qkv'], 'L0_xattn_b_qkv': _L0_xattn_in['b_qkv'], 'L0_xattn_w_so': _L0_xattn_in['w_so'], 'L0_xattn_b_so': _L0_xattn_in['b_so'], 'L0_xattn_w_q': _L0_xattn_in['w_q'], 'L0_xattn_b_q': _L0_xattn_in['b_q'], 'L0_xattn_w_k': _L0_xattn_in['w_k'], 'L0_xattn_b_k': _L0_xattn_in['b_k'], 'L0_xattn_w_v': _L0_xattn_in['w_v'], 'L0_xattn_b_v': _L0_xattn_in['b_v'], 'L0_xattn_w_co': _L0_xattn_in['w_co'], 'L0_xattn_b_co': _L0_xattn_in['b_co'], 'L0_xattn_w1': _L0_xattn_in['w1'], 'L0_xattn_b1': _L0_xattn_in['b1'], 'L0_xattn_w2': _L0_xattn_in['w2'], 'L0_xattn_b2': _L0_xattn_in['b2'], 'L0_xattn_w3': _L0_xattn_in['w3'], 'L0_xattn_b3': _L0_xattn_in['b3'], 'L0_xattn_ln_g': _L0_xattn_in['ln_g'], 'L0_xattn_ln_b': _L0_xattn_in['ln_b'], 'L1_xattn_Wq': _L1_xattn_in['Wq'], 'L1_xattn_Wk': _L1_xattn_in['Wk'], 'L1_xattn_Wv': _L1_xattn_in['Wv'], 'L1_xattn_Wo': _L1_xattn_in['Wo'], 'L1_xattn_bo': _L1_xattn_in['bo'], 'L1_xattn_gamma': _L1_xattn_in['gamma'], 'L1_xattn_beta': _L1_xattn_in['beta']}

def reference(x, ctx_768, L0_xattn_w_qkv, L0_xattn_b_qkv, L0_xattn_w_so, L0_xattn_b_so, L0_xattn_w_q, L0_xattn_b_q, L0_xattn_w_k, L0_xattn_b_k, L0_xattn_w_v, L0_xattn_b_v, L0_xattn_w_co, L0_xattn_b_co, L0_xattn_w1, L0_xattn_b1, L0_xattn_w2, L0_xattn_b2, L0_xattn_w3, L0_xattn_b3, L0_xattn_ln_g, L0_xattn_ln_b, L1_xattn_Wq, L1_xattn_Wk, L1_xattn_Wv, L1_xattn_Wo, L1_xattn_bo, L1_xattn_gamma, L1_xattn_beta):
    import jax
    import jax.numpy as jnp

    def _L0_xattn_ref(x, y, w_qkv, b_qkv, w_so, b_so, w_q, b_q, w_k, b_k, w_v, b_v, w_co, b_co, w1, b1, w2, b2, w3, b3, ln_g, ln_b):
        import jax, jax.numpy as jnp
        import numpy as np
        import math
        N_HEADS = 16
        D_EMBED = 128
        D_CROSS = 96
        FF_DIM = 512
        D_HEAD = D_EMBED // N_HEADS
        LN_EPS = 1e-05

        def layer_norm(h, g, b):
            mu = jnp.mean(h, axis=-1, keepdims=True)
            var = jnp.var(h, axis=-1, keepdims=True)
            return (h - mu) * jax.lax.rsqrt(var + LN_EPS) * g + b

        def mha(q, k, v):
            B, Sq, _ = q.shape
            Skv = k.shape[1]
            qh = q.reshape(B, Sq, N_HEADS, D_HEAD).transpose(0, 2, 1, 3)
            kh = k.reshape(B, Skv, N_HEADS, D_HEAD).transpose(0, 2, 1, 3)
            vh = v.reshape(B, Skv, N_HEADS, D_HEAD).transpose(0, 2, 1, 3)
            scores = jnp.einsum('bhqd,bhkd->bhqk', qh, kh) / math.sqrt(D_HEAD)
            attn = jax.nn.softmax(scores, axis=-1)
            out = jnp.einsum('bhqk,bhkd->bhqd', attn, vh)
            return out.transpose(0, 2, 1, 3).reshape(B, Sq, D_EMBED)
        qkv = x @ w_qkv + b_qkv
        q, k, v = jnp.split(qkv, 3, axis=-1)
        sa = mha(q, k, v) @ w_so + b_so
        x = layer_norm(x + sa, ln_g, ln_b)
        qc = x @ w_q + b_q
        kc = y @ w_k + b_k
        vc = y @ w_v + b_v
        ca = mha(qc, kc, vc) @ w_co + b_co
        x = layer_norm(x + ca, ln_g, ln_b)
        h = jax.nn.relu(x @ w1 + b1)
        h = jax.nn.relu(h @ w2 + b2)
        ff = h @ w3 + b3
        x = layer_norm(x + ff, ln_g, ln_b)
        return x

    def _L1_xattn_ref(x, context, Wq, Wk, Wv, Wo, bo, gamma, beta):
        import jax, jax.numpy as jnp
        import numpy as np
        D_Q, D_CTX, N_HEADS, HEAD_DIM = (128, 96, 16, 64)
        INNER = N_HEADS * HEAD_DIM
        EPS = 1e-05

        def _layernorm(x, gamma, beta):
            mu = jnp.mean(x, axis=-1, keepdims=True)
            var = jnp.var(x, axis=-1, keepdims=True)
            return (x - mu) * jax.lax.rsqrt(var + EPS) * gamma + beta
        scale = HEAD_DIM ** (-0.5)
        h = _layernorm(x, gamma, beta)
        B, NQ, _ = x.shape
        NC = context.shape[1]
        Q = (h @ Wq).reshape(B, NQ, N_HEADS, HEAD_DIM)
        K = (context @ Wk).reshape(B, NC, N_HEADS, HEAD_DIM)
        V = (context @ Wv).reshape(B, NC, N_HEADS, HEAD_DIM)
        attn = jnp.einsum('bihd,bjhd->bhij', Q, K)
        attn = jax.nn.softmax(attn, axis=-1) * scale
        vals = jnp.einsum('bhij,bjhd->bihd', attn, V).reshape(B, NQ, INNER)
        out = vals @ Wo + bo
        return x + out
    x = _L0_xattn_ref(x, ctx_768, L0_xattn_w_qkv, L0_xattn_b_qkv, L0_xattn_w_so, L0_xattn_b_so, L0_xattn_w_q, L0_xattn_b_q, L0_xattn_w_k, L0_xattn_b_k, L0_xattn_w_v, L0_xattn_b_v, L0_xattn_w_co, L0_xattn_b_co, L0_xattn_w1, L0_xattn_b1, L0_xattn_w2, L0_xattn_b2, L0_xattn_w3, L0_xattn_b3, L0_xattn_ln_g, L0_xattn_ln_b)
    x = _L1_xattn_ref(x, ctx_768, L1_xattn_Wq, L1_xattn_Wk, L1_xattn_Wv, L1_xattn_Wo, L1_xattn_bo, L1_xattn_gamma, L1_xattn_beta)
    return x

_drawn_inputs = setup_inputs


def setup_inputs(seed=0):
    import zlib

    import numpy as np

    out = dict(_drawn_inputs(seed))
    spreads = {'L0_xattn_b_qkv': (0.0, 0.412),
     'L0_xattn_b_so': (0.0, 0.1),
     'L0_xattn_b_q': (0.0, 0.8),
     'L0_xattn_b_k': (0.0, 0.8),
     'L0_xattn_b_v': (0.0, 0.344),
     'L0_xattn_b_co': (0.0, 0.1),
     'L0_xattn_b1': (0.0, 0.8),
     'L0_xattn_b2': (0.0, 0.42),
     'L0_xattn_b3': (0.0, 0.1),
     'L0_xattn_ln_g': (1.0, 0.2),
     'L0_xattn_ln_b': (0.0, 0.1),
     'L1_xattn_bo': (0.0, 0.1),
     'L1_xattn_gamma': (1.0, 0.2),
     'L1_xattn_beta': (0.0, 0.336)}
    factors = {'L0_xattn_w_qkv': 8.0,
     'L0_xattn_w_so': 2.955,
     'L0_xattn_w_q': 8.0,
     'L0_xattn_w_k': 8.0,
     'L0_xattn_w_v': 3.202,
     'L0_xattn_w1': 3.768,
     'L0_xattn_w2': 3.185}
    for name, (base, spread) in spreads.items():
        noise = np.random.default_rng([zlib.crc32(name.encode()), seed]).standard_normal(out[name].shape)
        drawn = base * np.exp(spread * noise) if base else spread * noise
        out[name] = jnp.asarray(drawn.astype(out[name].dtype))
    for name, factor in factors.items():
        out[name] = (out[name] * factor).astype(out[name].dtype)
    return out
```

```python
from contextlib import ExitStack

import numpy as np

import concourse.bass as bass
from concourse import mybir
from concourse.alu_op_type import AluOpType as ALU

ACT = mybir.ActivationFunctionType
AX = mybir.AxisListType
F32 = mybir.dt.float32
F16 = mybir.dt.float16
BF16 = mybir.dt.bfloat16

B, SQ, D = 16, 56, 128
SK, DC = 1500, 96
H = 16
DH0, DH1 = 8, 64
FF = 512
EPS = 1e-5
TOK = B * SQ
TP = 2 * SQ
NT = B // 2
HALF = TOK // 2
NQ = H * SQ
KC = 125
NC = SK // KC
SP = 500
NSP = SK // SP
G = 4
GH = H // G
PAIRS = H // 2
SCALE0 = DH0 ** -0.5
SCALE1 = DH1 ** -0.5
QT1 = NQ // 128
ON = 100
LIFT = 10 * float(np.log(2.0))

C_ID, C_M4, C_MM0, C_MM1, C_M16, C_MV, C_END = 0, 128, 132, 140, 147, 163, 165


def shape_table():
    t = np.zeros((128, C_END), np.float32)
    r = np.arange(128)[:, None]
    t[:, C_ID:C_M4] = np.eye(128)
    t[:, C_M4:C_MM0] = (r % 32) // DH0 == np.arange(GH)
    t[:, C_MM0:C_MM1] = (r >= 96) * (r < 112) * ((r - 96) % PAIRS == np.arange(PAIRS))
    t[:, C_MM1:C_M16] = (r >= 96) * (r < 110) * ((r - 96) % QT1 == np.arange(QT1))
    t[:, C_M16:C_MV] = r // DH0 == np.arange(H)
    t[:, C_MV:C_END] = r // SQ == np.arange(2)
    return t


def wait_for(eng, sem, count):
    if isinstance(count, int) and count <= 0:
        return
    eng.wait_ge(sem, count)


def spread(ap, dim, n):
    shape = list(ap.shape)
    return ap.unsqueeze(dim).broadcast_to(shape[:dim] + [n] + shape[dim:])


def over_pairs(eng, body, before=()):
    for i, par in before:
        body(i, par)
    for par in (0, 1):
        body(0, par)
    with eng.Fori(1, NT - 1) as i:
        body(i, 0)
        body(i, 1)
    for par in (0, 1):
        body(NT - 1, par)


def inside(i, par, ahead):
    return not isinstance(i, int) or 0 <= 2 * i + par + ahead < B


def program(nc, table, x, ctx_768, w_qkv, b_qkv, w_so, b_so, w_q, b_q, w_k, b_k, w_v, b_v, w_co, b_co,
            w1, b1, w2, b2, w3, b3, ln_g, ln_b, Wq, Wk, Wv, Wo, bo, gamma, beta, out):
    with ExitStack() as ctx:
        def sb_in(stack, name, shape, dt=F32):
            return stack.enter_context(nc.sbuf_tensor(name, shape, dt))

        def sb(name, shape, dt=F32):
            return sb_in(ctx, name, shape, dt)

        def sem(name):
            return ctx.enter_context(nc.semaphore(name))

        PS = ctx.enter_context(nc.psum_tensor("PS", [128, 8, 512], F32))

        tab = sb("tab", [128, C_END])
        ident = tab[:, C_ID:C_M4]
        X = sb("X", [TP, NT, D])
        T128 = sb("T128", [128, TOK])
        att = sb("att", [128, TOK])
        work = sb("work", [TP, NT, D])
        squares = sb("squares", [TP, NT, D])
        stat = sb("stat", [TP, 4, NT])
        rows = sb("rows", [TP, 9, D])
        R_BV, R_SO, R_CO, R_B3, R_G, R_B, R_BO, R_GA, R_BE = range(9)
        wso = sb("wso", [D, D])
        wco = sb("wco", [D, D])
        w1s = sb("w1s", [D, FF])
        w2s = sb("w2s", [128, 4, FF])
        w3s = sb("w3s", [128, 4, D])
        b1s = sb("b1s", [128, 4])
        b2s = sb("b2s", [128, 4])
        wq3 = sb("wq3", [D, G, 3, 32])
        bq3 = sb("bq3", [96, G])
        wk = sb("wk", [DC + 1, D])
        wv = sb("wv", [DC + 1, D])
        Q16 = sb("Q16", [96, G, TOK], F16)
        Wqk = sb("Wqk", [D, H, DC])
        Wvo = sb("Wvo", [DC, H, D])

        first = ctx.enter_context(ExitStack())
        wqkv = sb_in(first, "wqkv", [D, 3 * D])
        bqk = sb_in(first, "bqk", [D, 2])
        QT = sb_in(first, "QT", [D, B, SQ])
        KT = sb_in(first, "KT", [D, B, SQ])
        setup = ExitStack()
        Wqs = sb_in(setup, "Wqs", [D, H * DH1])
        Wks = sb_in(setup, "Wks", [DC, H * DH1])
        Wvs = sb_in(setup, "Wvs", [DC, H * DH1])
        Wos = sb_in(setup, "Wos", [128, H // 2, D])
        WqT = sb_in(setup, "WqT", [128, 8, D])
        WkT = sb_in(setup, "WkT", [128, 8, DC])
        WvT = sb_in(setup, "WvT", [128, 8, DC])

        table_in, x_in, qkv_in, small_in = sem("table_in"), sem("x_in"), sem("qkv_in"), sem("small_in")
        wq1_in, wk1_in, wv1_in, wo1_in, later_in = (
            sem("wq1_in"), sem("wk1_in"), sem("wv1_in"), sem("wo1_in"), sem("later_in"))
        x_turned, x_kept = sem("x_turned"), sem("x_kept")
        wqT_made, wkT_made, wvT_made = sem("wqT_made"), sem("wkT_made"), sem("wvT_made")
        wqT_kept, wkT_kept, wvT_kept = sem("wqT_kept"), sem("wkT_kept"), sem("wvT_kept")
        qk_made, qk_kept = sem("qk_made"), sem("qk_kept")
        wqk_made, wvo_made, wqk_kept, wvo_kept = sem("wqk_made"), sem("wvo_made"), sem("wqk_kept"), sem("wvo_kept")

        with nc.Block() as block:
            @block.sync
            def _(sp):
                sp.dma_start(tab[:], table).then_inc(table_in, 16)
                sp.dma_start(X[:], x.rearrange("b q d -> (b q) d").rearrange("(t p) d -> p t d", p=TP)).then_inc(x_in, 16)
                sp.dma_start(wqkv[:], w_qkv).then_inc(qkv_in, 16)
                sp.dma_start(bqk[:], b_qkv[0:2 * D].rearrange("(s p) -> p s", p=D), allow_slow_non_contiguous=True).then_inc(qkv_in, 16)
                sp.dma_start(Wqs[:], Wq).then_inc(wq1_in, 16)
                sp.dma_start(Wks[:], Wk).then_inc(wk1_in, 16)
                sp.dma_start(Wvs[:], Wv).then_inc(wv1_in, 16)
                sp.dma_start(Wos[:], Wo.rearrange("(t p) d -> p t d", p=128)).then_inc(wo1_in, 16)

            @block.gpsimd
            def _(pool):
                for k, row in enumerate((b_qkv[2 * D:3 * D], b_so, b_co, b3, ln_g, ln_b, bo, gamma, beta)):
                    pool.dma_start(rows[:, k, :], row.partition_broadcast(TP)).then_inc(small_in, 16)
                pool.dma_start(wso[:], w_so).then_inc(small_in, 16)
                pool.dma_start(wco[:], w_co).then_inc(small_in, 16)
                for rep in range(3):
                    pool.dma_start(wq3[:, :, rep, :], w_q.rearrange("d (g r) -> d g r", g=G)).then_inc(small_in, 16)
                    pool.dma_start(bq3[32 * rep:32 * rep + 32, :], b_q.rearrange("(g r) -> r g", g=G), allow_slow_non_contiguous=True).then_inc(small_in, 16)
                pool.dma_start(wk[0:DC, :], w_k).then_inc(small_in, 16)
                pool.dma_start(wk[DC:DC + 1, :], b_k.unsqueeze(0)).then_inc(small_in, 16)
                pool.dma_start(wv[0:DC, :], w_v).then_inc(small_in, 16)
                pool.dma_start(wv[DC:DC + 1, :], b_v.unsqueeze(0)).then_inc(small_in, 16)
                pool.dma_start(w1s[:], w1).then_inc(later_in, 16)
                pool.dma_start(w2s[:], w2.rearrange("(k p) n -> p k n", p=128)).then_inc(later_in, 16)
                pool.dma_start(w3s[:], w3.rearrange("(k p) n -> p k n", p=128)).then_inc(later_in, 16)
                pool.dma_start(b1s[:], b1.rearrange("(k p) -> p k", p=128), allow_slow_non_contiguous=True).then_inc(later_in, 16)
                pool.dma_start(b2s[:], b2.rearrange("(k p) -> p k", p=128), allow_slow_non_contiguous=True).then_inc(later_in, 16)
                pool.wait_ge(small_in, 16 * 21)
                pool.wait_ge(later_in, 16 * 5)

            @block.tensor
            def _(pe):
                pe.wait_ge(table_in, 16)
                pe.wait_ge(x_in, 16)
                for t in range(NT):
                    mm = pe.transpose(PS[:, t // 4, (t % 4) * TP:(t % 4 + 1) * TP], X[:, t, :], ident[0:TP, 0:TP])
                mm.then_inc(x_turned, 1)
                for src, arrived, made, bank, rows_in in (
                        (Wqs, wq1_in, wqT_made, 2, D), (Wks, wk1_in, wkT_made, 4, DC), (Wvs, wv1_in, wvT_made, 6, DC)):
                    pe.wait_ge(arrived, 16)
                    for t in range(8):
                        mm = pe.transpose(PS[:, bank + t // 4, (t % 4) * rows_in:(t % 4 + 1) * rows_in],
                                          src[:, t * 128:(t + 1) * 128], ident[0:rows_in, 0:rows_in])
                    mm.then_inc(made, 1)
                pe.wait_ge(qkv_in, 32)
                pe.wait_ge(x_kept, 1)
                pe.wait_ge(wqT_kept, 1)
                for s in range(2):
                    for half in range(2):
                        mm = pe.matmul(PS[:, 2 * s + half, 0:HALF], wqkv[:, s * D:(s + 1) * D],
                                       T128[:, half * HALF:(half + 1) * HALF], start=True, stop=True)
                mm.then_inc(qk_made, 1)
                pe.wait_ge(wkT_kept, 1)
                pe.wait_ge(wvT_kept, 1)
                for h in range(H):
                    at = 64 * (h % 2)
                    mm = pe.matmul(PS[:, 4 + 2 * (h % 2) + h // 8, (h // 2 % 4) * DC:(h // 2 % 4 + 1) * DC], WqT[at:at + 64, h // 2, :],
                                   WkT[at:at + 64, h // 2, :], start=True, stop=True)
                mm.then_inc(wqk_made, 1)
                pe.wait_ge(wo1_in, 16)
                pe.wait_ge(qk_kept, 2)
                for h in range(H):
                    at = 64 * (h % 2)
                    mm = pe.matmul(PS[0:DC, 2 * (h % 2) + h // 8, (h // 2 % 4) * D:(h // 2 % 4 + 1) * D], WvT[at:at + 64, h // 2, :],
                                   Wos[at:at + 64, h // 2, :], start=True, stop=True)
                mm.then_inc(wvo_made, 1)

            @block.vector
            def _(dve):
                dve.wait_ge(x_turned, 1)
                nc.vector.tensor_copy(T128[:].rearrange("p (h c) -> p h c", h=2), PS[:, 0:2, 0:HALF]).then_inc(x_kept, 1)
                dve.wait_ge(wkT_made, 1)
                nc.vector.tensor_copy(WkT[:].rearrange("p (a b) c -> p a (b c)", a=2), PS[:, 4:6, 0:4 * DC]).then_inc(wkT_kept, 1)
                dve.wait_ge(qk_made, 1)
                nc.vector.tensor_scalar(QT[:].rearrange("p (h b) q -> p h (b q)", h=2), PS[:, 0:2, 0:HALF],
                                        bqk[:, 0:1], None, ALU.add).then_inc(qk_kept, 1)
                nc.vector.tensor_scalar(KT[:].rearrange("p (h b) q -> p h (b q)", h=2), PS[:, 2:4, 0:HALF],
                                        bqk[:, 1:2], None, ALU.add).then_inc(qk_kept, 1)
                dve.wait_ge(wvo_made, 1)
                for j in range(2):
                    nc.vector.tensor_copy(Wvo[:].rearrange("p (a b j) c -> p j a b c", a=2, j=2)[:, j],
                                          PS[0:DC, 2 * j:2 * j + 2, 0:4 * D].rearrange("p a (b c) -> p a b c", b=4)).then_inc(wvo_kept, 1)

            @block.scalar
            def _(act):
                act.wait_ge(wqT_made, 1)
                nc.scalar.copy(WqT[:].rearrange("p (a b) c -> p a (b c)", a=2), PS[:, 2:4, 0:4 * D]).then_inc(wqT_kept, 1)
                act.wait_ge(wvT_made, 1)
                nc.scalar.copy(WvT[:].rearrange("p (a b) c -> p a (b c)", a=2), PS[:, 6:8, 0:4 * DC]).then_inc(wvT_kept, 1)
                act.wait_ge(wqk_made, 1)
                for j in range(2):
                    nc.scalar.copy(Wqk[:].rearrange("p (a b j) c -> p j a b c", a=2, j=2)[:, j],
                                   PS[:, 4 + 2 * j:6 + 2 * j, 0:4 * DC].rearrange("p a (b c) -> p a b c", b=4)).then_inc(wqk_kept, 1)
        setup.close()

        selfa = ExitStack()
        Kbd = sb_in(selfa, "Kbd", [D, 2, H, SQ])
        Qp = sb_in(selfa, "Qp", [D, 2, 2, 64])
        Xd = sb_in(selfa, "Xd", [D, 2, 2, 2, SQ])
        V2 = sb_in(selfa, "V2", [TP, 2, 2, D])
        Vbd = sb_in(selfa, "Vbd", [TP, 2, 2, PAIRS, 18])
        top = sb_in(selfa, "top", [128, 2, H])
        Sm = sb_in(selfa, "Sm", [128, 2, NQ])
        Pe = sb_in(selfa, "Pe", [128, 2, NQ])
        PT = sb_in(selfa, "PT", [TP, PAIRS, 128])
        rsum = sb_in(selfa, "rsum", [128, PAIRS, 2])
        ao = sb_in(selfa, "ao", [128, PAIRS, 2, DH0])
        s_zero, s_ones = sem("s_zero"), sem("s_ones")
        s_staged, s_kbd, s_vbd = sem("s_staged"), sem("s_kbd"), sem("s_vbd")
        s_v, s_vkept, s_scores = sem("s_v"), sem("s_vkept"), sem("s_scores")
        s_top, s_sm, s_exp, s_turned, s_pt = sem("s_top"), sem("s_sm"), sem("s_exp"), sem("s_turned"), sem("s_pt")
        s_pv, s_rsum, s_ao, s_aoT, s_att = sem("s_pv"), sem("s_rsum"), sem("s_ao"), sem("s_aoT"), sem("s_att")
        SB = 6

        def over_tiles(eng, body):
            body(0, 0, True, False)
            body(1, 1, True, True)
            with eng.Fori(1, NT // 2) as i:
                body(i * 2, 0, True, True)
                body(i * 2 + 1, 1, True, True)
            body(NT, 0, False, True)

        with nc.Block() as block:
            @block.gpsimd
            def _(pool):
                def step(t, slot, early, late):
                    if not early:
                        return
                    wait_for(pool, s_scores, t)
                    for j in range(2):
                        k = nc.gpsimd.tensor_tensor(Kbd[:, j], KT[:, bass.ds(t * 2 + j, 1), :].broadcast_to([D, H, SQ]),
                                                    spread(tab[:, C_M16:C_MV], 2, SQ), ALU.mult)
                    k.then_inc(s_kbd, 1)
                    pool.wait_ge(s_vkept, t + 1)
                    wait_for(pool, s_pv, t - 1)
                    for j in range(2):
                        v = nc.gpsimd.tensor_tensor(
                            Vbd[:, slot, j, :, 0:16].rearrange("p a (b c) -> p a b c", b=2),
                            V2[:, slot, j].rearrange("p (a b c) -> p a b c", a=PAIRS, b=2),
                            spread(spread(tab[0:TP, C_MV:C_END], 1, PAIRS), 3, DH0), ALU.mult)
                    v.then_inc(s_vbd, 1)
                over_tiles(pool, step)

            @block.scalar
            def _(act):
                act.wait_ge(s_zero, 1)

                def step(t, slot, early, late):
                    if early:
                        wait_for(act, s_scores, t - 1)
                        nc.scalar.copy(Qp[:, slot, :, 0:SQ], QT[:, bass.ds(t * 2, 2), :]).then_inc(s_staged, 1)
                        nc.scalar.copy(Xd[:, slot], spread(T128[:].rearrange("p (b q) -> p b q", b=B)[:, bass.ds(t * 2, 2), :], 2, 2)).then_inc(s_staged, 1)
                    if late:
                        act.wait_ge(s_turned, t)
                        nc.scalar.copy(PT[:].rearrange("p (a b) c -> p a (b c)", a=2), PS[0:TP, 4:6, :]).then_inc(s_pt, 1)
                    if early:
                        act.wait_ge(s_sm, t + 1)
                        nc.scalar.activation(Pe[:, slot], Sm[:, slot], ACT.Exp, scale=SCALE0).then_inc(s_exp, 1)
                    if late:
                        act.wait_ge(s_aoT, t)
                        nc.scalar.copy(att[:].rearrange("p (b q) -> p b q", b=B)[:, bass.ds(t * 2 - 2, 2), :],
                                       PS[:, SB, 256:384].rearrange("p (j q) -> p j q", j=2)[:, :, 0:SQ]).then_inc(s_att, 1)
                over_tiles(act, step)

            @block.tensor
            def _(pe):
                def step(t, slot, early, late):
                    if late:
                        other = 1 - slot
                        pe.wait_ge(s_exp, t)
                        wait_for(pe, s_pt, t - 1)
                        for p in range(PAIRS):
                            mm = pe.transpose(PS[0:TP, 4 + p // 4, (p % 4) * 128:(p % 4 + 1) * 128],
                                              Pe[:, other, p * TP:(p + 1) * TP], ident)
                        mm.then_inc(s_turned, 1)
                    if early:
                        pe.wait_ge(s_staged, t * 2 + 2)
                        wait_for(pe, s_vkept, t)
                        for j in range(2):
                            mm = pe.matmul(PS[0:TP, 7, j * D:(j + 1) * D], Xd[:, slot, j], wqkv[:, 2 * D:3 * D], start=True, stop=True)
                        mm.then_inc(s_v, 1)
                        pe.wait_ge(s_kbd, t + 1)
                        wait_for(pe, s_sm, t - 1)
                        for j in range(2):
                            for half in range(2):
                                mm = pe.matmul(PS[64 * j:64 * j + 64, 2 * slot + half, 0:HALF], Qp[:, slot, j, :],
                                               Kbd[:, j, 8 * half:8 * half + 8, :], start=True, stop=True)
                        mm.then_inc(s_scores, 1)
                    if late:
                        pe.wait_ge(s_pt, t)
                        pe.wait_ge(s_vbd, t)
                        wait_for(pe, s_att, t - 1)
                        for p in range(PAIRS):
                            for j in range(2):
                                mm = pe.matmul(PS[64 * j:64 * j + 64, SB, p * 18:(p + 1) * 18], PT[:, p, 64 * j:64 * j + 64],
                                               Vbd[:, other, j, p, :], start=True, stop=True)
                        mm.then_inc(s_pv, 1)
                        pe.wait_ge(s_ao, t)
                        pe.transpose(PS[:, SB, 256:384], ao[:].rearrange("p a b c -> p (a b c)"), ident).then_inc(s_aoT, 1)
                over_tiles(pe, step)

            @block.vector
            def _(dve):
                nc.vector.memset(Qp[:], 0.0).then_inc(s_zero, 1)
                for slot in range(2):
                    for j in range(2):
                        nc.vector.tensor_copy(Vbd[:, slot, j, :, 16:18], spread(tab[0:TP, C_MV:C_END], 1, PAIRS)).then_inc(s_ones, 1)

                def step(t, slot, early, late):
                    if early:
                        dve.wait_ge(s_v, t + 1)
                        wait_for(dve, s_vbd, t - 1)
                        nc.vector.tensor_tensor(V2[:, slot], PS[0:TP, 7, 0:2 * D].rearrange("p (j d) -> p j d", j=2),
                                                spread(rows[:, R_BV, :], 1, 2), ALU.add).then_inc(s_vkept, 1)
                        dve.wait_ge(s_scores, t + 1)
                        sc = PS[:, 2 * slot:2 * slot + 2, 0:HALF].rearrange("p a (h k) -> p a h k", h=8)
                        nc.vector.tensor_reduce(top[:, slot].rearrange("p (a h) -> p a h", a=2), sc, AX.X, ALU.max).then_inc(s_top, 1)
                        dve.wait_ge(s_top, t + 1)
                        wait_for(dve, s_exp, t - 1)
                        nc.vector.tensor_tensor(Sm[:, slot].rearrange("p (a h k) -> p a h k", a=2, h=8), sc,
                                                spread(top[:, slot].rearrange("p (a h) -> p a h", a=2), 3, SQ),
                                                ALU.subtract).then_inc(s_sm, 1)
                    if late:
                        dve.wait_ge(s_pv, t)
                        o = PS[:, SB, 0:PAIRS * 18].rearrange("p (a c) -> p a c", a=PAIRS)
                        nc.vector.reciprocal(rsum[:], o[:, :, 16:18]).then_inc(s_rsum, 1)
                        dve.wait_ge(s_rsum, t)
                        wait_for(dve, s_aoT, t - 1)
                        nc.vector.tensor_tensor(ao[:], o[:, :, 0:16].rearrange("p a (b c) -> p a b c", b=2),
                                                spread(rsum[:], 3, DH0), ALU.mult).then_inc(s_ao, 1)
                over_tiles(dve, step)
        selfa.close()
        first.close()

        def project_tiles(pe, src, w, done):
            for t in range(NT):
                mm = pe.matmul(PS[0:TP, t // 4, (t % 4) * D:(t % 4 + 1) * D], src[:, t * TP:(t + 1) * TP], w, start=True, stop=True)
            mm.then_inc(done, 1)

        def turn_tiles(pe, src, done, bank):
            for t in range(NT):
                mm = pe.transpose(PS[:, bank + t // 4, (t % 4) * TP:(t % 4 + 1) * TP], src[:, t, :], ident[0:TP, 0:TP])
            mm.then_inc(done, 1)

        def row(k):
            return spread(rows[:, k, :], 1, NT)

        def norm_vector(dve, tag, src, dst, gain, shift, link, var_ready, root_ready):
            nc.vector.tensor_reduce(stat[:, 0, :], src, AX.X, ALU.add).then_inc(link, 1)
            dve.wait_ge(link, tag + 1)
            nc.vector.tensor_scalar(stat[:, 0, :], stat[:, 0, :], -1.0 / D, None, ALU.mult).then_inc(link, 1)
            dve.wait_ge(link, tag + 2)
            nc.vector.tensor_tensor(work[:], src, spread(stat[:, 0, :], 2, D), ALU.add).then_inc(link, 1)
            dve.wait_ge(link, tag + 3)
            nc.vector.tensor_tensor(squares[:], work[:], work[:], ALU.mult).then_inc(link, 1)
            dve.wait_ge(link, tag + 4)
            nc.vector.tensor_reduce(stat[:, 1, :], squares[:], AX.X, ALU.add).then_inc(link, 1)
            dve.wait_ge(link, tag + 5)
            nc.vector.tensor_scalar(stat[:, 1, :], stat[:, 1, :], 1.0 / D, EPS, ALU.mult, ALU.add).then_inc(var_ready, 1)
            dve.wait_ge(root_ready, 1)
            nc.vector.reciprocal(stat[:, 3, :], stat[:, 2, :]).then_inc(link, 1)
            dve.wait_ge(link, tag + 6)
            nc.vector.tensor_tensor(work[:], work[:], spread(stat[:, 3, :], 2, D), ALU.mult).then_inc(link, 1)
            dve.wait_ge(link, tag + 7)
            nc.vector.tensor_tensor(work[:], work[:], row(gain), ALU.mult).then_inc(link, 1)
            dve.wait_ge(link, tag + 8)
            nc.vector.tensor_tensor(dst, work[:], row(shift), ALU.add).then_inc(link, 1)
            dve.wait_ge(link, tag + 9)
            return tag + 9

        def norm_root(act, var_ready, root_ready):
            act.wait_ge(var_ready, 1)
            nc.scalar.activation(stat[:, 2, :], stat[:, 1, :], ACT.Sqrt).then_inc(root_ready, 1)

        def add_residual(dve, tag, bias, link):
            nc.vector.tensor_tensor(work[:].rearrange("p (a t) d -> p a t d", a=2),
                                    PS[0:TP, 0:2, :].rearrange("p a (t d) -> p a t d", d=D),
                                    row(bias).rearrange("p (a t) d -> p a t d", a=2), ALU.add).then_inc(link, 1)
            dve.wait_ge(link, tag + 1)
            nc.vector.tensor_tensor(X[:], work[:], X[:], ALU.add).then_inc(link, 1)
            dve.wait_ge(link, tag + 2)
            return tag + 2

        a_proj, a_link, a_var, a_root = sem("a_proj"), sem("a_link"), sem("a_var"), sem("a_root")
        a_x, a_turned, a_kept, a_q, a_qkept, a_qlink = sem("a_x"), sem("a_turned"), sem("a_kept"), sem("a_q"), sem("a_qkept"), sem("a_qlink")
        qst = ExitStack()
        Q32 = sb_in(qst, "Q32", [96, G, TOK])
        with nc.Block() as block:
            @block.tensor
            def _(pe):
                project_tiles(pe, att, wso[:], a_proj)
                pe.wait_ge(a_x, 1)
                turn_tiles(pe, X, a_turned, 0)
                pe.wait_ge(a_kept, 1)
                for g in range(G):
                    for half in range(2):
                        mm = pe.matmul(PS[0:96, 2 * g + half, 0:HALF], wq3[:, g].rearrange("p a b -> p (a b)"),
                                       T128[:, half * HALF:(half + 1) * HALF], start=True, stop=True)
                    mm.then_inc(a_q, 1)

            @block.vector
            def _(dve):
                dve.wait_ge(a_proj, 1)
                n = add_residual(dve, 0, R_SO, a_link)
                n = norm_vector(dve, n, X[:], X[:], R_G, R_B, a_link, a_var, a_root)
                nc.vector.tensor_copy(stat[:, 0, :], stat[:, 3, :]).then_inc(a_x, 1)
                dve.wait_ge(a_turned, 1)
                nc.vector.tensor_copy(T128[:].rearrange("p (h c) -> p h c", h=2), PS[:, 0:2, 0:HALF]).then_inc(a_kept, 1)
                for g in range(G):
                    dve.wait_ge(a_qkept, g + 1)
                    nc.vector.tensor_copy(Q16[:, g, :], Q32[:, g, :]).then_inc(a_qlink, 1)
                    dve.wait_ge(a_qlink, 2 * g + 1)
                    nc.vector.tensor_tensor(Q16[64:96, g, :], Q32[64:96, g, :], Q16[64:96, g, :], ALU.subtract).then_inc(a_qlink, 1)

            @block.scalar
            def _(act):
                norm_root(act, a_var, a_root)
                for g in range(G):
                    act.wait_ge(a_q, g + 1)
                    nc.scalar.activation(Q32[:, g, :].rearrange("p (h c) -> p h c", h=2), PS[0:96, 2 * g:2 * g + 2, 0:HALF],
                                         ACT.Identity, bias=bq3[:, g:g + 1]).then_inc(a_qkept, 1)
        qst.close()

        cross = ExitStack()
        TURN = 72
        cx = sb_in(cross, "cx", [KC, 2, NC, DC])
        cT = sb_in(cross, "cT", [DC + 1, SK])
        KH = sb_in(cross, "KH", [D, 2, SK], F16)
        Kst = sb_in(cross, "Kst", [112, 2, G, SK], F16)
        Qst = sb_in(cross, "Qst", [112, 2, G, GH * SQ], F16)
        Vst = sb_in(cross, "Vst", [KC, 2, NC, PAIRS, 32])
        Pb = sb_in(cross, "Pb", [KC, 3, NQ])
        m24 = sb_in(cross, "m24", [TP, PAIRS, NSP])
        mtop = sb_in(cross, "mtop", [TP, PAIRS])
        mhigh = sb_in(cross, "mhigh", [TP, PAIRS], F16)
        mneg = sb_in(cross, "mneg", [TP, 2 * PAIRS])
        Os = sb_in(cross, "Os", [128, 5 * SQ])
        rs = sb_in(cross, "rs", [SQ, 4, 4])
        an = sb_in(cross, "an", [TURN, 2, 4, 2, DH0])
        cx_in = [sem("cx_in0"), sem("cx_in1")]
        kst_in = [sem("kst_in0"), sem("kst_in1")]
        ones_set = sem("ones_set")
        ct_turned, ct_kept = sem("ct_turned"), sem("ct_kept")
        k_made, k_high, k_split = sem("k_made"), sem("k_high"), sem("k_split")
        v_made, v_kept, q_laid = sem("v_made"), sem("v_kept"), sem("q_laid")
        s_filled, s_reduced = sem("s_filled"), sem("s_reduced")
        m_link, m_ready, m_turned, m_laid = sem("m_link"), sem("m_ready"), sem("m_turned"), sem("m_laid")
        st_done, exp_done, pv_done = sem("st_done"), sem("exp_done"), sem("pv_done")
        o_kept, o_turned, r_ready, an_ready, an_turned, att_kept = (
            sem("o_kept"), sem("o_turned"), sem("r_ready"), sem("an_ready"), sem("an_turned"), sem("att_kept"))
        OB, WB = 4, 5
        PER_KST = 3 * G * 16
        PIECES = [range(0), range(0)] + [range(5 * k // 2, 5 * (k + 1) // 2) for k in range(9)] + [range(22, 24)]

        with nc.Block() as block:
            @block.sync
            def _(sp):
                def load_context(i, par, ahead):
                    slot, pair, n = (par + ahead) % 2, i + (par + ahead) // 2, i * 2 + par + ahead
                    wait_for(sp, ct_turned, (n - 1) * 3)
                    sp.dma_start(cx[:, slot], ctx_768[n].rearrange("(p c) d -> p c d", c=NC)).then_inc(cx_in[slot], 16)

                def lay_keys(i, par, ahead):
                    slot, n = (par + ahead) % 2, i * 2 + par + ahead
                    sp.wait_ge(v_made, n * 3 + 1)
                    for block_row, half in enumerate((0, 1, 0)):
                        for g in range(G):
                            sp.dma_start(Kst[32 * block_row:32 * block_row + 32, slot, g, :],
                                         KH[32 * g:32 * g + 32, half, :]).then_inc(kst_in[slot], 16)

                def body(i, par):
                    if inside(i, par, 2):
                        load_context(i, par, 2)
                        lay_keys(i, par, 2)
                over_pairs(sp, body, before=((-1, 0), (-1, 1)))

            @block.gpsimd
            def _(pool):
                def body(i, par):
                    if not inside(i, par, 1):
                        return
                    slot, n = (par + 1) % 2, i * 2 + par + 1
                    wait_for(pool, st_done, (n - 1) * NC)
                    for g in range(G):
                        q = nc.gpsimd.tensor_tensor(
                            Qst[0:96, slot, g].rearrange("p (j q) -> p j q", j=GH),
                            Q16[:, g, :].rearrange("p (b q) -> p b q", b=B)[:, bass.ds(n, 1), :].broadcast_to([96, GH, SQ]),
                            spread(tab[0:96, C_M4:C_MM0], 2, SQ), ALU.mult)
                    q.then_inc(q_laid, 1)
                over_pairs(pool, body, before=((-1, 1),))

            @block.tensor
            def _(pe):
                def scores_t(i, par, c):
                    n = i * 2 + par
                    if c == 0:
                        pe.wait_ge(m_laid, n + 1)
                    wait_for(pe, exp_done, n * NC + c - 1)
                    for g in range(G):
                        mm = pe.matmul(PS[0:KC, 2 * (c % 2) + g // 2, (g % 2) * 224:(g % 2 + 1) * 224],
                                       Kst[:, par, g, c * KC:(c + 1) * KC], Qst[:, par, g, :], start=True, stop=True)
                    mm.then_inc(st_done, 1)

                def values(i, par, c):
                    n = i * 2 + par
                    pe.wait_ge(exp_done, n * NC + c + 1)
                    if c == 0:
                        pe.wait_ge(v_kept, n * 3 + 3)
                        wait_for(pe, o_kept, n)
                    for p in range(PAIRS):
                        mm = pe.matmul(PS[32 * (p % 4):32 * (p % 4) + 32, OB, (p // 4) * TP:(p // 4 + 1) * TP],
                                       Vst[:, par, c, p, :], Pb[:, c % 3, p * TP:(p + 1) * TP],
                                       start=(c == 0 and p < 4), stop=(c == NC - 1), skip_group_check=True)
                    mm.then_inc(pv_done, 1)

                def score_piece(i, par, k):
                    slot, pair, n = (par + 1) % 2, i + (par + 1) // 2, i * 2 + par + 1
                    if k == 0:
                        pe.wait_ge(q_laid, n + 1)
                        pe.wait_ge(kst_in[slot], pair * PER_KST + PER_KST)
                    wait_for(pe, s_reduced, n * 24 + k - 1)
                    p, part = k // NSP, k % NSP
                    pe.matmul(PS[0:TP, 6 + k % 2, 0:SP], Qst[0:96, slot, p // 2, (p % 2) * TP:(p % 2 + 1) * TP],
                              Kst[0:96, slot, p // 2, part * SP:(part + 1) * SP], start=True, stop=True).then_inc(s_filled, 1)

                def v_piece(i, par, k):
                    n = i * 2 + par + 1
                    if k == 0:
                        pe.wait_ge(ct_kept, n * 3 + 3)
                        pe.wait_ge(k_split, n * 3 + 3)
                        wait_for(pe, m_laid, n)
                    else:
                        pe.wait_ge(v_kept, n * 3 + k)
                        wait_for(pe, an_ready if k == 1 else att_kept, n - 1)
                    for c in range(4):
                        mm = pe.matmul(PS[0:KC, WB, c * D:(c + 1) * D], cT[:, (4 * k + c) * KC:(4 * k + c + 1) * KC], wv[:], start=True, stop=True)
                    mm.then_inc(v_made, 1)

                def turn_output(n, v_before):
                    pe.wait_ge(o_kept, n + 1)
                    if v_before is not None:
                        pe.wait_ge(v_kept, v_before)
                    for k in range(4):
                        mm = pe.transpose(PS[0:TURN, WB, k * 128:(k + 1) * 128], Os[:, k * SQ:k * SQ + TURN], ident)
                    mm.then_inc(o_turned, 1)

                def turn_attention(n, v_before):
                    pe.wait_ge(an_ready, n + 1)
                    if v_before is not None:
                        pe.wait_ge(v_kept, v_before)
                    pe.transpose(PS[:, WB, 0:TURN], an[:].rearrange("p a b c d -> p (a b c d)"), ident[0:TURN, 0:TURN]).then_inc(an_turned, 1)

                def turn_context(i, par, k):
                    slot, pair, n = par, i + 1, i * 2 + par + 2
                    if k == 0:
                        pe.wait_ge(cx_in[slot], pair * 16 + 16)
                        wait_for(pe, v_kept, n * 3)
                    else:
                        pe.wait_ge(ct_kept, n * 3 + k)
                    for c in range(4):
                        mm = pe.transpose(PS[0:DC, WB, c * KC:(c + 1) * KC], cx[:, slot, 4 * k + c, :], ident[0:KC, 0:KC])
                    mm.then_inc(ct_turned, 1)

                def k_piece(i, par, k):
                    n = i * 2 + par + 2
                    if k == 0:
                        pe.wait_ge(ct_kept, n * 3 + 3)
                    else:
                        pe.wait_ge(k_split, n * 3 + k)
                    pe.matmul(PS[:, WB, 0:SP], wk[:], cT[:, k * SP:(k + 1) * SP], start=True, stop=True).then_inc(k_made, 1)

                def turn_maximum(i, par):
                    n = i * 2 + par + 1
                    pe.wait_ge(m_ready, n + 1)
                    if inside(i, par, 2):
                        pe.wait_ge(k_split, n * 3 + 6)
                    else:
                        pe.wait_ge(v_kept, n * 3 + 3)
                    pe.matmul(PS[96:112, WB, 0:TP], mneg[:], ident[0:TP, 0:TP], start=True, stop=True).then_inc(m_turned, 1)

                def body(i, par):
                    b = i * 2 + par
                    has_b, has_1, has_2, has_old = inside(i, par, 0), inside(i, par, 1), inside(i, par, 2), inside(i, par, -1)
                    if isinstance(b, int) and b == -2:
                        has_1 = False
                    for c in range(NC):
                        if has_b:
                            scores_t(i, par, c)
                        if has_1 and c in (0, 2, 4):
                            v_piece(i, par, c // 2)
                        for k in PIECES[c] if has_1 else ():
                            score_piece(i, par, k)
                        if has_b and has_old and c == 1:
                            turn_output(b - 1, b * 3 + 4 if has_1 else None)
                        if has_b and has_old and c == 3:
                            turn_attention(b - 1, b * 3 + 5 if has_1 else None)
                        if has_2 and 5 <= c < 8:
                            turn_context(i, par, c - 5)
                        if has_2 and 8 <= c < 11:
                            k_piece(i, par, c - 8)
                        if has_b and c > 0:
                            values(i, par, c - 1)
                    if has_b:
                        values(i, par, NC - 1)
                    if has_1:
                        turn_maximum(i, par)
                pe.wait_ge(ones_set, 7)
                over_pairs(pe, body, before=((-1, 0), (-1, 1)))
                turn_output(B - 1, None)
                turn_attention(B - 1, None)

            @block.scalar
            def _(act):
                def keep_output(n):
                    act.wait_ge(pv_done, n * NC + NC)
                    nc.scalar.copy(Os[:, 0:4 * SQ], PS[:, OB, 0:4 * SQ]).then_inc(o_kept, 1)

                def keep_attention(n):
                    act.wait_ge(an_turned, n + 1)
                    nc.scalar.copy(att[:].rearrange("p (b q) -> p b q", b=B)[:, bass.ds(n, 1), :],
                                   PS[:, WB, 0:SQ].unsqueeze(1)).then_inc(att_kept, 1)

                def body(i, par):
                    b = i * 2 + par
                    has_b, has_1, has_2, has_old = inside(i, par, 0), inside(i, par, 1), inside(i, par, 2), inside(i, par, -1)
                    if isinstance(b, int) and b == -2:
                        has_1 = False
                    if has_b and has_old:
                        keep_output(b - 1)
                    for c in range(NC):
                        if has_b:
                            act.wait_ge(st_done, b * NC + c + 1)
                            wait_for(act, pv_done, b * NC + c - 2)
                            nc.scalar.activation(Pb[:, c % 3].rearrange("p (h k) -> p h k", h=2),
                                                 PS[0:KC, 2 * (c % 2):2 * (c % 2) + 2, 0:HALF], ACT.Exp, scale=SCALE0).then_inc(exp_done, 1)
                        if has_1 and c in (0, 2, 4):
                            k, slot = c // 2, (par + 1) % 2
                            act.wait_ge(v_made, b * 3 + 3 + k + 1)
                            wait_for(act, pv_done, b * NC)
                            nc.scalar.copy(Vst[:, slot, 4 * k:4 * k + 4, :, 0:16],
                                           PS[0:KC, WB, :].rearrange("p (c a d) -> p c a d", c=4, a=PAIRS)).then_inc(v_kept, 1)
                        if has_b and has_old and c == 3:
                            keep_attention(b - 1)
                        if has_2 and 5 <= c < 8:
                            k = c - 5
                            act.wait_ge(ct_turned, b * 3 + 6 + k + 1)
                            nc.scalar.copy(cT[0:DC, k * SP:(k + 1) * SP], PS[0:DC, WB, 0:SP]).then_inc(ct_kept, 1)
                        if has_2 and 8 <= c < 11:
                            k = c - 8
                            act.wait_ge(k_made, b * 3 + 6 + k + 1)
                            if k == 0:
                                slot, pair = (par + 1) % 2, i + (par + 1) // 2
                                wait_for(act, kst_in[slot], pair * PER_KST + PER_KST if has_1 else 0)
                            nc.scalar.copy(KH[:, 0, k * SP:(k + 1) * SP], PS[:, WB, 0:SP]).then_inc(k_high, 1)
                act.wait_ge(ones_set, 7)
                over_pairs(act, body, before=((-1, 0), (-1, 1)))
                keep_output(B - 1)
                keep_attention(B - 1)

            @block.vector
            def _(dve):
                nc.vector.memset(Vst[:], 0.0).then_inc(ones_set, 1)
                dve.wait_ge(ones_set, 1)
                for slot in range(2):
                    nc.vector.memset(Vst[:, slot, :, :, 16:17], 1.0).then_inc(ones_set, 1)
                nc.vector.memset(Kst[96:112], 1.0).then_inc(ones_set, 1)
                nc.vector.memset(cT[DC:DC + 1, :], 1.0).then_inc(ones_set, 1)
                nc.vector.memset(Os[:, 4 * SQ:], 0.0).then_inc(ones_set, 1)
                nc.vector.memset(an[:], 0.0).then_inc(ones_set, 1)
                dve.wait_ge(ones_set, 7)

                def reduce_piece(i, par, k):
                    n = i * 2 + par + 1
                    dve.wait_ge(s_filled, n * 24 + k + 1)
                    if k == 0:
                        wait_for(dve, m_link, n * 2)
                    nc.vector.tensor_reduce(m24[:, k // NSP, k % NSP:k % NSP + 1], PS[0:TP, 6 + k % 2, 0:SP], AX.X, ALU.max).then_inc(s_reduced, 1)

                def normalise(n):
                    dve.wait_ge(o_turned, n + 1)
                    w = PS[0:SQ, WB, :].rearrange("p (k t c) -> p k t c", k=4, t=4)
                    nc.vector.reciprocal(rs[:].unsqueeze(3), w[:, :, :, 16:17]).then_inc(r_ready, 1)
                    dve.wait_ge(r_ready, n + 1)
                    wait_for(dve, an_turned, n)
                    for j in range(2):
                        a = nc.vector.tensor_tensor(an[0:SQ, :, :, j, :], w[:, j::2, :, j * DH0:(j + 1) * DH0],
                                                    spread(rs[:, j::2, :], 3, DH0), ALU.mult)
                    a.then_inc(an_ready, 1)

                def body(i, par):
                    b = i * 2 + par
                    has_b, has_1, has_2, has_old = inside(i, par, 0), inside(i, par, 1), inside(i, par, 2), inside(i, par, -1)
                    if isinstance(b, int) and b == -2:
                        has_1 = False
                    for c in range(NC):
                        for k in PIECES[c] if has_1 else ():
                            reduce_piece(i, par, k)
                        if has_b and has_old and c == 1:
                            normalise(b - 1)
                        if has_2 and 8 <= c < 11:
                            k = c - 8
                            dve.wait_ge(k_high, b * 3 + 6 + k + 1)
                            nc.vector.tensor_tensor(KH[:, 1, k * SP:(k + 1) * SP], PS[:, WB, 0:SP],
                                                    KH[:, 0, k * SP:(k + 1) * SP], ALU.subtract).then_inc(k_split, 1)
                    if has_1:
                        n, slot = b + 1, (par + 1) % 2
                        dve.wait_ge(s_reduced, n * 24 + 24)
                        nc.vector.tensor_reduce(mtop[:], m24[:], AX.X, ALU.max).then_inc(m_link, 1)
                        dve.wait_ge(m_link, n * 2 + 1)
                        nc.vector.tensor_copy(mhigh[:], mtop[:]).then_inc(m_link, 1)
                        dve.wait_ge(m_link, n * 2 + 2)
                        wait_for(dve, m_turned, n)
                        nc.vector.tensor_scalar(mneg[:, 0:PAIRS], mhigh[:], -1.0, None, ALU.mult)
                        nc.vector.tensor_tensor(mneg[:, PAIRS:], mhigh[:], mtop[:], ALU.subtract).then_inc(m_ready, 1)
                        dve.wait_ge(m_turned, n + 1)
                        nc.vector.tensor_tensor(Qst[96:112, slot].rearrange("p g (j q) -> p (g j) q", j=2),
                                                spread(PS[96:112, WB, 0:TP], 1, PAIRS),
                                                spread(tab[96:112, C_MM0:C_MM1], 2, TP), ALU.mult).then_inc(m_laid, 1)
                over_pairs(dve, body, before=((-1, 0), (-1, 1)))
                normalise(B - 1)
        cross.close()

        late = ExitStack()
        QK = late.enter_context(nc.sbuf_tensor("QK", [DC, 2, B, H, SQ], F16))
        ffn = ExitStack()
        h1 = sb_in(ffn, "h1", [128, 4, TOK])
        h2 = sb_in(ffn, "h2", [128, 4, TOK])
        Hn = sb_in(ffn, "Hn", [TP, NT, D])
        c_proj, c_link, c_var, c_root, c_x, c_turned, c_kept = (
            sem("c_proj"), sem("c_link"), sem("c_var"), sem("c_root"), sem("c_x"), sem("c_turned"), sem("c_kept"))
        f1, f1_kept, f2, f2_kept, f3, d_var, d_root, e_var, e_root, e_x, e_turned, e_kept = (
            sem(n) for n in ("f1", "f1_kept", "f2", "f2_kept", "f3", "d_var", "d_root", "e_var", "e_root", "e_x", "e_turned", "e_kept"))
        g_made, g_high, g_low = sem("g_made"), sem("g_high"), sem("g_low")
        with nc.Block() as block:
            @block.tensor
            def _(pe):
                project_tiles(pe, att, wco[:], c_proj)
                pe.wait_ge(c_x, 1)
                turn_tiles(pe, X, c_turned, 0)
                pe.wait_ge(c_kept, 1)
                for m in range(4):
                    for half in range(2):
                        mm = pe.matmul(PS[:, 2 * m + half, 0:HALF], w1s[:, m * 128:(m + 1) * 128],
                                       T128[:, half * HALF:(half + 1) * HALF], start=True, stop=True)
                    mm.then_inc(f1, 1)
                pe.wait_ge(f1_kept, 4)
                for m in range(4):
                    for half in range(2):
                        for k in range(4):
                            mm = pe.matmul(PS[:, 2 * m + half, 0:HALF], w2s[:, k, m * 128:(m + 1) * 128],
                                           h1[:, k, half * HALF:(half + 1) * HALF], start=(k == 0), stop=(k == 3))
                    mm.then_inc(f2, 1)
                pe.wait_ge(f2_kept, 4)
                for t in range(NT):
                    for k in range(4):
                        mm = pe.matmul(PS[0:TP, t // 4, (t % 4) * D:(t % 4 + 1) * D], h2[:, k, t * TP:(t + 1) * TP],
                                       w3s[:, k, :], start=(k == 0), stop=(k == 3))
                mm.then_inc(f3, 1)
                pe.wait_ge(e_x, 1)
                turn_tiles(pe, Hn, e_turned, 0)
                pe.wait_ge(e_kept, 1)
                for h in range(H):
                    for half in range(2):
                        n = 2 * h + half
                        wait_for(pe, g_low, n - 7)
                        pe.matmul(PS[0:DC, n % 8, 0:HALF], Wqk[:, h, :], T128[:, half * HALF:(half + 1) * HALF],
                                  start=True, stop=True).then_inc(g_made, 1)

            @block.scalar
            def _(act):
                norm_root(act, c_var, c_root)
                for hidden, bias, made, kept in ((h1, b1s, f1, f1_kept), (h2, b2s, f2, f2_kept)):
                    for m in range(4):
                        act.wait_ge(made, m + 1)
                        nc.scalar.activation(hidden[:, m, :].rearrange("p (h c) -> p h c", h=2), PS[:, 2 * m:2 * m + 2, 0:HALF],
                                             ACT.Relu, bias=bias[:, m:m + 1]).then_inc(kept, 1)
                norm_root(act, d_var, d_root)
                norm_root(act, e_var, e_root)
                for n in range(2 * H):
                    act.wait_ge(g_made, n + 1)
                    nc.scalar.copy(QK[:, 0, 8 * (n % 2):8 * (n % 2) + 8, n // 2, :],
                                   PS[0:DC, n % 8, 0:HALF].rearrange("p (b q) -> p b q", b=8)).then_inc(g_high, 1)

            @block.vector
            def _(dve):
                dve.wait_ge(c_proj, 1)
                n = add_residual(dve, 0, R_CO, c_link)
                n = norm_vector(dve, n, X[:], X[:], R_G, R_B, c_link, c_var, c_root)
                nc.vector.tensor_copy(stat[:, 0, :], stat[:, 3, :]).then_inc(c_x, 1)
                dve.wait_ge(c_turned, 1)
                nc.vector.tensor_copy(T128[:].rearrange("p (h c) -> p h c", h=2), PS[:, 0:2, 0:HALF]).then_inc(c_kept, 1)
                dve.wait_ge(f3, 1)
                n = add_residual(dve, n, R_B3, c_link)
                n = norm_vector(dve, n, X[:], X[:], R_G, R_B, c_link, d_var, d_root)
                n = norm_vector(dve, n, X[:], Hn[:], R_GA, R_BE, c_link, e_var, e_root)
                nc.vector.tensor_copy(stat[:, 0, :], stat[:, 3, :]).then_inc(e_x, 1)
                dve.wait_ge(e_turned, 1)
                nc.vector.tensor_copy(T128[:].rearrange("p (h c) -> p h c", h=2), PS[:, 0:2, 0:HALF]).then_inc(e_kept, 1)
                for n in range(2 * H):
                    dve.wait_ge(g_high, n + 1)
                    at = slice(8 * (n % 2), 8 * (n % 2) + 8)
                    nc.vector.tensor_tensor(QK[:, 1, at, n // 2, :], PS[0:DC, n % 8, 0:HALF].rearrange("p (b q) -> p b q", b=8),
                                            QK[:, 0, at, n // 2, :], ALU.subtract).then_inc(g_low, 1)
        ffn.close()

        NP = 4
        LAG = 2
        MR = 2 * QT1
        d_cx = sb_in(late, "d_cx", [KC, 2, NC, DC])
        cNh = sb_in(late, "cNh", [KC, 2, NC, DC + 1], F16)
        cNl = sb_in(late, "cNl", [KC, 2, NC, DC], F16)
        cTh = sb_in(late, "cTh", [DC + MR, 2, SK], F16)
        cTl = sb_in(late, "cTl", [DC, 2, SK], F16)
        Qh = sb_in(late, "Qh", [DC + MR, 2, NQ], F16)
        Ql = sb_in(late, "Ql", [DC, 2, NQ], F16)
        P1 = sb_in(late, "P1", [KC, NP, NQ])
        Pl = sb_in(late, "Pl", [KC, NP, NQ], F16)
        m21 = sb_in(late, "m21", [128, QT1, NSP])
        mt1 = sb_in(late, "mt1", [128, QT1])
        mh1 = sb_in(late, "mh1", [128, QT1], F16)
        mn1 = sb_in(late, "mn1", [128, MR])
        r7 = sb_in(late, "r7", [128, 8])
        On = sb_in(late, "On", [128, QT1, DC])
        OT = sb_in(late, "OT", [DC, H, 2, SQ])
        Y = sb_in(late, "Y", [TP, D])
        Z = sb_in(late, "Z", [TP, D])
        O1, W1, S1 = 4, 6, 7
        n_cx = [sem("n_cx0"), sem("n_cx1")]
        n_q = [sem("n_q0"), sem("n_q1")]
        n_ones, n_cn, n_cnl, n_turned, n_cth, n_ctl = (sem(n) for n in ("n_ones", "n_cn", "n_cnl", "n_turned", "n_cth", "n_ctl"))
        n_fill, n_red, n_mlink, n_mready, n_mturned, n_mlaid = (sem(n) for n in ("n_fill", "n_red", "n_mlink", "n_mready", "n_mturned", "n_mlaid"))
        n_st, n_exp, n_low_d, n_low_p, n_pv = (sem(n) for n in ("n_st", "n_exp", "n_low_d", "n_low_p", "n_pv"))
        n_r, n_on, n_oturned, n_ot, n_proj, n_y, n_z, n_out = (sem(n) for n in ("n_r", "n_on", "n_oturned", "n_ot", "n_proj", "n_y", "n_z", "n_out"))
        out_tiles = out.rearrange("b q d -> (b q) d").rearrange("(t p) d -> t p d", p=TP)
        low_on_dve = [c % 3 == 2 for c in range(NC)]
        DV = sum(low_on_dve)

        with nc.Block() as block:
            @block.sync
            def _(sp):
                def load(i, par, ahead):
                    slot, n = (par + ahead) % 2, i * 2 + par + ahead
                    wait_for(sp, n_st, (n - 1) * NC)
                    sp.dma_start(d_cx[:, slot], ctx_768[n].rearrange("(p c) d -> p c d", c=NC)).then_inc(n_cx[slot], 16)
                    at = bass.ds(n, 1)
                    sp.dma_start(Qh[0:DC, slot].rearrange("p (h q) -> p h q", h=H).unsqueeze(1), QK[:, 0, at]).then_inc(n_q[slot], 16)
                    sp.dma_start(Ql[:, slot].rearrange("p (h q) -> p h q", h=H).unsqueeze(1), QK[:, 1, at]).then_inc(n_q[slot], 16)

                def body(i, par):
                    if inside(i, par, 1):
                        load(i, par, 1)
                    if par == 0 and not (isinstance(i, int) and i <= 0):
                        store(i - 1)

                def store(t):
                    sp.wait_ge(n_z, t + 1)
                    sp.dma_start(out_tiles[t], Z[:]).then_inc(n_out, 16)
                over_pairs(sp, body, before=((-1, 1),))
                store(NT - 1)
                sp.wait_ge(n_out, 16 * NT)

            @block.gpsimd
            def _(pool):
                def body(i, par):
                    b = i * 2 + par
                    if inside(i, par, 1):
                        slot, n = (par + 1) % 2, b + 1
                        pool.wait_ge(n_cn, n + 1)
                        nc.gpsimd.tensor_tensor(cNl[:, slot], d_cx[:, slot], cNh[:, slot, :, 0:DC], ALU.subtract).then_inc(n_cnl, 1)
                    if not inside(i, par, 0):
                        return
                    k = 0
                    for c in range(NC):
                        if low_on_dve[c]:
                            continue
                        k += 1
                        pool.wait_ge(n_exp, b * NC + c + 1)
                        high = P1[:, c % NP].bitcast(BF16)[:, 1::2]
                        nc.gpsimd.tensor_tensor(Pl[:, c % NP], P1[:, c % NP], high, ALU.subtract).then_inc(n_low_p, 1)
                over_pairs(pool, body, before=((-1, 1),))

            @block.tensor
            def _(pe):
                def scores_t(i, par, c):
                    n = i * 2 + par
                    if c == 0:
                        pe.wait_ge(n_mlaid, n + 1)
                    wait_for(pe, n_exp, n * NC + c - 1)
                    at = slice(c * KC, (c + 1) * KC)
                    for half in range(2):
                        o = PS[0:KC, 2 * (c % 2) + half, 0:HALF]
                        cols = slice(half * HALF, (half + 1) * HALF)
                        pe.matmul(o, cTh[:, par, at], Qh[:, par, cols], start=True, stop=False)
                        pe.matmul(o, cTh[0:DC, par, at], Ql[:, par, cols], start=False, stop=False)
                        mm = pe.matmul(o, cTl[:, par, at], Qh[0:DC, par, cols], start=False, stop=True)
                    mm.then_inc(n_st, 1)

                def values(i, par, c, tiles):
                    n = i * 2 + par
                    if tiles[0] == 0:
                        if low_on_dve[c]:
                            pe.wait_ge(n_low_d, n * DV + sum(low_on_dve[:c + 1]))
                        else:
                            pe.wait_ge(n_low_p, n * (NC - DV) + c + 1 - sum(low_on_dve[:c + 1]))
                        if c == 0:
                            pe.wait_ge(n_cnl, n + 1)
                            wait_for(pe, n_on, n)
                    for t in tiles:
                        o = PS[:, O1 + t // 4, (t % 4) * ON:(t % 4) * ON + DC + 1]
                        cols = slice(t * 128, (t + 1) * 128)
                        high = P1[:, c % NP].bitcast(BF16)[:, 1::2][:, cols]
                        pe.matmul(o, high, cNh[:, par, c, :], start=(c == 0 and t % 4 == 0), stop=False, skip_group_check=True)
                        pe.matmul(o[:, 0:DC], high, cNl[:, par, c, :], start=False, stop=False, skip_group_check=True)
                        mm = pe.matmul(o, Pl[:, c % NP, cols], cNh[:, par, c, :], start=False, stop=(c == NC - 1), skip_group_check=True)
                    if tiles[-1] == QT1 - 1:
                        mm.then_inc(n_pv, 1)

                def score_piece(i, par, k):
                    slot, n = (par + 1) % 2, i * 2 + par + 1
                    if k == 0:
                        pe.wait_ge(n_q[slot], (i + (par + 1) // 2) * 32 + 32)
                        pe.wait_ge(n_cth, n * 3 + 3)
                    wait_for(pe, n_red, n * 21 + k)
                    t, part = k // NSP, k % NSP
                    pe.matmul(PS[:, S1, 0:SP], Qh[0:DC, slot, t * 128:(t + 1) * 128], cTh[0:DC, slot, part * SP:(part + 1) * SP],
                              start=True, stop=True).then_inc(n_fill, 1)

                def turn_context(i, par, k):
                    slot, pair, n = (par + 1) % 2, i + (par + 1) // 2, i * 2 + par + 1
                    if k == 0:
                        pe.wait_ge(n_cx[slot], pair * 16 + 16)
                        wait_for(pe, n_mlaid, n)
                        wait_for(pe, n_ot, (n - 1) * 2)
                        if par == 0 and inside(i, par, -1) and inside(i, par, 0):
                            pe.wait_ge(n_y, i)
                    else:
                        pe.wait_ge(n_ctl, n * 3 + k)
                    for c in range(4):
                        mm = pe.transpose(PS[0:DC, W1, c * KC:(c + 1) * KC], d_cx[:, slot, 4 * k + c, :], ident[0:KC, 0:KC])
                    mm.then_inc(n_turned, 1)

                def turn_output(n, k):
                    pe.wait_ge(n_on, n + 1)
                    if k == 0:
                        if not (isinstance(n, int) and n == B - 1):
                            pe.wait_ge(n_mlaid, n + 2)
                    else:
                        pe.wait_ge(n_ot, n * 2 + 1)
                    for t in range(4 * k, min(4 * k + 4, QT1)):
                        mm = pe.transpose(PS[0:DC, W1, (t % 4) * 128:(t % 4 + 1) * 128], On[:, t, :], ident)
                    mm.then_inc(n_oturned, 1)

                def project(t):
                    pe.wait_ge(n_ot, t * 4 + 4)
                    for h in range(H):
                        mm = pe.matmul(PS[0:TP, W1, 0:D], OT[:, h].rearrange("p j q -> p (j q)"), Wvo[:, h, :], start=(h == 0), stop=(h == H - 1))
                    mm.then_inc(n_proj, 1)

                def turn_maximum(i, par):
                    n = i * 2 + par + 1
                    pe.wait_ge(n_mready, n + 1)
                    pe.wait_ge(n_ctl, n * 3 + 3)
                    pe.matmul(PS[96:96 + MR, W1, 0:128], mn1[:], ident, start=True, stop=True).then_inc(n_mturned, 1)

                def body(i, par):
                    b = i * 2 + par
                    has_b, has_1, has_old = inside(i, par, 0), inside(i, par, 1), inside(i, par, -1)
                    pieces = list(range(21)) if has_1 else []
                    for c in range(NC + LAG):
                        if has_b and c < NC:
                            scores_t(i, par, c)
                        if has_b and has_old and c in (0, 1):
                            turn_output(b - 1, c)
                        if has_b and has_old and par == 0 and c == 2:
                            project(i - 1)
                        if has_1 and 3 <= c < 6:
                            turn_context(i, par, c - 3)
                        for tiles in ((0, 1), (2, 3), (4, 5, 6)):
                            if has_b and c >= LAG:
                                values(i, par, c - LAG, tiles)
                            if c >= 6 and pieces:
                                score_piece(i, par, pieces.pop(0))
                    if has_1:
                        turn_maximum(i, par)
                pe.wait_ge(n_ones, 2)
                over_pairs(pe, body, before=((-1, 1),))
                turn_output(B - 1, 0)
                turn_output(B - 1, 1)
                project(NT - 1)

            @block.scalar
            def _(act):
                def body(i, par):
                    b = i * 2 + par
                    has_b, has_1, has_old = inside(i, par, 0), inside(i, par, 1), inside(i, par, -1)
                    slot = (par + 1) % 2
                    for c in range(NC):
                        if has_b:
                            act.wait_ge(n_st, b * NC + c + 1)
                            wait_for(act, n_pv, b * NC + c - NP + 1)
                            nc.scalar.activation(P1[:, c % NP].rearrange("p (h k) -> p h k", h=2),
                                                 PS[0:KC, 2 * (c % 2):2 * (c % 2) + 2, 0:HALF], ACT.Exp).then_inc(n_exp, 1)
                        if has_1 and c == 0:
                            act.wait_ge(n_cx[slot], (i + (par + 1) // 2) * 16 + 16)
                            wait_for(act, n_pv, b * NC)
                            nc.scalar.copy(cNh[:, slot, :, 0:DC], d_cx[:, slot]).then_inc(n_cn, 1)
                        if has_b and has_old and c in (0, 1):
                            keep_old(i, par, c)
                        if has_1 and 3 <= c < 6:
                            k = c - 3
                            act.wait_ge(n_turned, (b + 1) * 3 + k + 1)
                            nc.scalar.copy(cTh[0:DC, slot, k * SP:(k + 1) * SP], PS[0:DC, W1, 0:SP]).then_inc(n_cth, 1)

                def keep_old(i, par, k):
                    n = i * 2 + par - 1
                    old = (par + 1) % 2
                    act.wait_ge(n_oturned, n * 2 + k + 1)
                    if old == 0 and k == 0:
                        wait_for(act, n_proj, i)
                    cut, rest = divmod(4 * 128, SQ)
                    if k == 0:
                        nc.scalar.copy(OT[:, 0:cut, old, :], PS[0:DC, W1, 0:cut * SQ].rearrange("p (h q) -> p h q", q=SQ))
                        nc.scalar.copy(OT[:, cut, old, 0:rest], PS[0:DC, W1, cut * SQ:512]).then_inc(n_ot, 1)
                    else:
                        nc.scalar.copy(OT[:, cut, old, rest:SQ], PS[0:DC, W1, 0:SQ - rest])
                        nc.scalar.copy(OT[:, cut + 1:H, old, :], PS[0:DC, W1, SQ - rest:NQ - 512].rearrange("p (h q) -> p h q", q=SQ)).then_inc(n_ot, 1)
                act.wait_ge(n_ones, 2)
                over_pairs(act, body, before=((-1, 1),))
                keep_old(NT, 0, 0)
                keep_old(NT, 0, 1)

            @block.vector
            def _(dve):
                nc.vector.memset(cNh[:], 1.0).then_inc(n_ones, 1)
                nc.vector.memset(cTh[96:96 + MR], 1.0).then_inc(n_ones, 1)

                def finish_batch(n):
                    dve.wait_ge(n_pv, n * NC + NC)
                    o = [PS[:, O1, 0:4 * ON].rearrange("p (t c) -> p t c", t=4), PS[:, O1 + 1, 0:3 * ON].rearrange("p (t c) -> p t c", t=3)]
                    for k in range(2):
                        nc.vector.reciprocal(r7[:, 4 * k:4 * k + 4 - k].unsqueeze(2), o[k][:, :, DC:DC + 1]).then_inc(n_r, 1)
                    dve.wait_ge(n_r, n * 2 + 2)
                    wait_for(dve, n_oturned, n * 2)
                    for k in range(2):
                        m = nc.vector.scalar_tensor_tensor(out=On[:, 4 * k:4 * k + 4 - k, :], in0=o[k][:, :, 0:DC], scalar=SCALE1,
                                                           in1=spread(r7[:, 4 * k:4 * k + 4 - k], 2, DC), op0=ALU.mult, op1=ALU.mult)
                    m.then_inc(n_on, 1)

                def finish_tile(t):
                    dve.wait_ge(n_proj, t + 1)
                    nc.vector.tensor_tensor(Y[:], PS[0:TP, W1, 0:D], rows[:, R_BO, :], ALU.add).then_inc(n_y, 1)
                    dve.wait_ge(n_y, t + 1)
                    wait_for(dve, n_out, t * 16)
                    nc.vector.tensor_tensor(Z[:].unsqueeze(1), Y[:].unsqueeze(1), X[:, bass.ds(t, 1), :], ALU.add).then_inc(n_z, 1)

                def body(i, par):
                    b = i * 2 + par
                    has_b, has_1, has_old = inside(i, par, 0), inside(i, par, 1), inside(i, par, -1)
                    slot = (par + 1) % 2
                    pieces = list(range(21)) if has_1 else []
                    if has_b and has_old:
                        finish_batch(b - 1)
                    for c in range(NC + LAG):
                        if has_b and c < NC and low_on_dve[c]:
                            dve.wait_ge(n_exp, b * NC + c + 1)
                            high = P1[:, c % NP].bitcast(BF16)[:, 1::2]
                            nc.vector.tensor_tensor(Pl[:, c % NP], P1[:, c % NP], high, ALU.subtract).then_inc(n_low_d, 1)
                        if has_b and has_old and par == 0 and c == 2:
                            finish_tile(i - 1)
                        if has_1 and 3 <= c < 6:
                            k = c - 3
                            dve.wait_ge(n_cth, (b + 1) * 3 + k + 1)
                            nc.vector.tensor_tensor(cTl[:, slot, k * SP:(k + 1) * SP], PS[0:DC, W1, 0:SP],
                                                    cTh[0:DC, slot, k * SP:(k + 1) * SP], ALU.subtract).then_inc(n_ctl, 1)
                        for _ in range(3):
                            if c >= 6 and pieces:
                                k = pieces.pop(0)
                                dve.wait_ge(n_fill, (b + 1) * 21 + k + 1)
                                if k == 0:
                                    wait_for(dve, n_mlink, (b + 1) * 3)
                                nc.vector.tensor_reduce(m21[:, k // NSP, k % NSP:k % NSP + 1], PS[:, S1, 0:SP], AX.X, ALU.max).then_inc(n_red, 1)
                    if has_1:
                        n = b + 1
                        dve.wait_ge(n_red, n * 21 + 21)
                        nc.vector.tensor_reduce(mt1[:], m21[:], AX.X, ALU.max).then_inc(n_mlink, 1)
                        dve.wait_ge(n_mlink, n * 3 + 1)
                        nc.vector.tensor_scalar(mt1[:], mt1[:], -LIFT, None, ALU.add).then_inc(n_mlink, 1)
                        dve.wait_ge(n_mlink, n * 3 + 2)
                        nc.vector.tensor_copy(mh1[:], mt1[:]).then_inc(n_mlink, 1)
                        dve.wait_ge(n_mlink, n * 3 + 3)
                        wait_for(dve, n_mturned, n)
                        nc.vector.tensor_scalar(mn1[:, 0:QT1], mh1[:], -1.0, None, ALU.mult)
                        nc.vector.tensor_tensor(mn1[:, QT1:], mh1[:], mt1[:], ALU.subtract).then_inc(n_mready, 1)
                        dve.wait_ge(n_mturned, n + 1)
                        nc.vector.tensor_tensor(Qh[96:96 + MR, slot].rearrange("p (t q) -> p t q", t=QT1),
                                                spread(PS[96:96 + MR, W1, 0:128], 1, QT1),
                                                spread(tab[96:96 + MR, C_MM1:C_M16], 2, 128), ALU.mult).then_inc(n_mlaid, 1)
                over_pairs(dve, body, before=((-1, 1),))
                finish_batch(B - 1)
                finish_tile(NT - 1)
        late.close()


_INS = ['x', 'ctx_768', 'L0_xattn_w_qkv', 'L0_xattn_b_qkv', 'L0_xattn_w_so', 'L0_xattn_b_so', 'L0_xattn_w_q',
        'L0_xattn_b_q', 'L0_xattn_w_k', 'L0_xattn_b_k', 'L0_xattn_w_v', 'L0_xattn_b_v', 'L0_xattn_w_co',
        'L0_xattn_b_co', 'L0_xattn_w1', 'L0_xattn_b1', 'L0_xattn_w2', 'L0_xattn_b2', 'L0_xattn_w3', 'L0_xattn_b3',
        'L0_xattn_ln_g', 'L0_xattn_ln_b', 'L1_xattn_Wq', 'L1_xattn_Wk', 'L1_xattn_Wv', 'L1_xattn_Wo', 'L1_xattn_bo',
        'L1_xattn_gamma', 'L1_xattn_beta']


def kernel(**inputs):
    import concourse.bacc as bacc
    from concourse.bass_utils import run_bass_kernel_spmd

    nc = bacc.Bacc("TRN2", target_bir_lowering=False, num_devices=1)
    arrays = {"shape_table": shape_table()}
    args = [nc.dram_tensor("shape_table", arrays["shape_table"].shape, F32, kind="ExternalInput").ap()]
    for name in _INS:
        a = np.ascontiguousarray(inputs[name])
        arrays[f"in_{name}"] = a
        args.append(nc.dram_tensor(f"in_{name}", a.shape, mybir.dt.from_np(a.dtype), kind="ExternalInput").ap())
    args.append(nc.dram_tensor("out_0", (B, SQ, D), F32, kind="ExternalOutput").ap())
    program(nc, *args)
    r = run_bass_kernel_spmd(nc, [arrays], core_ids=[0])
    return r.results[0]["out_0"]
```

```python
from contextlib import ExitStack

import numpy as np

import concourse.bass as bass
from concourse import mybir
from concourse.alu_op_type import AluOpType as ALU

ACT = mybir.ActivationFunctionType
AX = mybir.AxisListType
F32 = mybir.dt.float32
F16 = mybir.dt.float16
BF16 = mybir.dt.bfloat16

B, SQ, D = 16, 56, 128
SK, DC = 1500, 96
H = 16
DH0, DH1 = 8, 64
FF = 512
EPS = 1e-5
TOK = B * SQ
TP = 2 * SQ
NT = B // 2
HALF = TOK // 2
NQ = H * SQ
KC = 125
NC = SK // KC
SP = 500
NSP = SK // SP
G = 4
GH = H // G
PAIRS = H // 2
SCALE0 = DH0 ** -0.5
SCALE1 = DH1 ** -0.5
QT1 = NQ // 128
ON = 100
LIFT = 10 * float(np.log(2.0))

C_ID, C_M4, C_MM0, C_MM1, C_M16, C_MV, C_END = 0, 128, 132, 140, 147, 163, 165


def shape_table():
    t = np.zeros((128, C_END), np.float32)
    r = np.arange(128)[:, None]
    t[:, C_ID:C_M4] = np.eye(128)
    t[:, C_M4:C_MM0] = (r % 32) // DH0 == np.arange(GH)
    t[:, C_MM0:C_MM1] = (r >= 96) * (r < 112) * ((r - 96) % PAIRS == np.arange(PAIRS))
    t[:, C_MM1:C_M16] = (r >= 96) * (r < 110) * ((r - 96) % QT1 == np.arange(QT1))
    t[:, C_M16:C_MV] = r // DH0 == np.arange(H)
    t[:, C_MV:C_END] = r // SQ == np.arange(2)
    return t


def wait_for(eng, sem, count):
    if isinstance(count, int) and count <= 0:
        return
    eng.wait_ge(sem, count)


def spread(ap, dim, n):
    shape = list(ap.shape)
    return ap.unsqueeze(dim).broadcast_to(shape[:dim] + [n] + shape[dim:])


def over_pairs(eng, body, before=(), last=1):
    for i, par in before:
        body(i, par)
    for par in (0, 1):
        body(0, par)
    with eng.Fori(1, NT - last) as i:
        body(i, 0)
        body(i, 1)
    for i in range(NT - last, NT):
        body(i, 0)
        body(i, 1)


def inside(i, par, ahead):
    return not isinstance(i, int) or 0 <= 2 * i + par + ahead < B


def program(nc, table, x, ctx_768, w_qkv, b_qkv, w_so, b_so, w_q, b_q, w_k, b_k, w_v, b_v, w_co, b_co,
            w1, b1, w2, b2, w3, b3, ln_g, ln_b, Wq, Wk, Wv, Wo, bo, gamma, beta, out):
    with ExitStack() as ctx:
        def sb_in(stack, name, shape, dt=F32):
            return stack.enter_context(nc.sbuf_tensor(name, shape, dt))

        def sb(name, shape, dt=F32):
            return sb_in(ctx, name, shape, dt)

        def sem(name):
            return ctx.enter_context(nc.semaphore(name))

        PS = ctx.enter_context(nc.psum_tensor("PS", [128, 8, 512], F32))

        tab = sb("tab", [128, C_END])
        ident = tab[:, C_ID:C_M4]
        X = sb("X", [TP, NT, D])
        T128 = sb("T128", [128, TOK])
        att = sb("att", [128, TOK])
        work = sb("work", [TP, NT, D])
        squares = sb("squares", [TP, NT, D])
        stat = sb("stat", [TP, 4, NT])
        rows = sb("rows", [TP, 9, D])
        R_BV, R_SO, R_CO, R_B3, R_G, R_B, R_BO, R_GA, R_BE = range(9)
        wso = sb("wso", [D, D])
        wco = sb("wco", [D, D])
        w1s = sb("w1s", [D, FF])
        w2s = sb("w2s", [128, 4, FF])
        w3s = sb("w3s", [128, 4, D])
        b1s = sb("b1s", [128, 4])
        b2s = sb("b2s", [128, 4])
        wq3 = sb("wq3", [D, G, 3, 32])
        bq3 = sb("bq3", [96, G])
        wk = sb("wk", [DC + 1, D])
        wv = sb("wv", [DC + 1, D])
        Q16 = sb("Q16", [96, G, TOK], F16)
        Wqk = sb("Wqk", [D, H, DC])
        Wvo = sb("Wvo", [DC, H, D])

        first = ctx.enter_context(ExitStack())
        wqkv = sb_in(first, "wqkv", [D, 3 * D])
        bqk = sb_in(first, "bqk", [D, 2])
        QT = sb_in(first, "QT", [D, B, SQ])
        KT = sb_in(first, "KT", [D, B, SQ])
        setup = ExitStack()
        Wqs = sb_in(setup, "Wqs", [D, H * DH1])
        Wks = sb_in(setup, "Wks", [DC, H * DH1])
        Wvs = sb_in(setup, "Wvs", [DC, H * DH1])
        Wos = sb_in(setup, "Wos", [128, H // 2, D])
        WqT = sb_in(setup, "WqT", [128, 8, D])
        WkT = sb_in(setup, "WkT", [128, 8, DC])
        WvT = sb_in(setup, "WvT", [128, 8, DC])

        table_in, x_in, qkv_in, small_in = sem("table_in"), sem("x_in"), sem("qkv_in"), sem("small_in")
        wq1_in, wk1_in, wv1_in, wo1_in, later_in = (
            sem("wq1_in"), sem("wk1_in"), sem("wv1_in"), sem("wo1_in"), sem("later_in"))
        x_turned, x_kept = sem("x_turned"), sem("x_kept")
        wqT_made, wkT_made, wvT_made = sem("wqT_made"), sem("wkT_made"), sem("wvT_made")
        wqT_kept, wkT_kept, wvT_kept = sem("wqT_kept"), sem("wkT_kept"), sem("wvT_kept")
        qk_made, qk_kept = sem("qk_made"), sem("qk_kept")
        wqk_made, wvo_made, wqk_kept, wvo_kept = sem("wqk_made"), sem("wvo_made"), sem("wqk_kept"), sem("wvo_kept")

        with nc.Block() as block:
            @block.sync
            def _(sp):
                sp.dma_start(tab[:], table).then_inc(table_in, 16)
                sp.dma_start(X[:], x.rearrange("b q d -> (b q) d").rearrange("(t p) d -> p t d", p=TP)).then_inc(x_in, 16)
                sp.dma_start(wqkv[:], w_qkv).then_inc(qkv_in, 16)
                sp.dma_start(bqk[:], b_qkv[0:2 * D].rearrange("(s p) -> p s", p=D), allow_slow_non_contiguous=True).then_inc(qkv_in, 16)
                sp.dma_start(Wqs[:], Wq).then_inc(wq1_in, 16)
                sp.dma_start(Wks[:], Wk).then_inc(wk1_in, 16)
                sp.dma_start(Wvs[:], Wv).then_inc(wv1_in, 16)
                sp.dma_start(Wos[:], Wo.rearrange("(t p) d -> p t d", p=128)).then_inc(wo1_in, 16)

            @block.gpsimd
            def _(pool):
                for k, row in enumerate((b_qkv[2 * D:3 * D], b_so, b_co, b3, ln_g, ln_b, bo, gamma, beta)):
                    pool.dma_start(rows[:, k, :], row.partition_broadcast(TP)).then_inc(small_in, 16)
                pool.dma_start(wso[:], w_so).then_inc(small_in, 16)
                pool.dma_start(wco[:], w_co).then_inc(small_in, 16)
                for rep in range(3):
                    pool.dma_start(wq3[:, :, rep, :], w_q.rearrange("d (g r) -> d g r", g=G)).then_inc(small_in, 16)
                    pool.dma_start(bq3[32 * rep:32 * rep + 32, :], b_q.rearrange("(g r) -> r g", g=G), allow_slow_non_contiguous=True).then_inc(small_in, 16)
                pool.dma_start(wk[0:DC, :], w_k).then_inc(small_in, 16)
                pool.dma_start(wk[DC:DC + 1, :], b_k.unsqueeze(0)).then_inc(small_in, 16)
                pool.dma_start(wv[0:DC, :], w_v).then_inc(small_in, 16)
                pool.dma_start(wv[DC:DC + 1, :], b_v.unsqueeze(0)).then_inc(small_in, 16)
                pool.dma_start(w1s[:], w1).then_inc(later_in, 16)
                pool.dma_start(w2s[:], w2.rearrange("(k p) n -> p k n", p=128)).then_inc(later_in, 16)
                pool.dma_start(w3s[:], w3.rearrange("(k p) n -> p k n", p=128)).then_inc(later_in, 16)
                pool.dma_start(b1s[:], b1.rearrange("(k p) -> p k", p=128), allow_slow_non_contiguous=True).then_inc(later_in, 16)
                pool.dma_start(b2s[:], b2.rearrange("(k p) -> p k", p=128), allow_slow_non_contiguous=True).then_inc(later_in, 16)
                pool.wait_ge(small_in, 16 * 21)
                pool.wait_ge(later_in, 16 * 5)

            @block.tensor
            def _(pe):
                pe.wait_ge(table_in, 16)
                pe.wait_ge(x_in, 16)
                for t in range(NT):
                    mm = pe.transpose(PS[:, t // 4, (t % 4) * TP:(t % 4 + 1) * TP], X[:, t, :], ident[0:TP, 0:TP])
                mm.then_inc(x_turned, 1)
                for src, arrived, made, bank, rows_in in (
                        (Wqs, wq1_in, wqT_made, 2, D), (Wks, wk1_in, wkT_made, 4, DC), (Wvs, wv1_in, wvT_made, 6, DC)):
                    pe.wait_ge(arrived, 16)
                    for t in range(8):
                        mm = pe.transpose(PS[:, bank + t // 4, (t % 4) * rows_in:(t % 4 + 1) * rows_in],
                                          src[:, t * 128:(t + 1) * 128], ident[0:rows_in, 0:rows_in])
                    mm.then_inc(made, 1)
                pe.wait_ge(qkv_in, 32)
                pe.wait_ge(x_kept, 1)
                pe.wait_ge(wqT_kept, 1)
                for s in range(2):
                    for half in range(2):
                        mm = pe.matmul(PS[:, 2 * s + half, 0:HALF], wqkv[:, s * D:(s + 1) * D],
                                       T128[:, half * HALF:(half + 1) * HALF], start=True, stop=True)
                mm.then_inc(qk_made, 1)
                pe.wait_ge(wkT_kept, 1)
                pe.wait_ge(wvT_kept, 1)
                for h in range(H):
                    at = 64 * (h % 2)
                    mm = pe.matmul(PS[:, 4 + 2 * (h % 2) + h // 8, (h // 2 % 4) * DC:(h // 2 % 4 + 1) * DC], WqT[at:at + 64, h // 2, :],
                                   WkT[at:at + 64, h // 2, :], start=True, stop=True)
                mm.then_inc(wqk_made, 1)
                pe.wait_ge(wo1_in, 16)
                pe.wait_ge(qk_kept, 2)
                for h in range(H):
                    at = 64 * (h % 2)
                    mm = pe.matmul(PS[0:DC, 2 * (h % 2) + h // 8, (h // 2 % 4) * D:(h // 2 % 4 + 1) * D], WvT[at:at + 64, h // 2, :],
                                   Wos[at:at + 64, h // 2, :], start=True, stop=True)
                mm.then_inc(wvo_made, 1)

            @block.vector
            def _(dve):
                dve.wait_ge(x_turned, 1)
                nc.vector.tensor_copy(T128[:].rearrange("p (h c) -> p h c", h=2), PS[:, 0:2, 0:HALF]).then_inc(x_kept, 1)
                dve.wait_ge(wkT_made, 1)
                nc.vector.tensor_copy(WkT[:].rearrange("p (a b) c -> p a (b c)", a=2), PS[:, 4:6, 0:4 * DC]).then_inc(wkT_kept, 1)
                dve.wait_ge(qk_made, 1)
                nc.vector.tensor_scalar(QT[:].rearrange("p (h b) q -> p h (b q)", h=2), PS[:, 0:2, 0:HALF],
                                        bqk[:, 0:1], None, ALU.add).then_inc(qk_kept, 1)
                nc.vector.tensor_scalar(KT[:].rearrange("p (h b) q -> p h (b q)", h=2), PS[:, 2:4, 0:HALF],
                                        bqk[:, 1:2], None, ALU.add).then_inc(qk_kept, 1)
                dve.wait_ge(wvo_made, 1)
                for j in range(2):
                    nc.vector.tensor_copy(Wvo[:].rearrange("p (a b j) c -> p j a b c", a=2, j=2)[:, j],
                                          PS[0:DC, 2 * j:2 * j + 2, 0:4 * D].rearrange("p a (b c) -> p a b c", b=4)).then_inc(wvo_kept, 1)

            @block.scalar
            def _(act):
                act.wait_ge(wqT_made, 1)
                nc.scalar.copy(WqT[:].rearrange("p (a b) c -> p a (b c)", a=2), PS[:, 2:4, 0:4 * D]).then_inc(wqT_kept, 1)
                act.wait_ge(wvT_made, 1)
                nc.scalar.copy(WvT[:].rearrange("p (a b) c -> p a (b c)", a=2), PS[:, 6:8, 0:4 * DC]).then_inc(wvT_kept, 1)
                act.wait_ge(wqk_made, 1)
                for j in range(2):
                    nc.scalar.copy(Wqk[:].rearrange("p (a b j) c -> p j a b c", a=2, j=2)[:, j],
                                   PS[:, 4 + 2 * j:6 + 2 * j, 0:4 * DC].rearrange("p a (b c) -> p a b c", b=4)).then_inc(wqk_kept, 1)
        setup.close()

        selfa = ExitStack()
        Kbd = sb_in(selfa, "Kbd", [D, 2, H, SQ])
        Qp = sb_in(selfa, "Qp", [D, 2, 2, 64])
        Xd = sb_in(selfa, "Xd", [D, 2, 2, 2, SQ])
        V2 = sb_in(selfa, "V2", [TP, 2, 2, D])
        Vbd = sb_in(selfa, "Vbd", [TP, 2, 2, PAIRS, 18])
        top = sb_in(selfa, "top", [128, 2, H])
        Sm = sb_in(selfa, "Sm", [128, 2, NQ])
        Pe = sb_in(selfa, "Pe", [128, 2, NQ])
        PT = sb_in(selfa, "PT", [TP, PAIRS, 128])
        rsum = sb_in(selfa, "rsum", [128, PAIRS, 2])
        ao = sb_in(selfa, "ao", [128, PAIRS, 2, DH0])
        s_zero, s_ones = sem("s_zero"), sem("s_ones")
        s_staged, s_kbd, s_vbd = sem("s_staged"), sem("s_kbd"), sem("s_vbd")
        s_v, s_vkept, s_scores = sem("s_v"), sem("s_vkept"), sem("s_scores")
        s_top, s_sm, s_exp, s_turned, s_pt = sem("s_top"), sem("s_sm"), sem("s_exp"), sem("s_turned"), sem("s_pt")
        s_pv, s_rsum, s_ao, s_aoT, s_att = sem("s_pv"), sem("s_rsum"), sem("s_ao"), sem("s_aoT"), sem("s_att")
        SB = 6

        def over_tiles(eng, body):
            body(0, 0, True, False)
            body(1, 1, True, True)
            with eng.Fori(1, NT // 2) as i:
                body(i * 2, 0, True, True)
                body(i * 2 + 1, 1, True, True)
            body(NT, 0, False, True)

        with nc.Block() as block:
            @block.gpsimd
            def _(pool):
                def step(t, slot, early, late):
                    if not early:
                        return
                    wait_for(pool, s_scores, t)
                    for j in range(2):
                        k = nc.gpsimd.tensor_tensor(Kbd[:, j], KT[:, bass.ds(t * 2 + j, 1), :].broadcast_to([D, H, SQ]),
                                                    spread(tab[:, C_M16:C_MV], 2, SQ), ALU.mult)
                    k.then_inc(s_kbd, 1)
                    pool.wait_ge(s_vkept, t + 1)
                    wait_for(pool, s_pv, t - 1)
                    for j in range(2):
                        v = nc.gpsimd.tensor_tensor(
                            Vbd[:, slot, j, :, 0:16].rearrange("p a (b c) -> p a b c", b=2),
                            V2[:, slot, j].rearrange("p (a b c) -> p a b c", a=PAIRS, b=2),
                            spread(spread(tab[0:TP, C_MV:C_END], 1, PAIRS), 3, DH0), ALU.mult)
                    v.then_inc(s_vbd, 1)
                over_tiles(pool, step)

            @block.scalar
            def _(act):
                act.wait_ge(s_zero, 1)

                def step(t, slot, early, late):
                    if early:
                        wait_for(act, s_scores, t - 1)
                        nc.scalar.copy(Qp[:, slot, :, 0:SQ], QT[:, bass.ds(t * 2, 2), :]).then_inc(s_staged, 1)
                        nc.scalar.copy(Xd[:, slot], spread(T128[:].rearrange("p (b q) -> p b q", b=B)[:, bass.ds(t * 2, 2), :], 2, 2)).then_inc(s_staged, 1)
                    if late:
                        act.wait_ge(s_turned, t)
                        nc.scalar.copy(PT[:].rearrange("p (a b) c -> p a (b c)", a=2), PS[0:TP, 4:6, :]).then_inc(s_pt, 1)
                    if early:
                        act.wait_ge(s_sm, t + 1)
                        nc.scalar.activation(Pe[:, slot], Sm[:, slot], ACT.Exp, scale=SCALE0).then_inc(s_exp, 1)
                    if late:
                        act.wait_ge(s_aoT, t)
                        nc.scalar.copy(att[:].rearrange("p (b q) -> p b q", b=B)[:, bass.ds(t * 2 - 2, 2), :],
                                       PS[:, SB, 256:384].rearrange("p (j q) -> p j q", j=2)[:, :, 0:SQ]).then_inc(s_att, 1)
                over_tiles(act, step)

            @block.tensor
            def _(pe):
                def step(t, slot, early, late):
                    if late:
                        other = 1 - slot
                        pe.wait_ge(s_exp, t)
                        wait_for(pe, s_pt, t - 1)
                        for p in range(PAIRS):
                            mm = pe.transpose(PS[0:TP, 4 + p // 4, (p % 4) * 128:(p % 4 + 1) * 128],
                                              Pe[:, other, p * TP:(p + 1) * TP], ident)
                        mm.then_inc(s_turned, 1)
                    if early:
                        pe.wait_ge(s_staged, t * 2 + 2)
                        wait_for(pe, s_vkept, t)
                        for j in range(2):
                            mm = pe.matmul(PS[0:TP, 7, j * D:(j + 1) * D], Xd[:, slot, j], wqkv[:, 2 * D:3 * D], start=True, stop=True)
                        mm.then_inc(s_v, 1)
                        pe.wait_ge(s_kbd, t + 1)
                        wait_for(pe, s_sm, t - 1)
                        for j in range(2):
                            for half in range(2):
                                mm = pe.matmul(PS[64 * j:64 * j + 64, 2 * slot + half, 0:HALF], Qp[:, slot, j, :],
                                               Kbd[:, j, 8 * half:8 * half + 8, :], start=True, stop=True)
                        mm.then_inc(s_scores, 1)
                    if late:
                        pe.wait_ge(s_pt, t)
                        pe.wait_ge(s_vbd, t)
                        wait_for(pe, s_att, t - 1)
                        for p in range(PAIRS):
                            for j in range(2):
                                mm = pe.matmul(PS[64 * j:64 * j + 64, SB, p * 18:(p + 1) * 18], PT[:, p, 64 * j:64 * j + 64],
                                               Vbd[:, other, j, p, :], start=True, stop=True)
                        mm.then_inc(s_pv, 1)
                        pe.wait_ge(s_ao, t)
                        pe.transpose(PS[:, SB, 256:384], ao[:].rearrange("p a b c -> p (a b c)"), ident).then_inc(s_aoT, 1)
                over_tiles(pe, step)

            @block.vector
            def _(dve):
                nc.vector.memset(Qp[:], 0.0).then_inc(s_zero, 1)
                for slot in range(2):
                    for j in range(2):
                        nc.vector.tensor_copy(Vbd[:, slot, j, :, 16:18], spread(tab[0:TP, C_MV:C_END], 1, PAIRS)).then_inc(s_ones, 1)

                def step(t, slot, early, late):
                    if early:
                        dve.wait_ge(s_v, t + 1)
                        wait_for(dve, s_vbd, t - 1)
                        nc.vector.tensor_tensor(V2[:, slot], PS[0:TP, 7, 0:2 * D].rearrange("p (j d) -> p j d", j=2),
                                                spread(rows[:, R_BV, :], 1, 2), ALU.add).then_inc(s_vkept, 1)
                        dve.wait_ge(s_scores, t + 1)
                        sc = PS[:, 2 * slot:2 * slot + 2, 0:HALF].rearrange("p a (h k) -> p a h k", h=8)
                        nc.vector.tensor_reduce(top[:, slot].rearrange("p (a h) -> p a h", a=2), sc, AX.X, ALU.max).then_inc(s_top, 1)
                        dve.wait_ge(s_top, t + 1)
                        wait_for(dve, s_exp, t - 1)
                        nc.vector.tensor_tensor(Sm[:, slot].rearrange("p (a h k) -> p a h k", a=2, h=8), sc,
                                                spread(top[:, slot].rearrange("p (a h) -> p a h", a=2), 3, SQ),
                                                ALU.subtract).then_inc(s_sm, 1)
                    if late:
                        dve.wait_ge(s_pv, t)
                        o = PS[:, SB, 0:PAIRS * 18].rearrange("p (a c) -> p a c", a=PAIRS)
                        nc.vector.reciprocal(rsum[:], o[:, :, 16:18]).then_inc(s_rsum, 1)
                        dve.wait_ge(s_rsum, t)
                        wait_for(dve, s_aoT, t - 1)
                        nc.vector.tensor_tensor(ao[:], o[:, :, 0:16].rearrange("p a (b c) -> p a b c", b=2),
                                                spread(rsum[:], 3, DH0), ALU.mult).then_inc(s_ao, 1)
                over_tiles(dve, step)
        selfa.close()
        first.close()

        def project_tiles(pe, src, w, done):
            for t in range(NT):
                mm = pe.matmul(PS[0:TP, t // 4, (t % 4) * D:(t % 4 + 1) * D], src[:, t * TP:(t + 1) * TP], w, start=True, stop=True)
            mm.then_inc(done, 1)

        def turn_tiles(pe, src, done, bank):
            for t in range(NT):
                mm = pe.transpose(PS[:, bank + t // 4, (t % 4) * TP:(t % 4 + 1) * TP], src[:, t, :], ident[0:TP, 0:TP])
            mm.then_inc(done, 1)

        def row(k):
            return spread(rows[:, k, :], 1, NT)

        def norm_vector(dve, tag, src, dst, gain, shift, link, var_ready, root_ready):
            nc.vector.tensor_reduce(stat[:, 0, :], src, AX.X, ALU.add).then_inc(link, 1)
            dve.wait_ge(link, tag + 1)
            nc.vector.tensor_scalar(stat[:, 0, :], stat[:, 0, :], -1.0 / D, None, ALU.mult).then_inc(link, 1)
            dve.wait_ge(link, tag + 2)
            nc.vector.tensor_tensor(work[:], src, spread(stat[:, 0, :], 2, D), ALU.add).then_inc(link, 1)
            dve.wait_ge(link, tag + 3)
            nc.vector.tensor_tensor(squares[:], work[:], work[:], ALU.mult).then_inc(link, 1)
            dve.wait_ge(link, tag + 4)
            nc.vector.tensor_reduce(stat[:, 1, :], squares[:], AX.X, ALU.add).then_inc(link, 1)
            dve.wait_ge(link, tag + 5)
            nc.vector.tensor_scalar(stat[:, 1, :], stat[:, 1, :], 1.0 / D, EPS, ALU.mult, ALU.add).then_inc(var_ready, 1)
            dve.wait_ge(root_ready, 1)
            nc.vector.reciprocal(stat[:, 3, :], stat[:, 2, :]).then_inc(link, 1)
            dve.wait_ge(link, tag + 6)
            nc.vector.tensor_tensor(work[:], work[:], spread(stat[:, 3, :], 2, D), ALU.mult).then_inc(link, 1)
            dve.wait_ge(link, tag + 7)
            nc.vector.tensor_tensor(work[:], work[:], row(gain), ALU.mult).then_inc(link, 1)
            dve.wait_ge(link, tag + 8)
            nc.vector.tensor_tensor(dst, work[:], row(shift), ALU.add).then_inc(link, 1)
            dve.wait_ge(link, tag + 9)
            return tag + 9

        def norm_root(act, var_ready, root_ready):
            act.wait_ge(var_ready, 1)
            nc.scalar.activation(stat[:, 2, :], stat[:, 1, :], ACT.Sqrt).then_inc(root_ready, 1)

        def add_residual(dve, tag, bias, link):
            nc.vector.tensor_tensor(work[:].rearrange("p (a t) d -> p a t d", a=2),
                                    PS[0:TP, 0:2, :].rearrange("p a (t d) -> p a t d", d=D),
                                    row(bias).rearrange("p (a t) d -> p a t d", a=2), ALU.add).then_inc(link, 1)
            dve.wait_ge(link, tag + 1)
            nc.vector.tensor_tensor(X[:], work[:], X[:], ALU.add).then_inc(link, 1)
            dve.wait_ge(link, tag + 2)
            return tag + 2

        a_proj, a_link, a_var, a_root = sem("a_proj"), sem("a_link"), sem("a_var"), sem("a_root")
        a_x, a_turned, a_kept, a_q, a_qkept, a_qlink = sem("a_x"), sem("a_turned"), sem("a_kept"), sem("a_q"), sem("a_qkept"), sem("a_qlink")
        qst = ExitStack()
        Q32 = sb_in(qst, "Q32", [96, G, TOK])
        with nc.Block() as block:
            @block.tensor
            def _(pe):
                project_tiles(pe, att, wso[:], a_proj)
                pe.wait_ge(a_x, 1)
                turn_tiles(pe, X, a_turned, 0)
                pe.wait_ge(a_kept, 1)
                for g in range(G):
                    for half in range(2):
                        mm = pe.matmul(PS[0:96, 2 * g + half, 0:HALF], wq3[:, g].rearrange("p a b -> p (a b)"),
                                       T128[:, half * HALF:(half + 1) * HALF], start=True, stop=True)
                    mm.then_inc(a_q, 1)

            @block.vector
            def _(dve):
                dve.wait_ge(a_proj, 1)
                n = add_residual(dve, 0, R_SO, a_link)
                n = norm_vector(dve, n, X[:], X[:], R_G, R_B, a_link, a_var, a_root)
                nc.vector.tensor_copy(stat[:, 0, :], stat[:, 3, :]).then_inc(a_x, 1)
                dve.wait_ge(a_turned, 1)
                nc.vector.tensor_copy(T128[:].rearrange("p (h c) -> p h c", h=2), PS[:, 0:2, 0:HALF]).then_inc(a_kept, 1)
                for g in range(G):
                    dve.wait_ge(a_qkept, g + 1)
                    nc.vector.tensor_copy(Q16[:, g, :], Q32[:, g, :]).then_inc(a_qlink, 1)
                    dve.wait_ge(a_qlink, 2 * g + 1)
                    nc.vector.tensor_tensor(Q16[64:96, g, :], Q32[64:96, g, :], Q16[64:96, g, :], ALU.subtract).then_inc(a_qlink, 1)

            @block.scalar
            def _(act):
                norm_root(act, a_var, a_root)
                for g in range(G):
                    act.wait_ge(a_q, g + 1)
                    nc.scalar.activation(Q32[:, g, :].rearrange("p (h c) -> p h c", h=2), PS[0:96, 2 * g:2 * g + 2, 0:HALF],
                                         ACT.Identity, bias=bq3[:, g:g + 1]).then_inc(a_qkept, 1)
        qst.close()

        cross = ExitStack()
        NPB = 4
        LAG0 = 2
        TURN = 72
        cx = sb_in(cross, "cx", [KC, 2, NC, DC])
        cT = sb_in(cross, "cT", [DC + 1, 2, SK])
        KH = sb_in(cross, "KH", [D, 2, SK], F16)
        Kst = sb_in(cross, "Kst", [112, 2, G, SK], F16)
        Qst = sb_in(cross, "Qst", [112, 2, G, GH * SQ], F16)
        Qmx = sb_in(cross, "Qmx", [96, 2, G, GH * SQ], F16)
        Vst = sb_in(cross, "Vst", [KC, 2, NC, PAIRS, 32])
        Pb = sb_in(cross, "Pb", [KC, NPB, NQ])
        m24 = sb_in(cross, "m24", [TP, PAIRS, NSP])
        mtop = sb_in(cross, "mtop", [TP, PAIRS])
        mhigh = sb_in(cross, "mhigh", [TP, PAIRS], F16)
        mneg = sb_in(cross, "mneg", [TP, 2 * PAIRS])
        Os = sb_in(cross, "Os", [128, 5 * SQ])
        rs = sb_in(cross, "rs", [SQ, 4, 4])
        an = sb_in(cross, "an", [TURN, 2, 4, 2, DH0])
        cx_in = [sem("cx_in0"), sem("cx_in1")]
        k_out, kst_in = sem("k_out"), [sem(f"kst_in{part}") for part in range(NSP)]
        k_halves = nc.dram_tensor("k_halves", (2, D, 2, SK), F16, kind="Internal").ap()
        ones_set = sem("ones_set")
        ct_turned, ct_kept = sem("ct_turned"), sem("ct_kept")
        k_made, k_high, k_split = sem("k_made"), sem("k_high"), sem("k_split")
        v_made, v_kept, q_laid, qmx_laid = sem("v_made"), sem("v_kept"), sem("q_laid"), sem("qmx_laid")
        s_filled, s_reduced = sem("s_filled"), sem("s_reduced")
        m_link, m_ready, m_turned, m_laid = sem("m_link"), sem("m_ready"), sem("m_turned"), sem("m_laid")
        st_done, exp_done, pv_done = sem("st_done"), sem("exp_done"), sem("pv_done")
        o_kept, o_turned, r_ready, an_ready, an_turned, att_kept = (
            sem("o_kept"), sem("o_turned"), sem("r_ready"), sem("an_ready"), sem("an_turned"), sem("att_kept"))
        OB, WB = 4, 5
        V_AT = {7: 0, 9: 1, 10: 2}
        PIECES = [(p, part) for part in range(NSP) for p in range(PAIRS)]
        BESIDE = [range(24 * min(c, 11) // 11, 24 * min(c + 1, 11) // 11) for c in range(NC + LAG0)]

        with nc.Block() as block:
            @block.sync
            def _(sp):
                def load_context(i, par, ahead):
                    slot, pair, n = (par + ahead) % 2, i + (par + ahead) // 2, i * 2 + par + ahead
                    wait_for(sp, ct_turned, (n - 1) * 3)
                    sp.dma_start(cx[:, slot], ctx_768[n].rearrange("(p c) d -> p c d", c=NC)).then_inc(cx_in[slot], 16)

                def lay_keys(i, par, ahead):
                    slot, n = (par + ahead) % 2, i * 2 + par + ahead

                    def lay(part):
                        cols = slice(part * SP, (part + 1) * SP)
                        for block_row, half in enumerate((0, 1, 0)):
                            sp.dma_start(Kst[32 * block_row:32 * block_row + 32, slot, :, cols],
                                         k_halves[slot, :, half, cols].rearrange("(g r) k -> r g k", g=G)).then_inc(kst_in[part], 16)
                    sp.wait_ge(k_split, n * 3 + 3)
                    sp.dma_start(k_halves[slot], KH[:]).then_inc(k_out, 16)
                    sp.wait_ge(k_out, n * 16 + 16)
                    lay(0)
                    for part in (1, 2):
                        wait_for(sp, st_done, (n - 2) * NC + (part + 1) * 4)
                        lay(part)

                def body(i, par):
                    if inside(i, par, 3):
                        load_context(i, par, 3)
                    if inside(i, par, 2):
                        lay_keys(i, par, 2)
                load_context(0, 0, 0)
                over_pairs(sp, body, before=((-1, 0), (-1, 1)), last=2)

            @block.gpsimd
            def _(pool):
                def body(i, par):
                    b = i * 2 + par
                    if inside(i, par, 2):
                        wait_for(pool, s_filled, (b + 1) * 24)
                    if inside(i, par, 1) and not (isinstance(b, int) and b == -2):
                        slot = (par + 1) % 2
                        pool.wait_ge(qmx_laid, b + 2)
                        wait_for(pool, st_done, b * NC)
                        for g in range(G):
                            q = nc.gpsimd.tensor_tensor(Qst[0:96, slot, g].rearrange("p (j q) -> p j q", j=GH),
                                                        Qmx[:, slot, g].rearrange("p (j q) -> p j q", j=GH),
                                                        spread(tab[0:96, C_M4:C_MM0], 2, SQ), ALU.mult)
                        q.then_inc(q_laid, 1)
                    if inside(i, par, 2):
                        for g in range(G):
                            q = nc.gpsimd.tensor_tensor(
                                Qmx[:, par, g].rearrange("p (j q) -> p j q", j=GH),
                                Q16[:, g, :].rearrange("p (b q) -> p b q", b=B)[:, bass.ds(b + 2, 1), :].broadcast_to([96, GH, SQ]),
                                spread(tab[0:96, C_M4:C_MM0], 2, SQ), ALU.mult)
                        q.then_inc(qmx_laid, 1)
                over_pairs(pool, body, before=((-1, 0), (-1, 1)))

            @block.tensor
            def _(pe):
                def scores_t(i, par, c):
                    n = i * 2 + par
                    if c == 0:
                        pe.wait_ge(q_laid, n + 1)
                        pe.wait_ge(m_laid, n + 1)
                    wait_for(pe, exp_done, n * NC + c - 1)
                    for g in range(G):
                        mm = pe.matmul(PS[0:KC, 2 * (c % 2) + g // 2, (g % 2) * 224:(g % 2 + 1) * 224],
                                       Kst[:, par, g, c * KC:(c + 1) * KC], Qst[:, par, g, :], start=True, stop=True)
                    mm.then_inc(st_done, 1)

                def values(i, par, c):
                    n = i * 2 + par
                    pe.wait_ge(exp_done, n * NC + c + 1)
                    if c == 0:
                        pe.wait_ge(v_kept, n * 3 + 3)
                        wait_for(pe, o_kept, n)
                    for p in range(PAIRS):
                        mm = pe.matmul(PS[32 * (p % 4):32 * (p % 4) + 32, OB, (p // 4) * TP:(p // 4 + 1) * TP],
                                       Vst[:, par, c, p, :], Pb[:, c % NPB, p * TP:(p + 1) * TP],
                                       start=(c == 0 and p < 4), stop=(c == NC - 1), skip_group_check=True)
                    mm.then_inc(pv_done, 1)

                def score_piece(i, par, k):
                    slot, n = (par + 1) % 2, i * 2 + par + 1
                    p, part = PIECES[k]
                    if k == 0:
                        pe.wait_ge(qmx_laid, n + 1)
                    if p == 0:
                        pe.wait_ge(kst_in[part], n * 48 + 48)
                    wait_for(pe, s_reduced, n * 24 + k - 1)
                    pe.matmul(PS[0:TP, 6 + k % 2, 0:SP], Qmx[:, slot, p // 2, (p % 2) * TP:(p % 2 + 1) * TP],
                              Kst[0:96, slot, p // 2, part * SP:(part + 1) * SP], start=True, stop=True).then_inc(s_filled, 1)

                def turn_context(i, par, k):
                    slot, pair, n = par, i + 1, i * 2 + par + 2
                    if k == 0:
                        pe.wait_ge(cx_in[slot], pair * 16 + 16)
                        wait_for(pe, k_split, n * 3)
                        wait_for(pe, m_laid, n - 1)
                    else:
                        pe.wait_ge(ct_kept, n * 3 + k)
                    for c in range(4):
                        mm = pe.transpose(PS[0:DC, WB, c * KC:(c + 1) * KC], cx[:, slot, 4 * k + c, :], ident[0:KC, 0:KC])
                    mm.then_inc(ct_turned, 1)

                def k_piece(i, par, k):
                    n = i * 2 + par + 2
                    if k == 0:
                        pe.wait_ge(ct_kept, n * 3 + 3)
                    else:
                        pe.wait_ge(k_split, n * 3 + k)
                    pe.matmul(PS[:, WB, 0:SP], wk[:], cT[:, par, k * SP:(k + 1) * SP], start=True, stop=True).then_inc(k_made, 1)

                def turn_output(n, k_before):
                    pe.wait_ge(o_kept, n + 1)
                    if k_before is not None:
                        pe.wait_ge(k_split, k_before)
                    for k in range(4):
                        mm = pe.transpose(PS[0:TURN, WB, k * 128:(k + 1) * 128], Os[:, k * SQ:k * SQ + TURN], ident)
                    mm.then_inc(o_turned, 1)

                def v_piece(i, par, k):
                    n = i * 2 + par + 1
                    if k == 0:
                        pe.wait_ge(ct_kept, n * 3 + 3)
                        if inside(i, par, 2):
                            pe.wait_ge(k_split, n * 3 + 6)
                        wait_for(pe, an_ready, n - 1)
                    else:
                        pe.wait_ge(v_kept, n * 3 + k)
                        wait_for(pe, att_kept, n - 1)
                    for c in range(4):
                        mm = pe.matmul(PS[0:KC, WB, c * D:(c + 1) * D], cT[:, (par + 1) % 2, (4 * k + c) * KC:(4 * k + c + 1) * KC], wv[:], start=True, stop=True)
                    mm.then_inc(v_made, 1)

                def turn_attention(n, v_before):
                    pe.wait_ge(an_ready, n + 1)
                    if v_before is not None:
                        pe.wait_ge(v_kept, v_before)
                    pe.transpose(PS[:, WB, 0:TURN], an[:].rearrange("p a b c d -> p (a b c d)"), ident[0:TURN, 0:TURN]).then_inc(an_turned, 1)

                def turn_maximum(i, par):
                    n = i * 2 + par + 1
                    pe.wait_ge(m_ready, n + 1)
                    pe.wait_ge(v_kept, n * 3 + 3)
                    pe.matmul(PS[96:112, WB, 0:TP], mneg[:], ident[0:TP, 0:TP], start=True, stop=True).then_inc(m_turned, 1)

                def body(i, par):
                    b = i * 2 + par
                    has_b, has_1, has_2, has_old = inside(i, par, 0), inside(i, par, 1), inside(i, par, 2), inside(i, par, -1)
                    if isinstance(b, int) and b == -2:
                        has_1 = False
                    for c in range(NC + LAG0):
                        pieces = list(BESIDE[c]) if has_1 else []
                        if has_b and c < NC:
                            scores_t(i, par, c)
                        for k in pieces[:1]:
                            score_piece(i, par, k)
                        if has_2 and c < 3:
                            turn_context(i, par, c)
                        if has_2 and 3 <= c < 6:
                            k_piece(i, par, c - 3)
                        if has_b and has_old and c == 6:
                            turn_output(b - 1, b * 3 + 9 if has_2 else None)
                        if has_1 and c in V_AT:
                            v_piece(i, par, V_AT[c])
                        if has_b and has_old and c == 8:
                            turn_attention(b - 1, b * 3 + 4 if has_1 else None)
                        for k in pieces[1:2]:
                            score_piece(i, par, k)
                        if has_b and c >= LAG0:
                            values(i, par, c - LAG0)
                        for k in pieces[2:]:
                            score_piece(i, par, k)
                        if has_1 and c == NC:
                            turn_maximum(i, par)
                pe.wait_ge(ones_set, 7)
                over_pairs(pe, body, before=((-1, 0), (-1, 1)))
                turn_output(B - 1, None)
                turn_attention(B - 1, None)

            @block.scalar
            def _(act):
                def keep_output(n):
                    act.wait_ge(pv_done, n * NC + NC)
                    nc.scalar.copy(Os[:, 0:4 * SQ], PS[:, OB, 0:4 * SQ]).then_inc(o_kept, 1)

                def keep_attention(n):
                    act.wait_ge(an_turned, n + 1)
                    nc.scalar.copy(att[:].rearrange("p (b q) -> p b q", b=B)[:, bass.ds(n, 1), :],
                                   PS[:, WB, 0:SQ].unsqueeze(1)).then_inc(att_kept, 1)

                def body(i, par):
                    b = i * 2 + par
                    has_b, has_1, has_2, has_old = inside(i, par, 0), inside(i, par, 1), inside(i, par, 2), inside(i, par, -1)
                    if isinstance(b, int) and b == -2:
                        has_1 = False
                    if has_b and has_old:
                        keep_output(b - 1)
                    for c in range(NC):
                        if has_b:
                            act.wait_ge(st_done, b * NC + c + 1)
                            wait_for(act, pv_done, b * NC + c - NPB + 1)
                            nc.scalar.activation(Pb[:, c % NPB].rearrange("p (h k) -> p h k", h=2),
                                                 PS[0:KC, 2 * (c % 2):2 * (c % 2) + 2, 0:HALF], ACT.Exp, scale=SCALE0).then_inc(exp_done, 1)
                        if has_2 and c < 3:
                            act.wait_ge(ct_turned, b * 3 + 6 + c + 1)
                            nc.scalar.copy(cT[0:DC, par, c * SP:(c + 1) * SP], PS[0:DC, WB, 0:SP]).then_inc(ct_kept, 1)
                        if has_2 and 3 <= c < 6:
                            k = c - 3
                            act.wait_ge(k_made, b * 3 + 6 + k + 1)
                            if k == 0:
                                wait_for(act, k_out, b * 16 + 32)
                            nc.scalar.copy(KH[:, 0, k * SP:(k + 1) * SP], PS[:, WB, 0:SP]).then_inc(k_high, 1)
                        if has_b and has_old and c == 8:
                            keep_attention(b - 1)
                        if has_1 and c in V_AT:
                            k, slot = V_AT[c], (par + 1) % 2
                            act.wait_ge(v_made, b * 3 + 3 + k + 1)
                            wait_for(act, pv_done, b * NC)
                            nc.scalar.copy(Vst[:, slot, 4 * k:4 * k + 4, :, 0:16],
                                           PS[0:KC, WB, :].rearrange("p (c a d) -> p c a d", c=4, a=PAIRS)).then_inc(v_kept, 1)
                act.wait_ge(ones_set, 7)
                over_pairs(act, body, before=((-1, 0), (-1, 1)))
                keep_output(B - 1)
                keep_attention(B - 1)

            @block.vector
            def _(dve):
                nc.vector.memset(Vst[:], 0.0).then_inc(ones_set, 1)
                dve.wait_ge(ones_set, 1)
                for slot in range(2):
                    nc.vector.memset(Vst[:, slot, :, :, 16:17], 1.0).then_inc(ones_set, 1)
                nc.vector.memset(Kst[96:112], 1.0).then_inc(ones_set, 1)
                nc.vector.memset(cT[DC:DC + 1], 1.0).then_inc(ones_set, 1)
                nc.vector.memset(Os[:, 4 * SQ:], 0.0).then_inc(ones_set, 1)
                nc.vector.memset(an[:], 0.0).then_inc(ones_set, 1)
                dve.wait_ge(ones_set, 7)

                def reduce_piece(i, par, k):
                    n = i * 2 + par + 1
                    dve.wait_ge(s_filled, n * 24 + k + 1)
                    if k == 0:
                        wait_for(dve, m_link, n * 2)
                    p, part = PIECES[k]
                    nc.vector.tensor_reduce(m24[:, p, part:part + 1], PS[0:TP, 6 + k % 2, 0:SP], AX.X, ALU.max).then_inc(s_reduced, 1)

                def normalise(n):
                    dve.wait_ge(o_turned, n + 1)
                    w = PS[0:SQ, WB, :].rearrange("p (k t c) -> p k t c", k=4, t=4)
                    nc.vector.reciprocal(rs[:].unsqueeze(3), w[:, :, :, 16:17]).then_inc(r_ready, 1)
                    dve.wait_ge(r_ready, n + 1)
                    wait_for(dve, an_turned, n)
                    for j in range(2):
                        a = nc.vector.tensor_tensor(an[0:SQ, :, :, j, :], w[:, j::2, :, j * DH0:(j + 1) * DH0],
                                                    spread(rs[:, j::2, :], 3, DH0), ALU.mult)
                    a.then_inc(an_ready, 1)

                def body(i, par):
                    b = i * 2 + par
                    has_b, has_1, has_2, has_old = inside(i, par, 0), inside(i, par, 1), inside(i, par, 2), inside(i, par, -1)
                    if isinstance(b, int) and b == -2:
                        has_1 = False
                    for c in range(NC):
                        for k in BESIDE[c] if has_1 else ():
                            reduce_piece(i, par, k)
                        if has_2 and 3 <= c < 6:
                            k = c - 3
                            dve.wait_ge(k_high, b * 3 + 6 + k + 1)
                            nc.vector.tensor_tensor(KH[:, 1, k * SP:(k + 1) * SP], PS[:, WB, 0:SP],
                                                    KH[:, 0, k * SP:(k + 1) * SP], ALU.subtract).then_inc(k_split, 1)
                        if has_b and has_old and c == 6:
                            normalise(b - 1)
                    if has_1:
                        n, slot = b + 1, (par + 1) % 2
                        dve.wait_ge(s_reduced, n * 24 + 24)
                        nc.vector.tensor_reduce(mtop[:], m24[:], AX.X, ALU.max).then_inc(m_link, 1)
                        dve.wait_ge(m_link, n * 2 + 1)
                        nc.vector.tensor_copy(mhigh[:], mtop[:]).then_inc(m_link, 1)
                        dve.wait_ge(m_link, n * 2 + 2)
                        wait_for(dve, m_turned, n)
                        nc.vector.tensor_scalar(mneg[:, 0:PAIRS], mhigh[:], -1.0, None, ALU.mult)
                        nc.vector.tensor_tensor(mneg[:, PAIRS:], mhigh[:], mtop[:], ALU.subtract).then_inc(m_ready, 1)
                        dve.wait_ge(m_turned, n + 1)
                        nc.vector.tensor_tensor(Qst[96:112, slot].rearrange("p g (j q) -> p (g j) q", j=2),
                                                spread(PS[96:112, WB, 0:TP], 1, PAIRS),
                                                spread(tab[96:112, C_MM0:C_MM1], 2, TP), ALU.mult).then_inc(m_laid, 1)
                over_pairs(dve, body, before=((-1, 0), (-1, 1)))
                normalise(B - 1)
        cross.close()

        late = ExitStack()
        QK = late.enter_context(nc.sbuf_tensor("QK", [DC, 2, B, H, SQ], F16))
        ffn = ExitStack()
        h1 = sb_in(ffn, "h1", [128, 4, TOK])
        h2 = sb_in(ffn, "h2", [128, 4, TOK])
        Hn = sb_in(ffn, "Hn", [TP, NT, D])
        c_proj, c_link, c_var, c_root, c_x, c_turned, c_kept = (
            sem("c_proj"), sem("c_link"), sem("c_var"), sem("c_root"), sem("c_x"), sem("c_turned"), sem("c_kept"))
        f1, f1_kept, f2, f2_kept, f3, d_var, d_root, e_var, e_root, e_x, e_turned, e_kept = (
            sem(n) for n in ("f1", "f1_kept", "f2", "f2_kept", "f3", "d_var", "d_root", "e_var", "e_root", "e_x", "e_turned", "e_kept"))
        g_made, g_high, g_low = sem("g_made"), sem("g_high"), sem("g_low")
        with nc.Block() as block:
            @block.tensor
            def _(pe):
                project_tiles(pe, att, wco[:], c_proj)
                pe.wait_ge(c_x, 1)
                turn_tiles(pe, X, c_turned, 0)
                pe.wait_ge(c_kept, 1)
                for m in range(4):
                    for half in range(2):
                        mm = pe.matmul(PS[:, 2 * m + half, 0:HALF], w1s[:, m * 128:(m + 1) * 128],
                                       T128[:, half * HALF:(half + 1) * HALF], start=True, stop=True)
                    mm.then_inc(f1, 1)
                pe.wait_ge(f1_kept, 4)
                for m in range(4):
                    for half in range(2):
                        for k in range(4):
                            mm = pe.matmul(PS[:, 2 * m + half, 0:HALF], w2s[:, k, m * 128:(m + 1) * 128],
                                           h1[:, k, half * HALF:(half + 1) * HALF], start=(k == 0), stop=(k == 3))
                    mm.then_inc(f2, 1)
                pe.wait_ge(f2_kept, 4)
                for t in range(NT):
                    for k in range(4):
                        mm = pe.matmul(PS[0:TP, t // 4, (t % 4) * D:(t % 4 + 1) * D], h2[:, k, t * TP:(t + 1) * TP],
                                       w3s[:, k, :], start=(k == 0), stop=(k == 3))
                mm.then_inc(f3, 1)
                pe.wait_ge(e_x, 1)
                turn_tiles(pe, Hn, e_turned, 0)
                pe.wait_ge(e_kept, 1)
                for h in range(H):
                    for half in range(2):
                        n = 2 * h + half
                        wait_for(pe, g_low, n - 7)
                        pe.matmul(PS[0:DC, n % 8, 0:HALF], Wqk[:, h, :], T128[:, half * HALF:(half + 1) * HALF],
                                  start=True, stop=True).then_inc(g_made, 1)

            @block.scalar
            def _(act):
                norm_root(act, c_var, c_root)
                for hidden, bias, made, kept in ((h1, b1s, f1, f1_kept), (h2, b2s, f2, f2_kept)):
                    for m in range(4):
                        act.wait_ge(made, m + 1)
                        nc.scalar.activation(hidden[:, m, :].rearrange("p (h c) -> p h c", h=2), PS[:, 2 * m:2 * m + 2, 0:HALF],
                                             ACT.Relu, bias=bias[:, m:m + 1]).then_inc(kept, 1)
                norm_root(act, d_var, d_root)
                norm_root(act, e_var, e_root)
                for n in range(2 * H):
                    act.wait_ge(g_made, n + 1)
                    nc.scalar.copy(QK[:, 0, 8 * (n % 2):8 * (n % 2) + 8, n // 2, :],
                                   PS[0:DC, n % 8, 0:HALF].rearrange("p (b q) -> p b q", b=8)).then_inc(g_high, 1)

            @block.vector
            def _(dve):
                dve.wait_ge(c_proj, 1)
                n = add_residual(dve, 0, R_CO, c_link)
                n = norm_vector(dve, n, X[:], X[:], R_G, R_B, c_link, c_var, c_root)
                nc.vector.tensor_copy(stat[:, 0, :], stat[:, 3, :]).then_inc(c_x, 1)
                dve.wait_ge(c_turned, 1)
                nc.vector.tensor_copy(T128[:].rearrange("p (h c) -> p h c", h=2), PS[:, 0:2, 0:HALF]).then_inc(c_kept, 1)
                dve.wait_ge(f3, 1)
                n = add_residual(dve, n, R_B3, c_link)
                n = norm_vector(dve, n, X[:], X[:], R_G, R_B, c_link, d_var, d_root)
                n = norm_vector(dve, n, X[:], Hn[:], R_GA, R_BE, c_link, e_var, e_root)
                nc.vector.tensor_copy(stat[:, 0, :], stat[:, 3, :]).then_inc(e_x, 1)
                dve.wait_ge(e_turned, 1)
                nc.vector.tensor_copy(T128[:].rearrange("p (h c) -> p h c", h=2), PS[:, 0:2, 0:HALF]).then_inc(e_kept, 1)
                for n in range(2 * H):
                    dve.wait_ge(g_high, n + 1)
                    at = slice(8 * (n % 2), 8 * (n % 2) + 8)
                    nc.vector.tensor_tensor(QK[:, 1, at, n // 2, :], PS[0:DC, n % 8, 0:HALF].rearrange("p (b q) -> p b q", b=8),
                                            QK[:, 0, at, n // 2, :], ALU.subtract).then_inc(g_low, 1)
        ffn.close()

        NP = 4
        LAG = 2
        MR = 2 * QT1
        d_cx = sb_in(late, "d_cx", [KC, 2, NC, DC])
        cNh = sb_in(late, "cNh", [KC, 2, NC, DC + 1], F16)
        cNl = sb_in(late, "cNl", [KC, 2, NC, DC], F16)
        cTh = sb_in(late, "cTh", [DC + MR, 2, SK], F16)
        cTl = sb_in(late, "cTl", [DC, 2, SK], F16)
        Qh = sb_in(late, "Qh", [DC + MR, 2, NQ], F16)
        Ql = sb_in(late, "Ql", [DC, 2, NQ], F16)
        P1 = sb_in(late, "P1", [KC, NP, NQ])
        Pl = sb_in(late, "Pl", [KC, NP, NQ], F16)
        m21 = sb_in(late, "m21", [128, QT1, NSP])
        mt1 = sb_in(late, "mt1", [128, QT1])
        mh1 = sb_in(late, "mh1", [128, QT1], F16)
        mn1 = sb_in(late, "mn1", [128, MR])
        r7 = sb_in(late, "r7", [128, 8])
        On = sb_in(late, "On", [128, QT1, DC])
        OT = sb_in(late, "OT", [DC, H, 2, SQ])
        Y = sb_in(late, "Y", [TP, D])
        Z = sb_in(late, "Z", [TP, D])
        O1, W1, S1 = 4, 6, (3, 7)
        PIECES1 = [(t, part) for part in range(NSP) for t in range(QT1)]
        BESIDE1 = [range(min(max(2 * (c - 1), 0), 21), min(max(2 * c, 0), 21)) for c in range(NC + LAG)]
        n_cx = [sem("n_cx0"), sem("n_cx1")]
        n_q = [sem("n_q0"), sem("n_q1")]
        n_ones, n_cn, n_cnl, n_turned, n_cth, n_ctl = (sem(n) for n in ("n_ones", "n_cn", "n_cnl", "n_turned", "n_cth", "n_ctl"))
        n_fill, n_red, n_mlink, n_mready, n_mturned, n_mlaid = (sem(n) for n in ("n_fill", "n_red", "n_mlink", "n_mready", "n_mturned", "n_mlaid"))
        n_st, n_exp, n_low_d, n_low_p, n_pv = (sem(n) for n in ("n_st", "n_exp", "n_low_d", "n_low_p", "n_pv"))
        n_r, n_on, n_oturned, n_ot, n_proj, n_y, n_z, n_out = (sem(n) for n in ("n_r", "n_on", "n_oturned", "n_ot", "n_proj", "n_y", "n_z", "n_out"))
        out_tiles = out.rearrange("b q d -> (b q) d").rearrange("(t p) d -> t p d", p=TP)
        low_on_dve = [c % 3 == 2 for c in range(NC)]
        DV = sum(low_on_dve)

        with nc.Block() as block:
            @block.sync
            def _(sp):
                def load_queries(i, par):
                    slot, n = (par + 1) % 2, i * 2 + par + 1
                    wait_for(sp, n_st, (n - 1) * 2 * NC)
                    at = bass.ds(n, 1)
                    sp.dma_start(Qh[0:DC, slot].rearrange("p (h q) -> p h q", h=H).unsqueeze(1), QK[:, 0, at]).then_inc(n_q[slot], 16)
                    sp.dma_start(Ql[:, slot].rearrange("p (h q) -> p h q", h=H).unsqueeze(1), QK[:, 1, at]).then_inc(n_q[slot], 16)

                def load_context(i, par):
                    slot, n = par, i * 2 + par + 2
                    wait_for(sp, n_st, (n - 2) * 2 * NC + 2 * (LAG + 2))
                    sp.dma_start(d_cx[:, slot], ctx_768[n].rearrange("(p c) d -> p c d", c=NC)).then_inc(n_cx[slot], 16)

                def body(i, par):
                    if inside(i, par, 1):
                        load_queries(i, par)
                    if inside(i, par, 2):
                        load_context(i, par)
                    if par == 0 and not (isinstance(i, int) and i <= 0):
                        store(i - 1)

                def store(t):
                    sp.wait_ge(n_z, t + 1)
                    sp.dma_start(out_tiles[t], Z[:]).then_inc(n_out, 16)
                load_context(-1, 0)
                over_pairs(sp, body, before=((-1, 1),))
                store(NT - 1)
                sp.wait_ge(n_out, 16 * NT)

            @block.gpsimd
            def _(pool):
                def body(i, par):
                    b = i * 2 + par
                    for c in range(NC):
                        if inside(i, par, 0) and not low_on_dve[c]:
                            pool.wait_ge(n_exp, (b * NC + c) * 2 + 2)
                            high = P1[:, c % NP].bitcast(BF16)[:, 1::2]
                            nc.gpsimd.tensor_tensor(Pl[:, c % NP], P1[:, c % NP], high, ALU.subtract).then_inc(n_low_p, 1)
                        if inside(i, par, 1) and c == 4:
                            slot, n = (par + 1) % 2, b + 1
                            pool.wait_ge(n_cn, n + 1)
                            nc.gpsimd.tensor_tensor(cNl[:, slot], d_cx[:, slot], cNh[:, slot, :, 0:DC], ALU.subtract).then_inc(n_cnl, 1)
                over_pairs(pool, body, before=((-1, 1),))

            @block.tensor
            def _(pe):
                def scores_t(i, par, c, half):
                    n, u = i * 2 + par, 2 * c + half
                    if u == 0:
                        pe.wait_ge(n_mlaid, n + 1)
                    wait_for(pe, n_exp, n * 2 * NC + u - 2)
                    at, cols = slice(c * KC, (c + 1) * KC), slice(half * HALF, (half + 1) * HALF)
                    o = PS[0:KC, u % 3, 0:HALF]
                    pe.matmul(o, cTh[:, par, at], Qh[:, par, cols], start=True, stop=False)
                    pe.matmul(o, cTh[0:DC, par, at], Ql[:, par, cols], start=False, stop=False)
                    pe.matmul(o, cTl[:, par, at], Qh[0:DC, par, cols], start=False, stop=True).then_inc(n_st, 1)

                def values(i, par, c, tiles):
                    n = i * 2 + par
                    if tiles[0] == 0:
                        if low_on_dve[c]:
                            pe.wait_ge(n_low_d, n * DV + sum(low_on_dve[:c + 1]))
                        else:
                            pe.wait_ge(n_low_p, n * (NC - DV) + c + 1 - sum(low_on_dve[:c + 1]))
                        if c == 0:
                            pe.wait_ge(n_cnl, n + 1)
                            wait_for(pe, n_on, n)
                    for t in tiles:
                        o = PS[:, O1 + t // 4, (t % 4) * ON:(t % 4) * ON + DC + 1]
                        cols = slice(t * 128, (t + 1) * 128)
                        high = P1[:, c % NP].bitcast(BF16)[:, 1::2][:, cols]
                        pe.matmul(o, high, cNh[:, par, c, :], start=(c == 0 and t % 4 == 0), stop=False, skip_group_check=True)
                        pe.matmul(o[:, 0:DC], high, cNl[:, par, c, :], start=False, stop=False, skip_group_check=True)
                        mm = pe.matmul(o, Pl[:, c % NP, cols], cNh[:, par, c, :], start=False, stop=(c == NC - 1), skip_group_check=True)
                    if tiles[-1] == QT1 - 1:
                        mm.then_inc(n_pv, 1)

                def score_piece(i, par, k):
                    slot, n = (par + 1) % 2, i * 2 + par + 1
                    t, part = PIECES1[k]
                    if k == 0:
                        pe.wait_ge(n_q[slot], (i + (par + 1) // 2) * 32 + 32)
                    if t == 0:
                        pe.wait_ge(n_cth, n * 3 + part + 1)
                    wait_for(pe, n_red, n * 21 + max(k - 1, 0))
                    pe.matmul(PS[:, S1[k % 2], 0:SP], Qh[0:DC, slot, t * 128:(t + 1) * 128], cTh[0:DC, slot, part * SP:(part + 1) * SP],
                              start=True, stop=True).then_inc(n_fill, 1)

                def turn_context(i, par, k):
                    slot, pair, n = (par + 1) % 2, i + (par + 1) // 2, i * 2 + par + 1
                    if k == 0:
                        pe.wait_ge(n_cx[slot], pair * 16 + 16)
                        wait_for(pe, n_mlaid, n)
                    else:
                        pe.wait_ge(n_ctl, n * 3 + k)
                    for c in range(4):
                        mm = pe.transpose(PS[0:DC, W1, c * KC:(c + 1) * KC], d_cx[:, slot, 4 * k + c, :], ident[0:KC, 0:KC])
                    mm.then_inc(n_turned, 1)

                def turn_output(n, k, split):
                    pe.wait_ge(n_on, n + 1)
                    if k == 1:
                        pe.wait_ge(n_ot, n * 2 + 1)
                    elif split is not None:
                        pe.wait_ge(n_ctl, split)
                    for t in range(4 * k, min(4 * k + 4, QT1)):
                        mm = pe.transpose(PS[0:DC, W1, (t % 4) * 128:(t % 4 + 1) * 128], On[:, t, :], ident)
                    mm.then_inc(n_oturned, 1)

                def project(t):
                    pe.wait_ge(n_ot, t * 4 + 4)
                    for h in range(H):
                        mm = pe.matmul(PS[0:TP, W1, 0:D], OT[:, h].rearrange("p j q -> p (j q)"), Wvo[:, h, :], start=(h == 0), stop=(h == H - 1))
                    mm.then_inc(n_proj, 1)

                def turn_maximum(i, par):
                    n = i * 2 + par + 1
                    pe.wait_ge(n_mready, n + 1)
                    pe.wait_ge(n_ctl, n * 3 + 3)
                    if inside(i, par, 0) and inside(i, par, -1):
                        pe.wait_ge(n_ot, n * 2 - 2)
                        if par == 0:
                            pe.wait_ge(n_y, i)
                    pe.matmul(PS[96:96 + MR, W1, 0:128], mn1[:], ident, start=True, stop=True).then_inc(n_mturned, 1)

                def body(i, par):
                    b = i * 2 + par
                    has_b, has_1, has_old = inside(i, par, 0), inside(i, par, 1), inside(i, par, -1)
                    for c in range(NC + LAG):
                        pieces = list(BESIDE1[c]) if has_1 else []
                        if has_b and c < NC:
                            scores_t(i, par, c, 0)
                        for k in pieces[:1]:
                            score_piece(i, par, k)
                        if has_b and c < NC:
                            scores_t(i, par, c, 1)
                        if has_1 and c < 3:
                            turn_context(i, par, c)
                        if has_b and has_old and c in (4, 5):
                            turn_output(b - 1, c - 4, b * 3 + 6 if has_1 else None)
                        if has_b and has_old and par == 0 and c == 6:
                            project(i - 1)
                        if has_1 and c == NC + LAG - 1:
                            turn_maximum(i, par)
                        if has_b and c >= LAG:
                            values(i, par, c - LAG, (0, 1, 2))
                        for k in pieces[1:]:
                            score_piece(i, par, k)
                        if has_b and c >= LAG:
                            values(i, par, c - LAG, (3, 4, 5, 6))
                pe.wait_ge(n_ones, 2)
                over_pairs(pe, body, before=((-1, 1),))
                pe.wait_ge(n_ot, B * 2 - 2)
                turn_output(B - 1, 0, None)
                turn_output(B - 1, 1, None)
                project(NT - 1)

            @block.scalar
            def _(act):
                def body(i, par):
                    b = i * 2 + par
                    has_b, has_1, has_old = inside(i, par, 0), inside(i, par, 1), inside(i, par, -1)
                    slot = (par + 1) % 2
                    for c in range(NC):
                        for half in range(2) if has_b else ():
                            u = 2 * c + half
                            act.wait_ge(n_st, b * 2 * NC + u + 1)
                            if half == 0:
                                wait_for(act, n_pv, b * NC + c - NP + 1)
                            nc.scalar.activation(P1[:, c % NP, half * HALF:(half + 1) * HALF], PS[0:KC, u % 3, 0:HALF], ACT.Exp).then_inc(n_exp, 1)
                        if has_1 and c < 3:
                            act.wait_ge(n_turned, (b + 1) * 3 + c + 1)
                            nc.scalar.copy(cTh[0:DC, slot, c * SP:(c + 1) * SP], PS[0:DC, W1, 0:SP]).then_inc(n_cth, 1)
                        if has_1 and c == 3:
                            act.wait_ge(n_cx[slot], (i + (par + 1) // 2) * 16 + 16)
                            wait_for(act, n_pv, b * NC)
                            nc.scalar.copy(cNh[:, slot, :, 0:DC], d_cx[:, slot]).then_inc(n_cn, 1)
                        if has_b and has_old and c in (4, 5):
                            keep_old(i, par, c - 4)

                def keep_old(i, par, k):
                    n = i * 2 + par - 1
                    old = (par + 1) % 2
                    act.wait_ge(n_oturned, n * 2 + k + 1)
                    if old == 0 and k == 0:
                        wait_for(act, n_proj, i)
                    cut, rest = divmod(4 * 128, SQ)
                    if k == 0:
                        nc.scalar.copy(OT[:, 0:cut, old, :], PS[0:DC, W1, 0:cut * SQ].rearrange("p (h q) -> p h q", q=SQ))
                        nc.scalar.copy(OT[:, cut, old, 0:rest], PS[0:DC, W1, cut * SQ:512]).then_inc(n_ot, 1)
                    else:
                        nc.scalar.copy(OT[:, cut, old, rest:SQ], PS[0:DC, W1, 0:SQ - rest])
                        nc.scalar.copy(OT[:, cut + 1:H, old, :], PS[0:DC, W1, SQ - rest:NQ - 512].rearrange("p (h q) -> p h q", q=SQ)).then_inc(n_ot, 1)
                act.wait_ge(n_ones, 2)
                over_pairs(act, body, before=((-1, 1),))
                keep_old(NT, 0, 0)
                keep_old(NT, 0, 1)

            @block.vector
            def _(dve):
                nc.vector.memset(cNh[:], 1.0).then_inc(n_ones, 1)
                nc.vector.memset(cTh[96:96 + MR], 1.0).then_inc(n_ones, 1)

                def finish_batch(n):
                    dve.wait_ge(n_pv, n * NC + NC)
                    o = [PS[:, O1, 0:4 * ON].rearrange("p (t c) -> p t c", t=4), PS[:, O1 + 1, 0:3 * ON].rearrange("p (t c) -> p t c", t=3)]
                    for k in range(2):
                        nc.vector.reciprocal(r7[:, 4 * k:4 * k + 4 - k].unsqueeze(2), o[k][:, :, DC:DC + 1]).then_inc(n_r, 1)
                    dve.wait_ge(n_r, n * 2 + 2)
                    wait_for(dve, n_oturned, n * 2)
                    for k in range(2):
                        m = nc.vector.scalar_tensor_tensor(out=On[:, 4 * k:4 * k + 4 - k, :], in0=o[k][:, :, 0:DC], scalar=SCALE1,
                                                           in1=spread(r7[:, 4 * k:4 * k + 4 - k], 2, DC), op0=ALU.mult, op1=ALU.mult)
                    m.then_inc(n_on, 1)

                def finish_tile(t):
                    dve.wait_ge(n_proj, t + 1)
                    nc.vector.tensor_tensor(Y[:], PS[0:TP, W1, 0:D], rows[:, R_BO, :], ALU.add).then_inc(n_y, 1)
                    dve.wait_ge(n_y, t + 1)
                    wait_for(dve, n_out, t * 16)
                    nc.vector.tensor_tensor(Z[:].unsqueeze(1), Y[:].unsqueeze(1), X[:, bass.ds(t, 1), :], ALU.add).then_inc(n_z, 1)

                def body(i, par):
                    b = i * 2 + par
                    has_b, has_1, has_old = inside(i, par, 0), inside(i, par, 1), inside(i, par, -1)
                    slot = (par + 1) % 2
                    if has_b and has_old:
                        finish_batch(b - 1)

                    def reduce_piece(k):
                        dve.wait_ge(n_fill, (b + 1) * 21 + k + 1)
                        if k == 0:
                            wait_for(dve, n_mlink, (b + 1) * 3)
                        t, part = PIECES1[k]
                        nc.vector.tensor_reduce(m21[:, t, part:part + 1], PS[:, S1[k % 2], 0:SP], AX.X, ALU.max).then_inc(n_red, 1)
                    for c in range(NC + LAG):
                        pieces = list(BESIDE1[c]) if has_1 else []
                        for k in pieces[:1]:
                            reduce_piece(k)
                        if has_b and 0 < c <= NC and low_on_dve[c - 1]:
                            dve.wait_ge(n_exp, (b * NC + c) * 2)
                            high = P1[:, (c - 1) % NP].bitcast(BF16)[:, 1::2]
                            nc.vector.tensor_tensor(Pl[:, (c - 1) % NP], P1[:, (c - 1) % NP], high, ALU.subtract).then_inc(n_low_d, 1)
                        for k in pieces[1:]:
                            reduce_piece(k)
                        if has_b and has_old and par == 0 and c == 6:
                            finish_tile(i - 1)
                        if has_1 and c < 3:
                            dve.wait_ge(n_cth, (b + 1) * 3 + c + 1)
                            nc.vector.tensor_tensor(cTl[:, slot, c * SP:(c + 1) * SP], PS[0:DC, W1, 0:SP],
                                                    cTh[0:DC, slot, c * SP:(c + 1) * SP], ALU.subtract).then_inc(n_ctl, 1)
                    if has_1:
                        n = b + 1
                        dve.wait_ge(n_red, n * 21 + 21)
                        nc.vector.tensor_reduce(mt1[:], m21[:], AX.X, ALU.max).then_inc(n_mlink, 1)
                        dve.wait_ge(n_mlink, n * 3 + 1)
                        nc.vector.tensor_scalar(mt1[:], mt1[:], -LIFT, None, ALU.add).then_inc(n_mlink, 1)
                        dve.wait_ge(n_mlink, n * 3 + 2)
                        nc.vector.tensor_copy(mh1[:], mt1[:]).then_inc(n_mlink, 1)
                        dve.wait_ge(n_mlink, n * 3 + 3)
                        wait_for(dve, n_mturned, n)
                        nc.vector.tensor_scalar(mn1[:, 0:QT1], mh1[:], -1.0, None, ALU.mult)
                        nc.vector.tensor_tensor(mn1[:, QT1:], mh1[:], mt1[:], ALU.subtract).then_inc(n_mready, 1)
                        dve.wait_ge(n_mturned, n + 1)
                        nc.vector.tensor_tensor(Qh[96:96 + MR, slot].rearrange("p (t q) -> p t q", t=QT1),
                                                spread(PS[96:96 + MR, W1, 0:128], 1, QT1),
                                                spread(tab[96:96 + MR, C_MM1:C_M16], 2, 128), ALU.mult).then_inc(n_mlaid, 1)
                over_pairs(dve, body, before=((-1, 1),))
                finish_batch(B - 1)
                finish_tile(NT - 1)
        late.close()


_INS = ['x', 'ctx_768', 'L0_xattn_w_qkv', 'L0_xattn_b_qkv', 'L0_xattn_w_so', 'L0_xattn_b_so', 'L0_xattn_w_q',
        'L0_xattn_b_q', 'L0_xattn_w_k', 'L0_xattn_b_k', 'L0_xattn_w_v', 'L0_xattn_b_v', 'L0_xattn_w_co',
        'L0_xattn_b_co', 'L0_xattn_w1', 'L0_xattn_b1', 'L0_xattn_w2', 'L0_xattn_b2', 'L0_xattn_w3', 'L0_xattn_b3',
        'L0_xattn_ln_g', 'L0_xattn_ln_b', 'L1_xattn_Wq', 'L1_xattn_Wk', 'L1_xattn_Wv', 'L1_xattn_Wo', 'L1_xattn_bo',
        'L1_xattn_gamma', 'L1_xattn_beta']


def kernel(**inputs):
    import concourse.bacc as bacc
    from concourse.bass_utils import run_bass_kernel_spmd

    nc = bacc.Bacc("TRN2", target_bir_lowering=False, num_devices=1)
    arrays = {"shape_table": shape_table()}
    args = [nc.dram_tensor("shape_table", arrays["shape_table"].shape, F32, kind="ExternalInput").ap()]
    for name in _INS:
        a = np.ascontiguousarray(inputs[name])
        arrays[f"in_{name}"] = a
        args.append(nc.dram_tensor(f"in_{name}", a.shape, mybir.dt.from_np(a.dtype), kind="ExternalInput").ap())
    args.append(nc.dram_tensor("out_0", (B, SQ, D), F32, kind="ExternalOutput").ap())
    program(nc, *args)
    r = run_bass_kernel_spmd(nc, [arrays], core_ids=[0])
    return r.results[0]["out_0"]
```

```python
from contextlib import ExitStack

import numpy as np

import concourse.bass as bass
from concourse import mybir
from concourse.alu_op_type import AluOpType as ALU

ACT = mybir.ActivationFunctionType
AX = mybir.AxisListType
F32 = mybir.dt.float32
F16 = mybir.dt.float16
BF16 = mybir.dt.bfloat16

B, SQ, D = 16, 56, 128
SK, DC = 1500, 96
H = 16
DH0, DH1 = 8, 64
FF = 512
EPS = 1e-5
TOK = B * SQ
TP = 2 * SQ
NT = B // 2
HALF = TOK // 2
NQ = H * SQ
KC = 125
NC = SK // KC
SP = 500
NSP = SK // SP
G = 4
GH = H // G
PAIRS = H // 2
SCALE0 = DH0 ** -0.5
SCALE1 = DH1 ** -0.5
QT = NQ // 128
MR = 2 * QT
ON = 100
WS = 64.0
LIFT = 10 * float(np.log(2.0))
TWO_ONES = float(np.array(0x3C003C00, np.uint32).view(np.float32))

C_ID, C_M4, C_MM, C_M16, C_MV, C_END = 0, 128, 132, 139, 155, 157


def shape_table():
    t = np.zeros((128, C_END), np.float32)
    r = np.arange(128)[:, None]
    t[:, C_ID:C_M4] = np.eye(128)
    t[:, C_M4:C_MM] = (r % 32) // DH0 == np.arange(GH)
    t[:, C_MM:C_M16] = (r >= 96) * (r < 96 + MR) * ((r - 96) % QT == np.arange(QT))
    t[:, C_M16:C_MV] = r // DH0 == np.arange(H)
    t[:, C_MV:C_END] = r // SQ == np.arange(2)
    return t


def wait_for(eng, sem, count):
    if isinstance(count, int) and count <= 0:
        return
    eng.wait_ge(sem, count)


def spread(ap, dim, n):
    shape = list(ap.shape)
    return ap.unsqueeze(dim).broadcast_to(shape[:dim] + [n] + shape[dim:])


def over_pairs(eng, body, before=(), last=1):
    for i, par in before:
        body(i, par)
    for par in (0, 1):
        body(0, par)
    with eng.Fori(1, NT - last) as i:
        body(i, 0)
        body(i, 1)
    for i in range(NT - last, NT):
        body(i, 0)
        body(i, 1)


def inside(i, par, ahead):
    return not isinstance(i, int) or 0 <= 2 * i + par + ahead < B


def program(nc, table, x, ctx_768, w_qkv, b_qkv, w_so, b_so, w_q, b_q, w_k, b_k, w_v, b_v, w_co, b_co,
            w1, b1, w2, b2, w3, b3, ln_g, ln_b, Wq, Wk, Wv, Wo, bo, gamma, beta, out):
    with ExitStack() as ctx:
        def sb_in(stack, name, shape, dt=F32):
            return stack.enter_context(nc.sbuf_tensor(name, shape, dt))

        def sb(name, shape, dt=F32):
            return sb_in(ctx, name, shape, dt)

        def sem(name):
            return ctx.enter_context(nc.semaphore(name))

        PS = ctx.enter_context(nc.psum_tensor("PS", [128, 8, 512], F32))

        tab = sb("tab", [128, C_END])
        ident = tab[:, C_ID:C_M4]
        X = sb("X", [TP, NT, D])
        T128 = sb("T128", [128, TOK])
        att = sb("att", [128, TOK])
        work = sb("work", [TP, NT, D])
        normed = sb("normed", [TP, NT, D])
        sums = sb("sums", [TP, NT, 6])
        mean_var = sb("mean_var", [TP, NT, 2])
        spreads = sb("spreads", [TP, 3, NT])
        gains = sb("gains", [D, 4])
        rows = sb("rows", [TP, 7, D])
        R_BV, R_SO, R_CO, R_B3, R_G, R_B, R_BO = range(7)
        wso = sb("wso", [D, D])
        wco = sb("wco", [D, D])
        w1s = sb("w1s", [D, FF])
        w2s = sb("w2s", [128, 4, FF])
        w3s = sb("w3s", [128, 4, D])
        b1s = sb("b1s", [128, 4])
        b2s = sb("b2s", [128, 4])
        wq3 = sb("wq3", [D, G, 3, 32])
        bq3 = sb("bq3", [96, G])
        wq = sb("wq", [D, D])
        bq = sb("bq", [D, 1])
        wkv = sb("wkv", [DC + 1, 2, D])
        wkv16 = sb("wkv16", [DC + 1, 2, 2, D], F16)
        Qall = sb("Qall", [D, TOK], F16)
        Q16 = sb("Q16", [96, G, TOK], F16)
        Wqk = sb("Wqk", [D, H, DC])

        cross = ExitStack()
        NPB = 4
        LAG0 = 2
        TURN = 72
        cx = sb_in(cross, "cx", [KC, 2, NC, DC])
        cHi = sb_in(cross, "cHi", [DC + 1, 2, SK], F16)
        cLo = sb_in(cross, "cLo", [DC, 2, SK], F16)
        KH = sb_in(cross, "KH", [D, 2, 2, SK], F16)
        Kst = sb_in(cross, "Kst", [96 + MR, 2, G, SK], F16)
        Vst = sb_in(cross, "Vst", [KC, 2, NC, PAIRS, 32])
        m_part = sb_in(cross, "m_part", [128, QT, NSP])
        mtop = sb_in(cross, "mtop", [128, QT])
        mhigh = sb_in(cross, "mhigh", [128, QT], F16)
        mneg = sb_in(cross, "mneg", [128, MR])
        Os = sb_in(cross, "Os", [128, 5 * SQ])
        rs = sb_in(cross, "rs", [SQ, 4, 4])
        an = sb_in(cross, "an", [TURN, 2, 4, 2, DH0])
        x_steps = sem("x_steps")
        cx_in = [sem("cx_in0"), sem("cx_in1")]
        k_out, kst_in = sem("k_out"), [sem(f"kst_in{part}") for part in range(NSP)]
        c_halves = nc.dram_tensor("c_halves", (B, 2, DC, SK), F16, kind="Internal").ap()
        k_halves = nc.dram_tensor("k_halves", (2, D, 2, SK), F16, kind="Internal").ap()
        ct_ones, v_zero, ones_set, zeros_set = sem("ct_ones"), sem("v_zero"), sem("ones_set"), sem("zeros_set")
        ct_turned, ct_kept, ct_split, c_out = sem("ct_turned"), sem("ct_kept"), sem("ct_split"), sem("c_out")
        k_made, k_high, k_split = sem("k_made"), sem("k_high"), sem("k_split")
        v_made, v_kept, q_laid, qmx_laid = sem("v_made"), sem("v_kept"), sem("q_laid"), sem("qmx_laid")
        s_filled, s_reduced = sem("s_filled"), sem("s_reduced")
        m_link, m_ready, m_turned, m_laid = sem("m_link"), sem("m_ready"), sem("m_turned"), sem("m_laid")
        st_done, exp_done, pv_done = sem("st_done"), sem("exp_done"), sem("pv_done")
        o_kept, o_turned, r_ready, an_ready, an_turned, att_kept = (
            sem("o_kept"), sem("o_turned"), sem("r_ready"), sem("an_ready"), sem("an_turned"), sem("att_kept"))
        OB, WB, WB2, MB = 4, 5, 3, 7
        T_BANK, K_BANK, V_BANK = (WB, WB2, WB), (WB2, WB, WB2), WB2
        V_AT = {7: 0, 9: 1, 12: 2}
        PIECES = [(t, part) for part in range(NSP) for t in range(QT)]
        NPC = len(PIECES)
        BESIDE = [range(min(2 * c, NPC), min(2 * c + 2, NPC)) for c in range(NC + LAG0)]

        first = ctx.enter_context(ExitStack())
        wqkv = sb_in(first, "wqkv", [D, 3 * D])
        bqk = sb_in(first, "bqk", [D, 2])
        SQT = sb_in(first, "SQT", [D, B, SQ])
        SKT = sb_in(first, "SKT", [D, B, SQ])
        selfa = ExitStack()
        Kbd = sb_in(selfa, "Kbd", [D, 2, H, SQ])
        Qp = sb_in(selfa, "Qp", [D, 2, 2, 64])
        Xd = sb_in(selfa, "Xd", [D, 2, 2, 2, SQ])
        V2 = sb_in(selfa, "V2", [TP, 2, 2, D])
        Vbd = sb_in(selfa, "Vbd", [TP, 2, 2, PAIRS, 18])
        top = sb_in(selfa, "top", [128, 2, H])
        Sm = sb_in(selfa, "Sm", [128, 2, NQ])
        Pe = sb_in(selfa, "Pe", [128, 2, NQ])
        PT = sb_in(selfa, "PT", [TP, PAIRS, 128])
        rsum = sb_in(selfa, "rsum", [128, PAIRS, 2])
        ao = sb_in(selfa, "ao", [128, PAIRS, 2, DH0])
        s_ones, s_biased = sem("s_ones"), sem("s_biased")
        s_staged, s_kbd, s_vbd = sem("s_staged"), sem("s_kbd"), sem("s_vbd")
        s_v, s_vkept, s_scores = sem("s_v"), sem("s_vkept"), sem("s_scores")
        s_top, s_sm, s_exp, s_turned, s_pt = sem("s_top"), sem("s_sm"), sem("s_exp"), sem("s_turned"), sem("s_pt")
        s_pv, s_rsum, s_ao, s_aoT, s_att = sem("s_pv"), sem("s_rsum"), sem("s_ao"), sem("s_aoT"), sem("s_att")
        SB = 6


        def load_context(sp, i, par, ahead):
            slot, pair, n = (par + ahead) % 2, i + (par + ahead) // 2, i * 2 + par + ahead
            wait_for(sp, ct_turned, (n - 1) * 3)
            sp.dma_start(cx[:, slot], ctx_768[n].rearrange("(p c) d -> p c d", c=NC)).then_inc(cx_in[slot], 16)

        def store_context(sp, i, par, ahead):
            slot, n = (par + ahead) % 2, i * 2 + par + ahead
            sp.wait_ge(ct_split, n * 3 + 3)
            at = bass.ds(n, 1)
            sp.dma_start(c_halves[at, 0].rearrange("b p k -> p b k"), cHi[0:DC, slot:slot + 1, :]).then_inc(c_out, 16)
            sp.dma_start(c_halves[at, 1].rearrange("b p k -> p b k"), cLo[:, slot:slot + 1, :]).then_inc(c_out, 16)

        def lay_keys(sp, i, par, ahead):
            slot, n = (par + ahead) % 2, i * 2 + par + ahead

            def lay(part):
                cols = slice(part * SP, (part + 1) * SP)
                for block_row, half in enumerate((0, 1, 0)):
                    sp.dma_start(Kst[32 * block_row:32 * block_row + 32, slot, :, cols],
                                 k_halves[slot, :, half, cols].rearrange("(g r) k -> r g k", g=G)).then_inc(kst_in[part], 16)
            sp.wait_ge(k_split, n * 3 + 3)
            sp.dma_start(k_halves[slot], KH[:, slot]).then_inc(k_out, 16)
            sp.wait_ge(k_out, n * 16 + 16)
            lay(0)
            for part in (1, 2):
                wait_for(sp, st_done, ((n - 2) * NC + (part + 1) * 4) * 2)
                lay(part)

        LOOP, ONE, OPEN = range(3)

        def work_bank(banks, k, mode):
            if mode == OPEN:
                return {T_BANK: (4, 5, 6), K_BANK: (7, 4, 5)}[banks][k]
            return WB if mode == ONE else banks[k]

        def turn_context(pe, i, par, k, mode=LOOP):
            slot, pair, n = par, i + 1, i * 2 + par + 2
            if k == 0:
                pe.wait_ge(cx_in[slot], pair * 16 + 16)
                wait_for(pe, att_kept, n - 3)
            elif mode == ONE:
                pe.wait_ge(ct_split, n * 3 + k)
            elif mode == OPEN:
                pass
            elif k == 1:
                pe.wait_ge(v_kept, (n - 1) * 3)
            else:
                pe.wait_ge(ct_split, n * 3 + 1)
            for c in range(4):
                mm = pe.transpose(PS[0:DC, work_bank(T_BANK, k, mode), c * KC:(c + 1) * KC], cx[:, slot, 4 * k + c, :], ident[0:KC, 0:KC])
            mm.then_inc(ct_turned, 1)

        def k_piece(pe, i, par, k, mode=LOOP):
            n = i * 2 + par + 2
            if mode == OPEN:
                pe.wait_ge(ct_split, n * 3 + k + 1)
            elif k < 2:
                pe.wait_ge(ct_split, n * 3 + 2 + k)
            else:
                pe.wait_ge(k_split, n * 3 + 1)
            o = PS[:, work_bank(K_BANK, k, mode), 0:SP]
            at = slice(k * SP, (k + 1) * SP)
            pe.matmul(o, wkv16[:, 0, 0, :], cHi[:, par, at], start=True, stop=False)
            pe.matmul(o, wkv16[:, 0, 1, :], cHi[:, par, at], start=False, stop=False)
            pe.matmul(o, wkv16[0:DC, 0, 0, :], cLo[:, par, at], start=False, stop=True).then_inc(k_made, 1)

        def v_piece(pe, i, par, k, early=False):
            n, slot = i * 2 + par + 1, (par + 1) % 2
            if k == 0:
                pe.wait_ge(ct_split, n * 3 + 3)
                if inside(i, par, 2) and not early:
                    pe.wait_ge(k_split, n * 3 + 6)
            else:
                pe.wait_ge(v_kept, n * 3 + k)
            for c in range(4):
                at = slice((4 * k + c) * KC, (4 * k + c + 1) * KC)
                o = PS[0:KC, V_BANK, c * D:(c + 1) * D]
                pe.matmul(o, cHi[:, slot, at], wkv16[:, 1, 0, :], start=True, stop=False)
                pe.matmul(o, cHi[:, slot, at], wkv16[:, 1, 1, :], start=False, stop=False)
                mm = pe.matmul(o, cLo[:, slot, at], wkv16[0:DC, 1, 0, :], start=False, stop=True)
            mm.then_inc(v_made, 1)

        def keep_values(act, i, par, k):
            n, slot = i * 2 + par + 1, (par + 1) % 2
            act.wait_ge(v_made, n * 3 + k + 1)
            wait_for(act, pv_done, (n - 1) * NC)
            nc.scalar.activation(Vst[:, slot, 4 * k:4 * k + 4, :, 0:16],
                                 PS[0:KC, V_BANK, :].rearrange("p (c a d) -> p c a d", c=4, a=PAIRS), ACT.Identity, scale=1 / WS).then_inc(v_kept, 1)

        def keep_context(act, i, par, k, mode=LOOP):
            n, bank = i * 2 + par + 2, work_bank(T_BANK, k, mode)
            act.wait_ge(ct_turned, n * 3 + k + 1)
            if k == 0:
                wait_for(act, c_out, (n - 1) * 32)
            nc.scalar.copy(cHi[0:DC, par, k * SP:(k + 1) * SP], PS[0:DC, bank, 0:SP]).then_inc(ct_kept, 1)

        def split_context(dve, i, par, k, mode=LOOP):
            n, bank = i * 2 + par + 2, work_bank(T_BANK, k, mode)
            dve.wait_ge(ct_kept, n * 3 + k + 1)
            nc.vector.tensor_tensor(cLo[:, par, k * SP:(k + 1) * SP], PS[0:DC, bank, 0:SP],
                                    cHi[0:DC, par, k * SP:(k + 1) * SP], ALU.subtract).then_inc(ct_split, 1)

        def keep_keys(act, i, par, k, mode=LOOP):
            n, bank = i * 2 + par + 2, work_bank(K_BANK, k, mode)
            act.wait_ge(k_made, n * 3 + k + 1)
            if k == 0:
                wait_for(act, k_out, (n - 1) * 16)
            nc.scalar.activation(KH[:, par, 0, k * SP:(k + 1) * SP], PS[:, bank, 0:SP], ACT.Identity, scale=1 / WS).then_inc(k_high, 1)

        def split_keys(dve, i, par, k, mode=LOOP):
            n, bank = i * 2 + par + 2, work_bank(K_BANK, k, mode)
            dve.wait_ge(k_high, n * 3 + k + 1)
            nc.vector.scalar_tensor_tensor(out=KH[:, par, 1, k * SP:(k + 1) * SP], in0=PS[:, bank, 0:SP], scalar=1 / WS,
                                           in1=KH[:, par, 0, k * SP:(k + 1) * SP], op0=ALU.mult, op1=ALU.subtract).then_inc(k_split, 1)

        def lay_queries(pool, i, par):
            nc.gpsimd.tensor_tensor(Qmx[:, par].rearrange("p (h q) -> p h q", h=H),
                                    Qall[:].rearrange("p (b q) -> p b q", b=B)[:, bass.ds(i * 2 + par + 2, 1), :].broadcast_to([D, H, SQ]),
                                    spread(tab[:, C_M16:C_MV], 2, SQ), ALU.mult).then_inc(qmx_laid, 1)

        def lay_own_keys(t, j):
            nc.gpsimd.tensor_tensor(Kbd[:, j], SKT[:, bass.ds(t * 2 + j, 1), :].broadcast_to([D, H, SQ]),
                                    spread(tab[:, C_M16:C_MV], 2, SQ), ALU.mult).then_inc(s_kbd, 1)

        table_in, x_in, qkv_in, bv_in, wkv_in, later_in = (
            sem("table_in"), sem("x_in"), sem("qkv_in"), sem("bv_in"), sem("wkv_in"), sem("later_in"))
        wkv_high, wkv_split = sem("wkv_high"), sem("wkv_split")
        x_turned, x_kept, qk_made, qk_kept = sem("x_turned"), sem("x_kept"), sem("qk_made"), sem("qk_kept")
        qp_zero = sem("qp_zero")

        with nc.Block() as block:
            @block.sync
            def _(sp):
                sp.dma_start(tab[:], table).then_inc(table_in, 16)
                sp.dma_start(X[:], x.rearrange("b q d -> (b q) d").rearrange("(t p) d -> p t d", p=TP)).then_inc(x_in, 16)
                load_context(sp, -1, 0, 2)
                sp.dma_start(wqkv[:], w_qkv).then_inc(qkv_in, 16)
                sp.dma_start(bqk[:], b_qkv[0:2 * D].rearrange("(s p) -> p s", p=D), allow_slow_non_contiguous=True).then_inc(qkv_in, 16)
                for which, (weight, bias) in enumerate(((w_k, b_k), (w_v, b_v))):
                    sp.dma_start(wkv[0:DC, which, :], weight).then_inc(wkv_in, 16)
                    sp.dma_start(wkv[DC:DC + 1, which, :], bias.unsqueeze(0)).then_inc(wkv_in, 16)
                sp.dma_start(rows[:, R_BV, :], b_qkv[2 * D:3 * D].partition_broadcast(TP)).then_inc(bv_in, 16)
                load_context(sp, -1, 0, 3)

            @block.gpsimd
            def _(pool):
                nc.gpsimd.memset(Vst[:, :, :, :, 16:32], 0.0).then_inc(v_zero, 1)
                pool.wait_ge(v_zero, 1)
                nc.gpsimd.memset(Vst[:, :, :, :, 16:17], 1.0).then_inc(ones_set, 1)
                pool.wait_ge(ones_set, 1)
                nc.gpsimd.memset(Kst[96:96 + MR].bitcast(F32), TWO_ONES).then_inc(ones_set, 1)
                pool.wait_ge(ones_set, 2)
                pool.wait_ge(qk_kept, 2)
                for j in range(2):
                    lay_own_keys(0, j)

            @block.tensor
            def _(pe):
                pe.wait_ge(table_in, 16)
                pe.wait_ge(x_in, 16)
                for t in range(NT):
                    mm = pe.transpose(PS[:, t // 4, (t % 4) * TP:(t % 4 + 1) * TP], X[:, t, :], ident[0:TP, 0:TP])
                mm.then_inc(x_turned, 1)
                turn_context(pe, -1, 0, 0, mode=OPEN)
                pe.wait_ge(qkv_in, 32)
                pe.wait_ge(x_kept, 1)
                for s in range(2):
                    for half in range(2):
                        mm = pe.matmul(PS[:, 2 * s + half, 0:HALF], wqkv[:, s * D:(s + 1) * D],
                                       T128[:, half * HALF:(half + 1) * HALF], start=True, stop=True)
                    mm.then_inc(qk_made, 1)
                    turn_context(pe, -1, 0, s + 1, mode=OPEN)
                pe.wait_ge(wkv_split, 1)
                pe.wait_ge(ct_ones, 1)
                for k in range(NSP):
                    k_piece(pe, -1, 0, k, mode=OPEN)

            @block.vector
            def _(dve):
                nc.vector.memset(Qp[:], 0.0).then_inc(qp_zero, 1)
                nc.vector.memset(cHi[DC:DC + 1].bitcast(F32), TWO_ONES).then_inc(ct_ones, 1)
                nc.vector.memset(Os[:, 4 * SQ:], 0.0).then_inc(zeros_set, 1)
                nc.vector.memset(an[:], 0.0).then_inc(zeros_set, 1)
                dve.wait_ge(x_turned, 1)
                nc.vector.tensor_copy(T128[:].rearrange("p (h c) -> p h c", h=2), PS[:, 0:2, 0:HALF]).then_inc(x_kept, 1)
                for slot in range(2):
                    for j in range(2):
                        nc.vector.tensor_copy(Vbd[:, slot, j, :, 16:18], spread(tab[0:TP, C_MV:C_END], 1, PAIRS)).then_inc(s_ones, 1)
                split_context(dve, -1, 0, 0, mode=OPEN)
                for s, rows_of in enumerate((SQT, SKT)):
                    dve.wait_ge(qk_made, s + 1)
                    if s == 0:
                        dve.wait_ge(qkv_in, 32)
                    nc.vector.tensor_scalar(rows_of[:].rearrange("p (h b) q -> p h (b q)", h=2), PS[:, 2 * s:2 * s + 2, 0:HALF],
                                            bqk[:, s:s + 1], None, ALU.add).then_inc(qk_kept, 1)
                    split_context(dve, -1, 0, s + 1, mode=OPEN)
                dve.wait_ge(wkv_high, 1)
                nc.vector.scalar_tensor_tensor(out=wkv16[:, :, 1, :], in0=wkv[:], scalar=WS, in1=wkv16[:, :, 0, :],
                                               op0=ALU.mult, op1=ALU.subtract).then_inc(wkv_split, 1)
                for k in range(NSP):
                    split_keys(dve, -1, 0, k, mode=OPEN)

            @block.scalar
            def _(act):
                for k in range(NSP):
                    keep_context(act, -1, 0, k, mode=OPEN)
                    if k == 0:
                        act.wait_ge(wkv_in, 64)
                        nc.scalar.activation(wkv16[:, :, 0, :], wkv[:], ACT.Identity, scale=WS).then_inc(wkv_high, 1)
                for k in range(NSP):
                    keep_keys(act, -1, 0, k, mode=OPEN)

        LATER = 25

        def row(k):
            return spread(rows[:, k, :], 1, NT)

        def over_tiles(eng, step):
            step(0, 0)
            step(1, 1)
            with eng.Fori(1, NT // 2 - 1) as i:
                step(i * 2, 0)
                step(i * 2 + 1, 1)
            for t in range(NT - 2, NT + 2):
                step(t, t % 2)

        def there(t, ahead):
            return not isinstance(t, int) or 0 <= t + ahead < NT

        with nc.Block() as block:
            @block.sync
            def _(sp):
                store_context(sp, -1, 0, 2)
                lay_keys(sp, -1, 0, 2)
                for k, row in ((R_SO, b_so), (R_CO, b_co), (R_B3, b3), (R_G, ln_g), (R_B, ln_b), (R_BO, bo)):
                    sp.dma_start(rows[:, k, :], row.partition_broadcast(TP)).then_inc(later_in, 16)
                for k, column in enumerate((ln_g, ln_b, gamma, beta)):
                    sp.dma_start(gains[:, k:k + 1], column.unsqueeze(1)).then_inc(later_in, 16)
                sp.dma_start(wso[:], w_so).then_inc(later_in, 16)
                sp.dma_start(wco[:], w_co).then_inc(later_in, 16)
                for rep in range(3):
                    sp.dma_start(wq3[:, :, rep, :], w_q.rearrange("d (g r) -> d g r", g=G)).then_inc(later_in, 16)
                    sp.dma_start(bq3[32 * rep:32 * rep + 32, :], b_q.rearrange("(g r) -> r g", g=G), allow_slow_non_contiguous=True).then_inc(later_in, 16)
                sp.dma_start(wq[:], w_q).then_inc(later_in, 16)
                sp.dma_start(bq[:], b_q.unsqueeze(1)).then_inc(later_in, 16)
                sp.dma_start(w1s[:], w1).then_inc(later_in, 16)
                sp.dma_start(w2s[:], w2.rearrange("(k p) n -> p k n", p=128)).then_inc(later_in, 16)
                sp.dma_start(w3s[:], w3.rearrange("(k p) n -> p k n", p=128)).then_inc(later_in, 16)
                sp.dma_start(b1s[:], b1.rearrange("(k p) -> p k", p=128), allow_slow_non_contiguous=True).then_inc(later_in, 16)
                sp.dma_start(b2s[:], b2.rearrange("(k p) -> p k", p=128), allow_slow_non_contiguous=True).then_inc(later_in, 16)
                sp.wait_ge(later_in, 16 * LATER)

            @block.gpsimd
            def _(pool):
                def step(t, slot):
                    if there(t, 0) and not (isinstance(t, int) and t == 0):
                        for j in range(2):
                            wait_for(pool, s_scores, t * 2 + j - 1)
                            lay_own_keys(t, j)
                    if there(t, -1):
                        pool.wait_ge(s_vkept, t)
                        wait_for(pool, s_pv, t - 2)
                        for j in range(2):
                            v = nc.gpsimd.tensor_tensor(
                                Vbd[:, 1 - slot, j, :, 0:16].rearrange("p a (b c) -> p a b c", b=2),
                                V2[:, 1 - slot, j].rearrange("p (a b c) -> p a b c", a=PAIRS, b=2),
                                spread(spread(tab[0:TP, C_MV:C_END], 1, PAIRS), 3, DH0), ALU.mult)
                        v.then_inc(s_vbd, 1)
                over_tiles(pool, step)
                pool.wait_ge(later_in, 16 * LATER)
                nc.gpsimd.tensor_tensor(X[:], X[:], row(R_SO), ALU.add).then_inc(s_biased, 1)

            @block.scalar
            def _(act):
                def stage(t, slot):
                    nc.scalar.copy(Qp[:, slot, :, 0:SQ], SQT[:, bass.ds(t * 2, 2), :]).then_inc(s_staged, 1)
                    nc.scalar.copy(Xd[:, slot], spread(T128[:].rearrange("p (b q) -> p b q", b=B)[:, bass.ds(t * 2, 2), :], 2, 2)).then_inc(s_staged, 1)

                def step(t, slot):
                    if there(t, -2):
                        act.wait_ge(s_aoT, t - 1)
                        nc.scalar.copy(att[:].rearrange("p (b q) -> p b q", b=B)[:, bass.ds(t * 2 - 4, 2), :],
                                       PS[:, SB, 256:384].rearrange("p (j q) -> p j q", j=2)[:, :, 0:SQ]).then_inc(s_att, 1)
                    if there(t, -1):
                        for half in range(2):
                            act.wait_ge(s_turned, t * 2 - 1 + half)
                            nc.scalar.copy(PT[:, 4 * half:4 * half + 4].rearrange("p b c -> p (b c)"), PS[0:TP, 4 + half, :]).then_inc(s_pt, 1)
                    if there(t, 1):
                        wait_for(act, s_v, t)
                        stage(t + 1, 1 - slot)
                    if there(t, 0):
                        act.wait_ge(s_sm, t + 1)
                        nc.scalar.activation(Pe[:, slot], Sm[:, slot], ACT.Exp, scale=SCALE0).then_inc(s_exp, 1)
                stage(0, 0)
                over_tiles(act, step)

            @block.tensor
            def _(pe):
                def step(t, slot):
                    other = 1 - slot
                    if there(t, 0):
                        pe.wait_ge(s_staged, t * 2 + 2)
                        wait_for(pe, s_sm, t - 1)
                        for j in range(2):
                            pe.wait_ge(s_kbd, t * 2 + j + 1)
                            for half in range(2):
                                mm = pe.matmul(PS[64 * j:64 * j + 64, 2 * slot + half, 0:HALF], Qp[:, slot, j, :],
                                               Kbd[:, j, 8 * half:8 * half + 8, :], start=True, stop=True)
                            mm.then_inc(s_scores, 1)
                    if there(t, -2):
                        pe.wait_ge(s_ao, t - 1)
                        pe.transpose(PS[:, SB, 256:384], ao[:].rearrange("p a b c -> p (a b c)"), ident).then_inc(s_aoT, 1)
                    if there(t, -1):
                        pe.wait_ge(s_exp, t)
                        wait_for(pe, s_pt, t * 2 - 2)
                        for p in range(PAIRS):
                            mm = pe.transpose(PS[0:TP, 4 + p // 4, (p % 4) * 128:(p % 4 + 1) * 128],
                                              Pe[:, other, p * TP:(p + 1) * TP], ident)
                            if p % 4 == 3:
                                mm.then_inc(s_turned, 1)
                    if there(t, 0):
                        wait_for(pe, s_vkept, t)
                        for j in range(2):
                            mm = pe.matmul(PS[0:TP, 7, j * D:(j + 1) * D], Xd[:, slot, j], wqkv[:, 2 * D:3 * D], start=True, stop=True)
                        mm.then_inc(s_v, 1)
                    if there(t, -1):
                        pe.wait_ge(s_vbd, t)
                        wait_for(pe, s_att, t - 1)
                        for p in range(PAIRS):
                            if p % 4 == 0:
                                pe.wait_ge(s_pt, t * 2 - 1 + p // 4)
                            for j in range(2):
                                mm = pe.matmul(PS[64 * j:64 * j + 64, SB, p * 18:(p + 1) * 18], PT[:, p, 64 * j:64 * j + 64],
                                               Vbd[:, other, j, p, :], start=True, stop=True)
                        mm.then_inc(s_pv, 1)
                over_tiles(pe, step)

            @block.vector
            def _(dve):
                def step(t, slot):
                    if there(t, 0):
                        dve.wait_ge(s_scores, t * 2 + 2)
                        sc = PS[:, 2 * slot:2 * slot + 2, 0:HALF].rearrange("p a (h k) -> p a h k", h=8)
                        nc.vector.tensor_reduce(top[:, slot].rearrange("p (a h) -> p a h", a=2), sc, AX.X, ALU.max).then_inc(s_top, 1)
                        dve.wait_ge(s_top, t + 1)
                        wait_for(dve, s_exp, t - 1)
                        nc.vector.tensor_tensor(Sm[:, slot].rearrange("p (a h k) -> p a h k", a=2, h=8), sc,
                                                spread(top[:, slot].rearrange("p (a h) -> p a h", a=2), 3, SQ),
                                                ALU.subtract).then_inc(s_sm, 1)
                        dve.wait_ge(s_v, t + 1)
                        if isinstance(t, int) and t == 0:
                            dve.wait_ge(bv_in, 16)
                        wait_for(dve, s_vbd, t - 1)
                        nc.vector.tensor_tensor(V2[:, slot], PS[0:TP, 7, 0:2 * D].rearrange("p (j d) -> p j d", j=2),
                                                spread(rows[:, R_BV, :], 1, 2), ALU.add).then_inc(s_vkept, 1)
                    if there(t, -1):
                        dve.wait_ge(s_pv, t)
                        o = PS[:, SB, 0:PAIRS * 18].rearrange("p (a c) -> p a c", a=PAIRS)
                        nc.vector.reciprocal(rsum[:], o[:, :, 16:18]).then_inc(s_rsum, 1)
                        dve.wait_ge(s_rsum, t)
                        wait_for(dve, s_aoT, t - 1)
                        nc.vector.tensor_tensor(ao[:], o[:, :, 0:16].rearrange("p a (b c) -> p a b c", b=2),
                                                spread(rsum[:], 3, DH0), ALU.mult).then_inc(s_ao, 1)
                over_tiles(dve, step)
        selfa.close()
        first.close()

        beyond = ExitStack()
        Qst = sb_in(beyond, "Qst", [96 + MR, 2, G, GH * SQ], F16)
        Qmx = sb_in(beyond, "Qmx", [D, 2, NQ], F16)
        Pb = sb_in(beyond, "Pb", [KC, NPB, NQ])

        def project_tiles(pe, src, w, done):
            for t in range(NT):
                mm = pe.matmul(PS[0:TP, t // 4, (t % 4) * D:(t % 4 + 1) * D], src[:, t * TP:(t + 1) * TP], w, start=True, stop=True)
                if t % 4 == 3:
                    mm.then_inc(done, 1)

        def turn_normed(pe, tile_ready, done, base=0):
            for t in range(NT):
                pe.wait_ge(tile_ready, base + t + 1)
                mm = pe.transpose(PS[:, t // 4, (t % 4) * TP:(t % 4 + 1) * TP], normed[:, t, :], ident[0:TP, 0:TP])
                if t % 4 == 3:
                    mm.then_inc(done, 1)

        def sum_tiles(dve, link, tag, src, tiles):
            for t in tiles:
                nc.vector.bn_stats(sums[:, t, :], src[:, t, :]).then_inc(link, 1)
            return tag + len(tiles)

        def add_and_sum(dve, link, tag, made):
            for half in range(2):
                dve.wait_ge(made, half + 1)
                tiles = range(4 * half, 4 * half + 4)
                at = slice(tiles[0], tiles[-1] + 1)
                nc.vector.tensor_tensor(work[:, at], PS[0:TP, half, :].rearrange("p (t d) -> p t d", d=D), X[:, at], ALU.add).then_inc(link, 1)
                dve.wait_ge(link, tag + 1)
                tag = sum_tiles(dve, link, tag + 1, work, tiles)
            return tag

        def norm_spread(dve, link, tag, var_ready, root_ready):
            dve.wait_ge(link, tag)
            for t in range(NT):
                nc.vector.bn_aggr(mean_var[:, t, :], sums[:, t, :]).then_inc(link, 1)
            dve.wait_ge(link, tag + NT)
            nc.vector.tensor_scalar(spreads[:, 0, :].unsqueeze(2), mean_var[:, :, 1:2], EPS, None, ALU.add).then_inc(var_ready, 1)
            dve.wait_ge(root_ready, 1)
            nc.vector.reciprocal(spreads[:, 2, :], spreads[:, 1, :]).then_inc(link, 1)
            dve.wait_ge(link, tag + NT + 1)
            return tag + NT + 1

        def norm_tiles(dve, src, tile_ready):
            for t in range(NT):
                nc.vector.tensor_scalar(normed[:, t, :], src[:, t, :], mean_var[:, t, 0:1], spreads[:, 2, t:t + 1],
                                        ALU.subtract, ALU.mult).then_inc(tile_ready, 1)

        def norm_root(act, var_ready, root_ready):
            act.wait_ge(var_ready, 1)
            nc.scalar.activation(spreads[:, 1, :], spreads[:, 0, :], ACT.Sqrt).then_inc(root_ready, 1)

        def keep_turned_dve(dve, turned, kept, gain):
            dve.wait_ge(turned, 1)
            nc.vector.tensor_scalar(T128[:, 0:HALF], PS[:, 0, 0:HALF], gains[:, gain:gain + 1], gains[:, gain + 1:gain + 2],
                                    ALU.mult, ALU.add).then_inc(kept, 1)

        def keep_turned_act(act, turned, kept, gain):
            act.wait_ge(turned, 2)
            nc.scalar.activation(T128[:, HALF:TOK], PS[:, 1, 0:HALF], ACT.Identity, bias=gains[:, gain + 1:gain + 2],
                                 scale=gains[:, gain:gain + 1]).then_inc(kept, 1)

        def norm_to_residual(pool, step, bias):
            nc.gpsimd.tensor_tensor(X[:], normed[:], row(R_G), ALU.mult).then_inc(step, 1)
            pool.wait_ge(step, 1)
            nc.gpsimd.tensor_tensor(X[:], X[:], row(R_B), ALU.add).then_inc(step, 1)
            pool.wait_ge(step, 2)
            nc.gpsimd.tensor_tensor(X[:], X[:], row(bias), ALU.add).then_inc(step, 1)

        a_proj, a_link, a_var, a_root = sem("a_proj"), sem("a_link"), sem("a_var"), sem("a_root")
        a_normed, a_turned, a_kept, a_kept_act, a_all, a_all_kept, a_q, a_high, a_low = (
            sem(n) for n in ("a_normed", "a_turned", "a_kept", "a_kept_act", "a_all", "a_all_kept", "a_q", "a_high", "a_low"))
        A_BANK = (0, 2, 6, 0)
        with nc.Block() as block:
            @block.gpsimd
            def _(pool):
                pool.wait_ge(a_all_kept, 1)
                lay_queries(pool, -1, 0)

            @block.tensor
            def _(pe):
                project_tiles(pe, att, wso[:], a_proj)
                for k in range(NSP):
                    v_piece(pe, -1, 1, k, early=True)
                turn_normed(pe, a_normed, a_turned)
                pe.wait_ge(a_kept, 1)
                pe.wait_ge(a_kept_act, 1)
                for half in range(2):
                    mm = pe.matmul(PS[:, 6 + half, 0:HALF], wq[:], T128[:, half * HALF:(half + 1) * HALF], start=True, stop=True)
                mm.then_inc(a_all, 1)
                pe.wait_ge(v_kept, 3)
                for g in range(G):
                    if g == 2:
                        pe.wait_ge(a_all_kept, 1)
                    if g == 3:
                        pe.wait_ge(a_low, 1)
                    for half in range(2):
                        mm = pe.matmul(PS[0:96, A_BANK[g] + half, 0:HALF], wq3[:, g].rearrange("p a b -> p (a b)"),
                                       T128[:, half * HALF:(half + 1) * HALF], start=True, stop=True)
                    mm.then_inc(a_q, 1)
                    if g < NSP:
                        turn_context(pe, -1, 1, g, mode=ONE)

            @block.vector
            def _(dve):
                tag = add_and_sum(dve, a_link, 0, a_proj)
                norm_spread(dve, a_link, tag, a_var, a_root)
                norm_tiles(dve, work, a_normed)
                keep_turned_dve(dve, a_turned, a_kept, 0)
                for g in range(G):
                    dve.wait_ge(a_high, g + 1)
                    nc.vector.scalar_tensor_tensor(out=Q16[64:96, g, :].rearrange("p (h c) -> p h c", h=2),
                                                   in0=PS[64:96, A_BANK[g]:A_BANK[g] + 2, 0:HALF],
                                                   scalar=bq3[64:96, g:g + 1], in1=Q16[64:96, g, :].rearrange("p (h c) -> p h c", h=2),
                                                   op0=ALU.add, op1=ALU.subtract).then_inc(a_low, 1)
                    if g < NSP:
                        split_context(dve, -1, 1, g, mode=ONE)

            @block.scalar
            def _(act):
                for k in range(NSP):
                    keep_values(act, -1, 1, k)
                norm_root(act, a_var, a_root)
                keep_turned_act(act, a_turned, a_kept_act, 0)
                act.wait_ge(a_all, 1)
                nc.scalar.activation(Qall[:].rearrange("p (h c) -> p h c", h=2), PS[:, 6:8, 0:HALF], ACT.Identity, bias=bq[:, 0:1]).then_inc(a_all_kept, 1)
                for g in range(G):
                    act.wait_ge(a_q, g + 1)
                    nc.scalar.activation(Q16[:, g, :].rearrange("p (h c) -> p h c", h=2), PS[0:96, A_BANK[g]:A_BANK[g] + 2, 0:HALF],
                                         ACT.Identity, bias=bq3[:, g:g + 1]).then_inc(a_high, 1)
                    if g < NSP:
                        keep_context(act, -1, 1, g, mode=ONE)

        with nc.Block() as block:
            @block.sync
            def _(sp):
                def body(i, par):
                    if inside(i, par, 3):
                        load_context(sp, i, par, 3)
                    if inside(i, par, 2):
                        store_context(sp, i, par, 2)
                        lay_keys(sp, i, par, 2)
                over_pairs(sp, body, before=((-1, 1),), last=2)
                sp.wait_ge(c_out, 32 * B)

            @block.gpsimd
            def _(pool):
                def body(i, par):
                    b = i * 2 + par
                    if inside(i, par, 1):
                        slot, n = (par + 1) % 2, b + 1
                        wait_for(pool, st_done, b * NC * 2)
                        for g in range(G):
                            q = nc.gpsimd.tensor_tensor(
                                Qst[0:96, slot, g].rearrange("p (j q) -> p j q", j=GH),
                                Q16[:, g, :].rearrange("p (b q) -> p b q", b=B)[:, bass.ds(n, 1), :].broadcast_to([96, GH, SQ]),
                                spread(tab[0:96, C_M4:C_MM], 2, SQ), ALU.mult)
                        q.then_inc(q_laid, 1)
                    if inside(i, par, 2):
                        wait_for(pool, s_filled, (b + 1) * NPC)
                        lay_queries(pool, i, par)
                over_pairs(pool, body, before=((-1, 1),))
                norm_to_residual(pool, x_steps, R_CO)

            @block.tensor
            def _(pe):
                def scores_t(i, par, c):
                    n = i * 2 + par
                    if c == 0:
                        for part in range(NSP):
                            pe.wait_ge(kst_in[part], n * 48 + 48)
                        pe.wait_ge(q_laid, n + 1)
                        pe.wait_ge(m_laid, n + 1)
                    for half in range(2):
                        u = 2 * c + half
                        wait_for(pe, exp_done, n * 2 * NC + u - 2)
                        for g in (2 * half, 2 * half + 1):
                            mm = pe.matmul(PS[0:KC, u % 3, (g % 2) * 224:(g % 2 + 1) * 224],
                                           Kst[:, par, g, c * KC:(c + 1) * KC], Qst[:, par, g, :], start=True, stop=True)
                        mm.then_inc(st_done, 1)

                def values(i, par, c):
                    n = i * 2 + par
                    pe.wait_ge(exp_done, (n * NC + c) * 2 + 2)
                    if c == 0:
                        pe.wait_ge(v_kept, n * 3 + 3)
                        wait_for(pe, o_kept, n)
                    for p in range(PAIRS):
                        mm = pe.matmul(PS[32 * (p % 4):32 * (p % 4) + 32, OB, (p // 4) * TP:(p // 4 + 1) * TP],
                                       Vst[:, par, c, p, :], Pb[:, c % NPB, p * TP:(p + 1) * TP],
                                       start=(c == 0 and p < 4), stop=(c == NC - 1), skip_group_check=True)
                    mm.then_inc(pv_done, 1)

                def score_piece(i, par, k):
                    slot, n = (par + 1) % 2, i * 2 + par + 1
                    t, part = PIECES[k]
                    if k == 0:
                        pe.wait_ge(qmx_laid, n + 1)
                    if t == 0:
                        pe.wait_ge(k_high, n * 3 + part + 1)
                    wait_for(pe, s_reduced, n * NPC + k - 1)
                    pe.matmul(PS[:, 6 + k % 2, 0:SP], Qmx[:, slot, t * 128:(t + 1) * 128],
                              KH[:, slot, 0, part * SP:(part + 1) * SP], start=True, stop=True).then_inc(s_filled, 1)

                def turn_output(n, k_before):
                    pe.wait_ge(o_kept, n + 1)
                    if k_before is not None:
                        pe.wait_ge(k_split, k_before)
                    for k in range(4):
                        mm = pe.transpose(PS[0:TURN, WB, k * 128:(k + 1) * 128], Os[:, k * SQ:k * SQ + TURN], ident)
                    mm.then_inc(o_turned, 1)

                def turn_attention(n):
                    pe.wait_ge(an_ready, n + 1)
                    pe.transpose(PS[:, WB, 0:TURN], an[:].rearrange("p a b c d -> p (a b c d)"), ident[0:TURN, 0:TURN]).then_inc(an_turned, 1)

                def turn_maximum(i, par):
                    n = i * 2 + par + 1
                    pe.wait_ge(m_ready, n + 1)
                    pe.matmul(PS[96:96 + MR, MB, 0:128], mneg[:], ident, start=True, stop=True).then_inc(m_turned, 1)

                def body(i, par):
                    b = i * 2 + par
                    has_b, has_1, has_2, has_old = inside(i, par, 0), inside(i, par, 1), inside(i, par, 2), inside(i, par, -1)
                    at_start = not has_b
                    for c in range(NC + LAG0):
                        pieces = list(BESIDE[c]) if has_1 else []
                        if has_b and c < NC:
                            scores_t(i, par, c)
                        for k in pieces[:1]:
                            score_piece(i, par, k)
                        if has_b and c >= LAG0:
                            values(i, par, c - LAG0)
                        if has_2 and not at_start and c < 3:
                            turn_context(pe, i, par, c)
                        if has_2 and 3 <= c < 6:
                            k_piece(pe, i, par, c - 3)
                        if has_b and has_old and c == 6:
                            turn_output(b - 1, b * 3 + 8 if has_2 else None)
                        if has_1 and not at_start and c in V_AT:
                            v_piece(pe, i, par, V_AT[c])
                        if has_b and has_old and c == 8:
                            turn_attention(b - 1)
                        if has_1 and c == 11:
                            turn_maximum(i, par)
                        for k in pieces[1:]:
                            score_piece(i, par, k)
                over_pairs(pe, body, before=((-1, 1),))
                turn_output(B - 1, None)
                turn_attention(B - 1)

            @block.scalar
            def _(act):
                def keep_output(n):
                    act.wait_ge(pv_done, n * NC + NC)
                    nc.scalar.copy(Os[:, 0:4 * SQ], PS[:, OB, 0:4 * SQ]).then_inc(o_kept, 1)

                def keep_attention(n):
                    act.wait_ge(an_turned, n + 1)
                    nc.scalar.copy(att[:].rearrange("p (b q) -> p b q", b=B)[:, bass.ds(n, 1), :],
                                   PS[:, WB, 0:SQ].unsqueeze(1)).then_inc(att_kept, 1)

                def body(i, par):
                    b = i * 2 + par
                    has_b, has_1, has_2, has_old = inside(i, par, 0), inside(i, par, 1), inside(i, par, 2), inside(i, par, -1)
                    at_start = not has_b
                    if has_b and has_old:
                        keep_output(b - 1)
                    for c in range(NC + LAG0):
                        for half in range(2) if has_b and c < NC else ():
                            u = 2 * c + half
                            act.wait_ge(st_done, b * 2 * NC + u + 1)
                            if half == 0:
                                wait_for(act, pv_done, b * NC + c - NPB + 1)
                            nc.scalar.activation(Pb[:, c % NPB, half * HALF:(half + 1) * HALF], PS[0:KC, u % 3, 0:HALF],
                                                 ACT.Exp, scale=SCALE0).then_inc(exp_done, 1)
                        if has_2 and not at_start and c < 3:
                            keep_context(act, i, par, c)
                        if has_2 and 3 <= c < 6:
                            keep_keys(act, i, par, c - 3)
                        if has_b and has_old and c == 8:
                            keep_attention(b - 1)
                        if has_1 and not at_start and c in V_AT:
                            keep_values(act, i, par, V_AT[c])
                over_pairs(act, body, before=((-1, 1),))
                keep_output(B - 1)
                keep_attention(B - 1)

            @block.vector
            def _(dve):
                def reduce_piece(i, par, k):
                    n = i * 2 + par + 1
                    dve.wait_ge(s_filled, n * NPC + k + 1)
                    if k == 0:
                        wait_for(dve, m_link, n * 2)
                    t, part = PIECES[k]
                    nc.vector.tensor_reduce(m_part[:, t, part:part + 1], PS[:, 6 + k % 2, 0:SP], AX.X, ALU.max).then_inc(s_reduced, 1)

                def normalise(n):
                    dve.wait_ge(o_turned, n + 1)
                    w = PS[0:SQ, WB, :].rearrange("p (k t c) -> p k t c", k=4, t=4)
                    nc.vector.reciprocal(rs[:].unsqueeze(3), w[:, :, :, 16:17]).then_inc(r_ready, 1)
                    dve.wait_ge(r_ready, n + 1)
                    wait_for(dve, an_turned, n)
                    for j in range(2):
                        a = nc.vector.tensor_tensor(an[0:SQ, :, :, j, :], w[:, j::2, :, j * DH0:(j + 1) * DH0],
                                                    spread(rs[:, j::2, :], 3, DH0), ALU.mult)
                    a.then_inc(an_ready, 1)

                def body(i, par):
                    b = i * 2 + par
                    has_b, has_1, has_2, has_old = inside(i, par, 0), inside(i, par, 1), inside(i, par, 2), inside(i, par, -1)
                    at_start = not has_b
                    for c in range(NC):
                        pieces = list(BESIDE[c]) if has_1 else []
                        for k in pieces[:1]:
                            reduce_piece(i, par, k)
                        if has_2 and not at_start and 1 <= c < 4:
                            split_context(dve, i, par, c - 1)
                        if has_2 and 4 <= c < 7:
                            split_keys(dve, i, par, c - 4)
                        if has_b and has_old and c == 7:
                            normalise(b - 1)
                        for k in pieces[1:]:
                            reduce_piece(i, par, k)
                    if has_1:
                        n, slot = b + 1, (par + 1) % 2
                        dve.wait_ge(s_reduced, n * NPC + NPC)
                        nc.vector.tensor_reduce(mtop[:], m_part[:], AX.X, ALU.max).then_inc(m_link, 1)
                        dve.wait_ge(m_link, n * 2 + 1)
                        nc.vector.tensor_copy(mhigh[:], mtop[:]).then_inc(m_link, 1)
                        dve.wait_ge(m_link, n * 2 + 2)
                        wait_for(dve, m_turned, n)
                        nc.vector.tensor_scalar(mneg[:, 0:QT], mhigh[:], -1.0, None, ALU.mult)
                        nc.vector.tensor_tensor(mneg[:, QT:], mhigh[:], mtop[:], ALU.subtract).then_inc(m_ready, 1)
                        dve.wait_ge(m_turned, n + 1)
                        nc.vector.tensor_tensor(Qst[96:96 + MR, slot].rearrange("p g c -> p (g c)").rearrange("p (t q) -> p t q", t=QT),
                                                spread(PS[96:96 + MR, MB, 0:128], 1, QT),
                                                spread(tab[96:96 + MR, C_MM:C_M16], 2, 128), ALU.mult).then_inc(m_laid, 1)
                over_pairs(dve, body, before=((-1, 1),))
                normalise(B - 1)
        beyond.close()
        cross.close()

        late = ExitStack()
        QK = late.enter_context(nc.sbuf_tensor("QK", [DC, 2, B, H, SQ], F16))
        d_cx = sb_in(late, "d_cx", [KC, 2, NC, DC])
        cNh = sb_in(late, "cNh", [KC, 2, NC, DC + 1], F16)
        cTh = sb_in(late, "cTh", [DC + MR, 2, SK], F16)
        cTl = sb_in(late, "cTl", [DC, 2, SK], F16)
        Qh = sb_in(late, "Qh", [DC + MR, 2, NQ], F16)
        Ql = sb_in(late, "Ql", [DC, 2, NQ], F16)
        m21 = sb_in(late, "m21", [128, QT, NSP])
        n_ones, n_cx = sem("n_ones"), [sem("n_cx0"), sem("n_cx1")]
        n_in = [[sem("n_high0"), sem("n_high1")], [sem("n_low0"), sem("n_low1")]]
        n_st, n_fill, n_red, n_mlink = sem("n_st"), sem("n_fill"), sem("n_red"), sem("n_mlink")
        O1, W1, S1 = 4, 6, (3, 7)
        PIECES1 = [(t, part) for part in range(NSP) for t in range(QT)]

        def load_halves(sp, i, par, half, queries_made=None):
            slot, n = (par + 1) % 2, i * 2 + par + 1
            keys, queries = ((cTh, Qh), (cTl, Ql))[half]
            if half == 0:
                wait_for(sp, n_st, (n - 1) * 2 * NC)
            at = bass.ds(n, 1)
            sp.dma_start(keys[0:DC, slot:slot + 1, :], c_halves[at, half].rearrange("b p k -> p b k")).then_inc(n_in[half][slot], 16)
            if queries_made is not None:
                sp.wait_ge(queries_made, H)
            sp.dma_start(queries[0:DC, slot].rearrange("p (h q) -> p h q", h=H).unsqueeze(1), QK[:, half, at]).then_inc(n_in[half][slot], 16)

        def score_piece1(pe, i, par, k):
            slot, n = (par + 1) % 2, i * 2 + par + 1
            t, part = PIECES1[k]
            if k == 0:
                pe.wait_ge(n_in[0][slot], (i + (par + 1) // 2) * 32 + 32)
            wait_for(pe, n_red, n * 21 + max(k - 1, 0))
            pe.matmul(PS[:, S1[k % 2], 0:SP], Qh[0:DC, slot, t * 128:(t + 1) * 128], cTh[0:DC, slot, part * SP:(part + 1) * SP],
                      start=True, stop=True).then_inc(n_fill, 1)

        def reduce_piece1(dve, i, par, k):
            b = i * 2 + par
            dve.wait_ge(n_fill, (b + 1) * 21 + k + 1)
            if k == 0:
                wait_for(dve, n_mlink, (b + 1) * 3)
            t, part = PIECES1[k]
            nc.vector.tensor_reduce(m21[:, t, part:part + 1], PS[:, S1[k % 2], 0:SP], AX.X, ALU.max).then_inc(n_red, 1)
        Wvo16 = sb_in(late, "Wvo16", [DC, 2, H, D], F16)
        ffn = ExitStack()
        h1 = sb_in(ffn, "h1", [128, 4, TOK])
        h2 = sb_in(ffn, "h2", [128, 4, TOK])
        Wqs = sb_in(ffn, "Wqs", [D, H * DH1])
        Wks = sb_in(ffn, "Wks", [DC, H * DH1])
        Wvs = sb_in(ffn, "Wvs", [DC, H * DH1])
        Wos = sb_in(ffn, "Wos", [128, H // 2, D])
        WqT = sb_in(ffn, "WqT", [128, 8, D])
        WkT = sb_in(ffn, "WkT", [128, 8, DC])
        WvT = sb_in(ffn, "WvT", [128, 8, DC])
        Wvo = h1[:].rearrange("p a b -> p (a b)")[0:DC, 0:H * D].rearrange("p (h d) -> p h d", h=H)
        wq1_in, wk1_in, wv1_in, wo1_in = sem("wq1_in"), sem("wk1_in"), sem("wv1_in"), sem("wo1_in")
        wqT_made, wkT_made, wvT_made = sem("wqT_made"), sem("wkT_made"), sem("wvT_made")
        wqT_kept, wkT_kept, wvT_kept = sem("wqT_kept"), sem("wkT_kept"), sem("wvT_kept")
        wvo_split = sem("wvo_split")
        wqk_made, wvo_made, wqk_kept, wvo_kept = sem("wqk_made"), sem("wvo_made"), sem("wqk_kept"), sem("wvo_kept")
        c_proj, c_link, c_var, c_root, c_normed, c_turned, c_kept, c_kept_act, c_x = (
            sem(n) for n in ("c_proj", "c_link", "c_var", "c_root", "c_normed", "c_turned", "c_kept", "c_kept_act", "c_x"))
        f1, f1_kept, f2, f2_kept, f3 = (sem(n) for n in ("f1", "f1_kept", "f2", "f2_kept", "f3"))
        d_link, d_var, d_root, e_link, e_var, e_root, e_normed, e_turned, e_kept, e_kept_act = (
            sem(n) for n in ("d_link", "d_var", "d_root", "e_link", "e_var", "e_root", "e_normed", "e_turned", "e_kept", "e_kept_act"))
        g_made, g_high, g_low = sem("g_made"), sem("g_high"), sem("g_low")
        QK_BANKS = (0, 1, 2, 4, 5, 6)

        def pieces_beside(n):
            return range(min(2 * max(n - H - 4, 0), NPC), min(2 * max(n - H - 3, 0), NPC))
        with nc.Block() as block:
            @block.sync
            def _(sp):
                sp.dma_start(Wqs[:], Wq).then_inc(wq1_in, 16)
                sp.dma_start(Wks[:], Wk).then_inc(wk1_in, 16)
                sp.dma_start(Wvs[:], Wv).then_inc(wv1_in, 16)
                sp.dma_start(Wos[:], Wo.rearrange("(t p) d -> p t d", p=128)).then_inc(wo1_in, 16)
                sp.dma_start(d_cx[:, 0], ctx_768[0].rearrange("(p c) d -> p c d", c=NC)).then_inc(n_cx[0], 16)
                load_halves(sp, -1, 1, 0, g_high)
                load_halves(sp, -1, 1, 1, g_low)

            @block.gpsimd
            def _(pool):
                nc.gpsimd.memset(cTh[96:96 + MR].bitcast(F32), TWO_ONES).then_inc(n_ones, 1)
                pool.wait_ge(n_ones, 1)
                nc.gpsimd.memset(cNh[:, :, :, DC:DC + 1], 1.0).then_inc(n_ones, 1)
                pool.wait_ge(n_ones, 2)
                pool.wait_ge(c_normed, NT)
                norm_to_residual(pool, c_x, R_B3)
                pool.wait_ge(c_x, 3)
                pool.wait_ge(wvo_kept, 2)
                nc.gpsimd.tensor_tensor(Wvo16[:, 1], Wvo, Wvo16[:, 0], ALU.subtract).then_inc(wvo_split, 1)

            @block.tensor
            def _(pe):
                project_tiles(pe, att, wco[:], c_proj)
                for src, arrived, made, bank, rows_in in (
                        (Wqs, wq1_in, wqT_made, 2, D), (Wks, wk1_in, wkT_made, 4, DC), (Wvs, wv1_in, wvT_made, 6, DC)):
                    pe.wait_ge(arrived, 16)
                    for t in range(8):
                        mm = pe.transpose(PS[:, bank + t // 4, (t % 4) * rows_in:(t % 4 + 1) * rows_in],
                                          src[:, t * 128:(t + 1) * 128], ident[0:rows_in, 0:rows_in])
                    mm.then_inc(made, 1)
                turn_normed(pe, c_normed, c_turned)
                pe.wait_ge(c_kept, 1)
                pe.wait_ge(wqT_kept, 1)
                pe.wait_ge(wkT_kept, 1)
                pe.wait_ge(wvT_kept, 1)
                for m in range(4):
                    for half in range(2):
                        if m == 0 and half == 1:
                            pe.wait_ge(c_kept_act, 1)
                        mm = pe.matmul(PS[:, 2 * m + half, 0:HALF], w1s[:, m * 128:(m + 1) * 128],
                                       T128[:, half * HALF:(half + 1) * HALF], start=True, stop=True)
                    mm.then_inc(f1, 1)
                for m in range(4):
                    for half in range(2):
                        for k in range(4):
                            if m == 0 and half == 0:
                                pe.wait_ge(f1_kept, k + 1)
                            mm = pe.matmul(PS[:, 2 * m + half, 0:HALF], w2s[:, k, m * 128:(m + 1) * 128],
                                           h1[:, k, half * HALF:(half + 1) * HALF], start=(k == 0), stop=(k == 3))
                    mm.then_inc(f2, 1)
                for t in range(NT):
                    for k in range(4):
                        if t == 0:
                            pe.wait_ge(f2_kept, k + 1)
                        mm = pe.matmul(PS[0:TP, t // 4, (t % 4) * D:(t % 4 + 1) * D], h2[:, k, t * TP:(t + 1) * TP],
                                       w3s[:, k, :], start=(k == 0), stop=(k == 3))
                    if t % 4 == 3:
                        mm.then_inc(f3, 1)
                for h in range(H):
                    at = 64 * (h % 2)
                    mm = pe.matmul(PS[:, 4 + 2 * (h % 2) + h // 8, (h // 2 % 4) * DC:(h // 2 % 4 + 1) * DC], WqT[at:at + 64, h // 2, :],
                                   WkT[at:at + 64, h // 2, :], start=True, stop=True)
                mm.then_inc(wqk_made, 1)
                pe.wait_ge(wo1_in, 16)
                pe.wait_ge(wqk_kept, 2)
                for h in range(H):
                    at = 64 * (h % 2)
                    mm = pe.matmul(PS[0:DC, 4 + 2 * (h % 2) + h // 8, (h // 2 % 4) * D:(h // 2 % 4 + 1) * D], WvT[at:at + 64, h // 2, :],
                                   Wos[at:at + 64, h // 2, :], start=True, stop=True)
                mm.then_inc(wvo_made, 1)
                turn_normed(pe, e_normed, e_turned)
                pe.wait_ge(e_kept, 1)
                pe.wait_ge(wvo_kept, 2)
                for n in range(2 * H):
                    half, h = divmod(n, H)
                    wait_for(pe, g_low, n - 5)
                    if n == 1:
                        pe.wait_ge(e_kept_act, 1)
                    pe.matmul(PS[0:DC, QK_BANKS[n % 6], 0:HALF], Wqk[:, h, :], T128[:, half * HALF:(half + 1) * HALF],
                              start=True, stop=True).then_inc(g_made, 1)
                    for k in pieces_beside(n):
                        score_piece1(pe, -1, 1, k)

            @block.scalar
            def _(act):
                for made, kept, out_, bank, rows_in in ((wqT_made, wqT_kept, WqT, 2, D), (wkT_made, wkT_kept, WkT, 4, DC), (wvT_made, wvT_kept, WvT, 6, DC)):
                    act.wait_ge(made, 1)
                    nc.scalar.copy(out_[:].rearrange("p (a b) c -> p a (b c)", a=2), PS[:, bank:bank + 2, 0:4 * rows_in]).then_inc(kept, 1)
                norm_root(act, c_var, c_root)
                keep_turned_act(act, c_turned, c_kept_act, 0)
                for hidden, bias, made, kept in ((h1, b1s, f1, f1_kept), (h2, b2s, f2, f2_kept)):
                    for m in range(4):
                        act.wait_ge(made, m + 1)
                        nc.scalar.activation(hidden[:, m, :].rearrange("p (h c) -> p h c", h=2), PS[:, 2 * m:2 * m + 2, 0:HALF],
                                             ACT.Relu, bias=bias[:, m:m + 1]).then_inc(kept, 1)
                act.wait_ge(wqk_made, 1)
                for j in range(2):
                    nc.scalar.copy(Wqk[:].rearrange("p (a b j) c -> p j a b c", a=2, j=2)[:, j],
                                   PS[:, 4 + 2 * j:6 + 2 * j, 0:4 * DC].rearrange("p a (b c) -> p a b c", b=4)).then_inc(wqk_kept, 1)
                norm_root(act, d_var, d_root)
                act.wait_ge(wvo_made, 1)
                for j in range(2):
                    for into in (Wvo, Wvo16[:, 0]):
                        w = nc.scalar.activation(into.rearrange("p (a b j) c -> p j a b c", a=2, j=2)[:, j],
                                                 PS[0:DC, 4 + 2 * j:6 + 2 * j, 0:4 * D].rearrange("p a (b c) -> p a b c", b=4),
                                                 ACT.Identity, scale=WS)
                    w.then_inc(wvo_kept, 1)
                norm_root(act, e_var, e_root)
                keep_turned_act(act, e_turned, e_kept_act, 2)
                for n in range(2 * H):
                    act.wait_ge(g_made, n + 1)
                    half, h = divmod(n, H)
                    nc.scalar.copy(QK[:, 0, 8 * half:8 * half + 8, h, :],
                                   PS[0:DC, QK_BANKS[n % 6], 0:HALF].rearrange("p (b q) -> p b q", b=8)).then_inc(g_high, 1)

            @block.vector
            def _(dve):
                tag = add_and_sum(dve, c_link, 0, c_proj)
                norm_spread(dve, c_link, tag, c_var, c_root)
                norm_tiles(dve, work, c_normed)
                keep_turned_dve(dve, c_turned, c_kept, 0)
                dve.wait_ge(c_x, 3)
                tag = add_and_sum(dve, d_link, 0, f3)
                tag = norm_spread(dve, d_link, tag, d_var, d_root)
                for t in range(NT):
                    nc.vector.scalar_tensor_tensor(out=work[:, t, :], in0=work[:, t, :], scalar=mean_var[:, t, 0:1], in1=rows[:, R_G, :],
                                                   op0=ALU.subtract, op1=ALU.mult).then_inc(d_link, 1)
                for t in range(NT):
                    dve.wait_ge(d_link, tag + t + 1)
                    nc.vector.scalar_tensor_tensor(out=X[:, t, :], in0=work[:, t, :], scalar=spreads[:, 2, t:t + 1], in1=rows[:, R_B, :],
                                                   op0=ALU.mult, op1=ALU.add).then_inc(d_link, 1)
                dve.wait_ge(d_link, tag + 2 * NT)
                tag = sum_tiles(dve, e_link, 0, X, range(NT))
                norm_spread(dve, e_link, tag, e_var, e_root)
                norm_tiles(dve, X, e_normed)
                keep_turned_dve(dve, e_turned, e_kept, 2)
                for n in range(2 * H):
                    dve.wait_ge(g_high, n + 1)
                    half, h = divmod(n, H)
                    at = slice(8 * half, 8 * half + 8)
                    nc.vector.tensor_tensor(QK[:, 1, at, h, :], PS[0:DC, QK_BANKS[n % 6], 0:HALF].rearrange("p (b q) -> p b q", b=8),
                                            QK[:, 0, at, h, :], ALU.subtract).then_inc(g_low, 1)
                    for k in pieces_beside(n):
                        reduce_piece1(dve, -1, 1, k)
        ffn.close()

        NP = 4
        LAG = 2
        cNl = sb_in(late, "cNl", [KC, 2, NC, DC], F16)
        P1 = sb_in(late, "P1", [KC, NP, NQ])
        Pl = sb_in(late, "Pl", [KC, NP, NQ], F16)
        mt1 = sb_in(late, "mt1", [128, QT])
        mh1 = sb_in(late, "mh1", [128, QT], F16)
        mn1 = sb_in(late, "mn1", [128, MR])
        r7 = sb_in(late, "r7", [128, 8])
        On = sb_in(late, "On", [128, QT, DC])
        OTh = sb_in(late, "OTh", [DC, H, 2, SQ], F16)
        OTl = sb_in(late, "OTl", [DC, H, 2, SQ], F16)
        Y = sb_in(late, "Y", [TP, D])
        Z = sb_in(late, "Z", [TP, D])
        BESIDE1 = [range(NPC * min(max(c - 1, 0), 9) // 9, NPC * min(c, 9) // 9) for c in range(NC + LAG)]
        n_cn, n_cnl = sem("n_cn"), sem("n_cnl")
        n_mready, n_mturned, n_mlaid = (sem(n) for n in ("n_mready", "n_mturned", "n_mlaid"))
        n_exp, n_low_d, n_low_p, n_pv = (sem(n) for n in ("n_exp", "n_low_d", "n_low_p", "n_pv"))
        n_oth = sem("n_oth")
        n_r, n_on, n_oturned, n_ot, n_proj, n_y, n_z, n_out = (sem(n) for n in ("n_r", "n_on", "n_oturned", "n_ot", "n_proj", "n_y", "n_z", "n_out"))
        out_tiles = out.rearrange("b q d -> (b q) d").rearrange("(t p) d -> t p d", p=TP)
        low_on_dve = [c % 3 == 2 for c in range(NC)]
        DV = sum(low_on_dve)

        def turned_parts(k):
            cut, rest = divmod(4 * 128, SQ)
            src = PS[0:DC, W1]
            if k == 0:
                return ((slice(0, cut), slice(0, SQ), src[:, 0:cut * SQ].rearrange("p (h q) -> p h q", q=SQ)),
                        (cut, slice(0, rest), src[:, cut * SQ:512]))
            return ((cut, slice(rest, SQ), src[:, 0:SQ - rest]),
                    (slice(cut + 1, H), slice(0, SQ), src[:, SQ - rest:NQ - 512].rearrange("p (h q) -> p h q", q=SQ)))

        with nc.Block() as block:
            @block.sync
            def _(sp):
                def load_context(i, par):
                    slot, n = par, i * 2 + par + 2
                    wait_for(sp, n_st, (n - 2) * 2 * NC + 2 * (LAG + 2))
                    sp.dma_start(d_cx[:, slot], ctx_768[n].rearrange("(p c) d -> p c d", c=NC)).then_inc(n_cx[slot], 16)

                def body(i, par):
                    if inside(i, par, 0) and inside(i, par, 1):
                        load_halves(sp, i, par, 0)
                        load_halves(sp, i, par, 1)
                    if inside(i, par, 2):
                        load_context(i, par)
                    if par == 0 and not (isinstance(i, int) and i <= 0):
                        store(i - 1)

                def store(t):
                    sp.wait_ge(n_z, t + 1)
                    sp.dma_start(out_tiles[t], Z[:]).then_inc(n_out, 16)
                over_pairs(sp, body, before=((-1, 1),))
                store(NT - 1)
                sp.wait_ge(n_out, 16 * NT)

            @block.gpsimd
            def _(pool):
                def body(i, par):
                    b = i * 2 + par
                    for c in range(NC):
                        if inside(i, par, 0) and not low_on_dve[c]:
                            pool.wait_ge(n_exp, (b * NC + c) * 2 + 2)
                            high = P1[:, c % NP].bitcast(BF16)[:, 1::2]
                            nc.gpsimd.tensor_tensor(Pl[:, c % NP], P1[:, c % NP], high, ALU.subtract).then_inc(n_low_p, 1)
                        if inside(i, par, 1) and c == 4:
                            slot, n = (par + 1) % 2, b + 1
                            pool.wait_ge(n_cn, n + 1)
                            nc.gpsimd.tensor_tensor(cNl[:, slot], d_cx[:, slot], cNh[:, slot, :, 0:DC], ALU.subtract).then_inc(n_cnl, 1)
                over_pairs(pool, body, before=((-1, 1),))

            @block.tensor
            def _(pe):
                def scores_t(i, par, c, half):
                    n, u = i * 2 + par, 2 * c + half
                    if u == 0:
                        pe.wait_ge(n_in[1][par], i * 32 + 32)
                        pe.wait_ge(n_mlaid, n + 1)
                    wait_for(pe, n_exp, n * 2 * NC + u - 2)
                    at, cols = slice(c * KC, (c + 1) * KC), slice(half * HALF, (half + 1) * HALF)
                    o = PS[0:KC, u % 3, 0:HALF]
                    pe.matmul(o, cTh[:, par, at], Qh[:, par, cols], start=True, stop=False)
                    pe.matmul(o, cTh[0:DC, par, at], Ql[:, par, cols], start=False, stop=False)
                    pe.matmul(o, cTl[:, par, at], Qh[0:DC, par, cols], start=False, stop=True).then_inc(n_st, 1)

                def values(i, par, c, tiles):
                    n = i * 2 + par
                    if tiles[0] == 0:
                        if low_on_dve[c]:
                            pe.wait_ge(n_low_d, n * DV + sum(low_on_dve[:c + 1]))
                        else:
                            pe.wait_ge(n_low_p, n * (NC - DV) + c + 1 - sum(low_on_dve[:c + 1]))
                        if c == 0:
                            pe.wait_ge(n_cnl, n + 1)
                            wait_for(pe, n_on, n)
                    for t in tiles:
                        o = PS[:, O1 + t // 4, (t % 4) * ON:(t % 4) * ON + DC + 1]
                        cols = slice(t * 128, (t + 1) * 128)
                        high = P1[:, c % NP].bitcast(BF16)[:, 1::2][:, cols]
                        pe.matmul(o, high, cNh[:, par, c, :], start=(c == 0 and t % 4 == 0), stop=False, skip_group_check=True)
                        pe.matmul(o[:, 0:DC], high, cNl[:, par, c, :], start=False, stop=False, skip_group_check=True)
                        mm = pe.matmul(o, Pl[:, c % NP, cols], cNh[:, par, c, :], start=False, stop=(c == NC - 1), skip_group_check=True)
                    if tiles[-1] == QT - 1:
                        mm.then_inc(n_pv, 1)

                def turn_output(n, k):
                    pe.wait_ge(n_on, n + 1)
                    if k == 1:
                        pe.wait_ge(n_ot, n * 2 + 1)
                    for t in range(4 * k, min(4 * k + 4, QT)):
                        mm = pe.transpose(PS[0:DC, W1, (t % 4) * 128:(t % 4 + 1) * 128], On[:, t, :], ident)
                    mm.then_inc(n_oturned, 1)

                def project(t):
                    pe.wait_ge(n_ot, t * 4 + 4)
                    for h in range(H):
                        for o, w in ((OTh, 0), (OTh, 1), (OTl, 0)):
                            mm = pe.matmul(PS[0:TP, W1, 0:D], o[:, h].rearrange("p j q -> p (j q)"), Wvo16[:, w, h, :],
                                           start=(h == 0 and w == 0 and o is OTh), stop=(h == H - 1 and o is OTl))
                    mm.then_inc(n_proj, 1)

                def turn_maximum(i, par):
                    n = i * 2 + par + 1
                    pe.wait_ge(n_mready, n + 1)
                    if inside(i, par, 0) and inside(i, par, -1):
                        pe.wait_ge(n_ot, n * 2 - 2)
                        if par == 0:
                            pe.wait_ge(n_y, i)
                    pe.matmul(PS[96:96 + MR, W1, 0:128], mn1[:], ident, start=True, stop=True).then_inc(n_mturned, 1)

                def body(i, par):
                    b = i * 2 + par
                    has_b, has_1, has_old = inside(i, par, 0), inside(i, par, 1), inside(i, par, -1)
                    for c in range(NC + LAG):
                        pieces = list(BESIDE1[c]) if has_b and has_1 else []
                        if has_b and c < NC:
                            scores_t(i, par, c, 0)
                        for k in pieces[:1]:
                            score_piece1(pe, i, par, k)
                        if has_b and c < NC:
                            scores_t(i, par, c, 1)
                        if has_b and has_old and c in (4, 6):
                            turn_output(b - 1, (c - 4) // 2)
                        if has_b and has_old and par == 0 and c == 8:
                            project(i - 1)
                        if has_1 and c == NC:
                            turn_maximum(i, par)
                        if has_b and c >= LAG:
                            values(i, par, c - LAG, (0, 1, 2))
                        for k in pieces[1:]:
                            score_piece1(pe, i, par, k)
                        if has_b and c >= LAG:
                            values(i, par, c - LAG, (3, 4, 5, 6))
                over_pairs(pe, body, before=((-1, 1),))
                pe.wait_ge(n_ot, B * 2 - 2)
                turn_output(B - 1, 0)
                turn_output(B - 1, 1)
                project(NT - 1)

            @block.scalar
            def _(act):
                def body(i, par):
                    b = i * 2 + par
                    has_b, has_1, has_old = inside(i, par, 0), inside(i, par, 1), inside(i, par, -1)
                    slot = (par + 1) % 2
                    for c in range(NC):
                        for half in range(2) if has_b else ():
                            u = 2 * c + half
                            act.wait_ge(n_st, b * 2 * NC + u + 1)
                            if half == 0:
                                wait_for(act, n_pv, b * NC + c - NP + 1)
                            nc.scalar.activation(P1[:, c % NP, half * HALF:(half + 1) * HALF], PS[0:KC, u % 3, 0:HALF], ACT.Exp).then_inc(n_exp, 1)
                        if has_1 and c == 3:
                            act.wait_ge(n_cx[slot], (i + (par + 1) // 2) * 16 + 16)
                            wait_for(act, n_pv, b * NC)
                            nc.scalar.copy(cNh[:, slot, :, 0:DC], d_cx[:, slot]).then_inc(n_cn, 1)
                        if has_b and has_old and c in (4, 6):
                            keep_old(i, par, (c - 4) // 2)

                def keep_old(i, par, k):
                    n = i * 2 + par - 1
                    old = (par + 1) % 2
                    act.wait_ge(n_oturned, n * 2 + k + 1)
                    if old == 0 and k == 0:
                        wait_for(act, n_proj, i)
                    for heads, queries, bank in turned_parts(k):
                        o = nc.scalar.copy(OTh[:, heads, old, queries], bank)
                    o.then_inc(n_oth, 1)
                over_pairs(act, body, before=((-1, 1),))
                keep_old(NT, 0, 0)
                keep_old(NT, 0, 1)

            @block.vector
            def _(dve):
                def finish_batch(n):
                    dve.wait_ge(n_pv, n * NC + NC)
                    o = [PS[:, O1, 0:4 * ON].rearrange("p (t c) -> p t c", t=4), PS[:, O1 + 1, 0:3 * ON].rearrange("p (t c) -> p t c", t=3)]
                    for k in range(2):
                        nc.vector.reciprocal(r7[:, 4 * k:4 * k + 4 - k].unsqueeze(2), o[k][:, :, DC:DC + 1]).then_inc(n_r, 1)
                    dve.wait_ge(n_r, n * 2 + 2)
                    wait_for(dve, n_oturned, n * 2)
                    for k in range(2):
                        m = nc.vector.scalar_tensor_tensor(out=On[:, 4 * k:4 * k + 4 - k, :], in0=o[k][:, :, 0:DC], scalar=SCALE1,
                                                           in1=spread(r7[:, 4 * k:4 * k + 4 - k], 2, DC), op0=ALU.mult, op1=ALU.mult)
                    m.then_inc(n_on, 1)

                def split_old(i, par, k):
                    n, old = i * 2 + par - 1, (par + 1) % 2
                    dve.wait_ge(n_oth, n * 2 + k + 1)
                    for heads, queries, bank in turned_parts(k):
                        o = nc.vector.tensor_tensor(OTl[:, heads, old, queries], bank, OTh[:, heads, old, queries], ALU.subtract)
                    o.then_inc(n_ot, 1)

                def finish_tile(t):
                    dve.wait_ge(n_proj, t + 1)
                    nc.vector.scalar_tensor_tensor(out=Y[:], in0=PS[0:TP, W1, 0:D], scalar=1 / WS, in1=rows[:, R_BO, :],
                                                   op0=ALU.mult, op1=ALU.add).then_inc(n_y, 1)
                    dve.wait_ge(n_y, t + 1)
                    wait_for(dve, n_out, t * 16)
                    nc.vector.tensor_tensor(Z[:].unsqueeze(1), Y[:].unsqueeze(1), X[:, bass.ds(t, 1), :], ALU.add).then_inc(n_z, 1)

                def body(i, par):
                    b = i * 2 + par
                    has_b, has_1, has_old = inside(i, par, 0), inside(i, par, 1), inside(i, par, -1)
                    slot = (par + 1) % 2
                    if has_b and has_old:
                        finish_batch(b - 1)

                    def negate_maximum():
                        n = b + 1
                        dve.wait_ge(n_red, n * 21 + 21)
                        nc.vector.tensor_reduce(mt1[:], m21[:], AX.X, ALU.max).then_inc(n_mlink, 1)
                        dve.wait_ge(n_mlink, n * 3 + 1)
                        nc.vector.tensor_scalar(mt1[:], mt1[:], -LIFT, None, ALU.add).then_inc(n_mlink, 1)
                        dve.wait_ge(n_mlink, n * 3 + 2)
                        nc.vector.tensor_copy(mh1[:], mt1[:]).then_inc(n_mlink, 1)
                        dve.wait_ge(n_mlink, n * 3 + 3)
                        wait_for(dve, n_mturned, n)
                        nc.vector.tensor_scalar(mn1[:, 0:QT], mh1[:], -1.0, None, ALU.mult)
                        nc.vector.tensor_tensor(mn1[:, QT:], mh1[:], mt1[:], ALU.subtract).then_inc(n_mready, 1)

                    def lay_maximum():
                        n = b + 1
                        dve.wait_ge(n_mturned, n + 1)
                        nc.vector.tensor_tensor(Qh[96:96 + MR, slot].rearrange("p (t q) -> p t q", t=QT),
                                                spread(PS[96:96 + MR, W1, 0:128], 1, QT),
                                                spread(tab[96:96 + MR, C_MM:C_M16], 2, 128), ALU.mult).then_inc(n_mlaid, 1)

                    for c in range(NC + LAG):
                        pieces = list(BESIDE1[c]) if has_b and has_1 else []
                        if has_b and has_old and c in (5, 7):
                            split_old(i, par, (c - 5) // 2)
                        for k in pieces[:1]:
                            reduce_piece1(dve, i, par, k)
                        if has_b and 0 < c <= NC and low_on_dve[c - 1]:
                            dve.wait_ge(n_exp, (b * NC + c) * 2)
                            high = P1[:, (c - 1) % NP].bitcast(BF16)[:, 1::2]
                            nc.vector.tensor_tensor(Pl[:, (c - 1) % NP], P1[:, (c - 1) % NP], high, ALU.subtract).then_inc(n_low_d, 1)
                        for k in pieces[1:]:
                            reduce_piece1(dve, i, par, k)
                        if has_b and has_old and par == 0 and c == 9:
                            finish_tile(i - 1)
                        if has_1 and c == 10:
                            negate_maximum()
                        if has_1 and c == NC:
                            lay_maximum()
                over_pairs(dve, body, before=((-1, 1),))
                finish_batch(B - 1)
                split_old(NT, 0, 0)
                split_old(NT, 0, 1)
                finish_tile(NT - 1)
        late.close()


_INS = ['x', 'ctx_768', 'L0_xattn_w_qkv', 'L0_xattn_b_qkv', 'L0_xattn_w_so', 'L0_xattn_b_so', 'L0_xattn_w_q',
        'L0_xattn_b_q', 'L0_xattn_w_k', 'L0_xattn_b_k', 'L0_xattn_w_v', 'L0_xattn_b_v', 'L0_xattn_w_co',
        'L0_xattn_b_co', 'L0_xattn_w1', 'L0_xattn_b1', 'L0_xattn_w2', 'L0_xattn_b2', 'L0_xattn_w3', 'L0_xattn_b3',
        'L0_xattn_ln_g', 'L0_xattn_ln_b', 'L1_xattn_Wq', 'L1_xattn_Wk', 'L1_xattn_Wv', 'L1_xattn_Wo', 'L1_xattn_bo',
        'L1_xattn_gamma', 'L1_xattn_beta']


def kernel(**inputs):
    import concourse.bacc as bacc
    from concourse.bass_utils import run_bass_kernel_spmd

    nc = bacc.Bacc("TRN2", target_bir_lowering=False, num_devices=1)
    arrays = {"shape_table": shape_table()}
    args = [nc.dram_tensor("shape_table", arrays["shape_table"].shape, F32, kind="ExternalInput").ap()]
    for name in _INS:
        a = np.ascontiguousarray(inputs[name])
        arrays[f"in_{name}"] = a
        args.append(nc.dram_tensor(f"in_{name}", a.shape, mybir.dt.from_np(a.dtype), kind="ExternalInput").ap())
    args.append(nc.dram_tensor("out_0", (B, SQ, D), F32, kind="ExternalOutput").ap())
    program(nc, *args)
    r = run_bass_kernel_spmd(nc, [arrays], core_ids=[0])
    return r.results[0]["out_0"]
```
